# Optimizing a Trainium2 kernel written in Bass

```python
import numpy as np
import jax
import jax.numpy as jnp

def _softmax(x, axis=-1):
    return jax.nn.softmax(x, axis=axis)

def _gelu(x):
    return jax.nn.gelu(x, approximate=True)

def _silu(x):
    return jax.nn.silu(x)

def _sigmoid(x):
    return jax.nn.sigmoid(x)

def _layernorm(x, axis=-1, eps=1e-05):
    m = jnp.mean(x, axis=axis, keepdims=True)
    v = jnp.var(x, axis=axis, keepdims=True)
    return (x - m) / jnp.sqrt(v + eps)

def _scatter_add(tgt, idx, src, axis=0):
    return tgt.at[idx].add(src)

def _segment_sum(src, seg, n):
    return jax.ops.segment_sum(src, seg, n)
kernel_name = 'mk_early_fusion_embed_d4_tok_img768_r4_b00562'

def setup_inputs(seed: int=0):
    np.random.seed(seed)
    _w = jnp.asarray

    def _rec_inputs():
        import jax
        import jax.numpy as jnp
        _rk = jax.random.key(seed)
        x = -0.000222058 + 0.999998 * jax.random.normal(jax.random.fold_in(_rk, 1), (16, 3, 84, 84), jnp.float32)
        x_txt = jax.random.randint(jax.random.fold_in(_rk, 51), (16, 77), 0, 50226, jnp.int32)
        return (x, x_txt)
    x, x_txt = _rec_inputs()

    def _L0_tok_setup():
        import jax, jax.numpy as jnp
        import numpy as np
        from jax import lax
        HIDDEN = 192
        C_IN = 3
        PATCH = 16
        SIDE = 32
        NUM_PATCHES = SIDE * SIDE

        def _position_ids(nb_h, nb_w):
            boundaries = np.arange(1.0 / SIDE, 1.0, 1.0 / SIDE, dtype=np.float32)
            frac_h = np.arange(0.0, 1.0 - 1e-06, 1.0 / nb_h, dtype=np.float32)
            frac_w = np.arange(0.0, 1.0 - 1e-06, 1.0 / nb_w, dtype=np.float32)
            bh = np.searchsorted(boundaries, frac_h, side='right')
            bw = np.searchsorted(boundaries, frac_w, side='right')
            return jnp.asarray((bh[:, None] * SIDE + bw).reshape(-1), dtype=jnp.int32)
        key = jax.random.key(seed)
        k1, k2, k3 = jax.random.split(key, 3)
        pixel_values = jax.random.normal(k1, (32, C_IN, 128, 128), dtype=jnp.float32)
        conv_w = jax.random.normal(k2, (HIDDEN, C_IN, PATCH, PATCH), dtype=jnp.float32) * 0.02
        conv_b = jnp.zeros((HIDDEN,), dtype=jnp.float32)
        pos_table = jax.random.normal(k3, (NUM_PATCHES, HIDDEN), dtype=jnp.float32) * 0.02
        return {'pixel_values': pixel_values, 'conv_w': conv_w, 'conv_b': conv_b, 'pos_table': pos_table}
    _L0_tok_all = _L0_tok_setup()
    _L0_tok_in = {k: v for k, v in _L0_tok_all.items() if k in ('conv_w', 'conv_b', 'pos_table')}
    del _L0_tok_all

    def _L0_txt_setup():
        import jax, jax.numpy as jnp
        import numpy as np
        VOCAB = 50257
        EMBED = 192
        key = jax.random.key(seed)
        k1, k2 = jax.random.split(key)
        input_ids = jax.random.randint(k1, (8, 256), 0, VOCAB, dtype=jnp.int64 if jax.config.jax_enable_x64 else jnp.int32)
        token_embeddings = jax.random.normal(k2, (VOCAB, EMBED), dtype=jnp.float32)
        return {'input_ids': input_ids, 'token_embeddings': token_embeddings}
    _L0_txt_all = _L0_txt_setup()
    _L0_txt_in = {k: v for k, v in _L0_txt_all.items() if k in ('token_embeddings',)}
    del _L0_txt_all

    def _L0_attn_setup():
        import jax, jax.numpy as jnp
        import numpy as np
        B, S, D_MODEL, N_HEAD, D_HEAD, GROUPS = (2, 256, 192, 12, 64, 4)
        EPS = 1e-09
        SCALE = 1.0 / np.sqrt(D_HEAD).astype(np.float32)

        def grouped_proj(x, W, b=None):
            g = W.shape[0]
            b_, s_, d = x.shape
            y = jnp.einsum('bsgi,gio->bsgo', x.reshape(b_, s_, g, d // g), W).reshape(b_, s_, -1)
            return y if b is None else y + b

        def rel_shift_gather(pos_attn, context_len, shift):
            b, n, s, m = pos_attn.shape
            pos_attn = pos_attn.reshape(b, n, m, s)[:, :, shift:, :]
            pos_attn = pos_attn.reshape(b, n, s, m - shift)[..., :context_len]
            return pos_attn
        key = jax.random.key(seed)
        ks = jax.random.split(key, 16)
        dg = D_MODEL // GROUPS
        og = N_HEAD * D_HEAD // GROUPS
        std = 0.02
        return {'query': jax.random.normal(ks[0], (B, S, D_MODEL), jnp.float32), 'position_embeds': jax.random.normal(ks[1], (2 * S - 1, D_MODEL), jnp.float32), 'Wq': jax.random.normal(ks[2], (GROUPS, dg, og), jnp.float32) * std, 'Wk': jax.random.normal(ks[3], (GROUPS, dg, og), jnp.float32) * std, 'bk': jnp.zeros((N_HEAD * D_HEAD,), jnp.float32), 'Wv': jax.random.normal(ks[4], (GROUPS, dg, dg), jnp.float32) * std, 'bv': jnp.zeros((D_MODEL,), jnp.float32), 'r_kernel': jax.random.normal(ks[5], (D_MODEL, N_HEAD, D_HEAD), jnp.float32) * std, 'r_w_bias': jax.random.normal(ks[6], (N_HEAD, D_HEAD), jnp.float32) * std, 'r_r_bias': jax.random.normal(ks[7], (N_HEAD, D_HEAD), jnp.float32) * std, 'Wo': jax.random.normal(ks[8], (D_MODEL, D_MODEL), jnp.float32) * std, 'bo': jnp.zeros((D_MODEL,), jnp.float32), 'gamma': jnp.ones((D_MODEL,), jnp.float32), 'beta': jnp.zeros((D_MODEL,), jnp.float32)}
    _L0_attn_all = _L0_attn_setup()
    _L0_attn_in = {k: v for k, v in _L0_attn_all.items() if k in ('position_embeds', 'Wq', 'Wk', 'bk', 'Wv', 'bv', 'r_kernel', 'r_w_bias', 'r_r_bias', 'Wo', 'bo', 'gamma', 'beta')}
    del _L0_attn_all

    def _L0_ffn_setup():
        import jax, jax.numpy as jnp
        import numpy as np
        EPS_NORM = 1e-05
        RMS_EPS = 1e-05

        def _l2_normalize(v):
            n = jnp.sqrt(jnp.sum(v * v, axis=-1, keepdims=True))
            return v / jnp.maximum(n, EPS_NORM)

        def _rms_norm(x, weight, eps):
            ms = jnp.mean(x * x, axis=-1, keepdims=True)
            return x * jax.lax.rsqrt(ms + eps) * weight
        key = jax.random.key(seed)
        ks = jax.random.split(key, 6)
        B, T, D = (8, 1024, 192)
        S, F = (64, 768)
        x = jax.random.normal(ks[0], (B, T, D), dtype=jnp.float32)
        slots = 0.02 * jax.random.normal(ks[1], (S, D), dtype=jnp.float32)
        scale = jnp.ones((S,), dtype=jnp.float32)
        fc1_weight = 0.02 * jax.random.normal(ks[2], (S, D, F), dtype=jnp.float32)
        fc1_bias = jnp.zeros((S, F), dtype=jnp.float32)
        fc2_weight = 0.02 * jax.random.normal(ks[3], (S, F, D), dtype=jnp.float32)
        fc2_bias = jnp.zeros((S, D), dtype=jnp.float32)
        norm_weight = jnp.ones((D,), dtype=jnp.float32)
        return {'x': x, 'slots': slots, 'scale': scale, 'fc1_weight': fc1_weight, 'fc1_bias': fc1_bias, 'fc2_weight': fc2_weight, 'fc2_bias': fc2_bias, 'norm_weight': norm_weight}
    _L0_ffn_all = _L0_ffn_setup()
    _L0_ffn_in = {k: v for k, v in _L0_ffn_all.items() if k in ('slots', 'scale', 'fc1_weight', 'fc1_bias', 'fc2_weight', 'fc2_bias', 'norm_weight')}
    del _L0_ffn_all

    def _L1_attn_setup():
        import jax, jax.numpy as jnp
        import numpy as np
        D = 192
        H = 12
        D_INNER = 384
        K_CONV = 4
        HIDDEN = 768
        EPS = 1e-05

        def _ln(x, g, b):
            m = x.mean(-1, keepdims=True)
            v = ((x - m) ** 2).mean(-1, keepdims=True)
            return (x - m) * jax.lax.rsqrt(v + EPS) * g + b

        def _ssm(x, in_proj_w, conv_w, conv_b, out_proj_w):
            xz = x @ in_proj_w
            xb, z = jnp.split(xz, 2, axis=-1)
            lhs = xb.transpose(0, 2, 1)
            rhs = conv_w[:, None, :]
            y = jax.lax.conv_general_dilated(lhs, rhs, window_strides=(1,), padding=[(K_CONV - 1, 0)], dimension_numbers=('NCH', 'OIH', 'NCH'), feature_group_count=D_INNER)
            y = (y + conv_b[None, :, None]).transpose(0, 2, 1)
            y = jax.nn.silu(y) * jax.nn.silu(z)
            return y @ out_proj_w

        def _attn(x, qkv_w, qkv_b, num_heads):
            B, N, Dm = x.shape
            hd = Dm // num_heads
            qkv = (x @ qkv_w + qkv_b).reshape(B, N, 3, num_heads, hd)
            q, k, v = (qkv[:, :, 0], qkv[:, :, 1], qkv[:, :, 2])
            scale = hd ** (-0.5)
            scores = jnp.einsum('bqhd,bkhd->bhqk', q, k) * scale
            attn = jax.nn.softmax(scores, axis=-1)
            out = jnp.einsum('bhqk,bkhd->bqhd', attn, v)
            return out.reshape(B, N, Dm)
        key = jax.random.key(seed)
        ks = jax.random.split(key, 20)
        s = 0.02
        inp = {'x': jax.random.normal(ks[0], (2, 512, D), dtype=jnp.float32), 'ln1_g': jnp.ones((D,), jnp.float32), 'ln1_b': jnp.zeros((D,), jnp.float32), 'in_proj_w': jax.random.normal(ks[1], (D, 2 * D_INNER), jnp.float32) * s, 'conv_w': jax.random.normal(ks[2], (D_INNER, K_CONV), jnp.float32) * s, 'conv_b': jnp.zeros((D_INNER,), jnp.float32), 'out_proj_w': jax.random.normal(ks[3], (D_INNER, D), jnp.float32) * s, 'ln2_g': jnp.ones((D,), jnp.float32), 'ln2_b': jnp.zeros((D,), jnp.float32), 'qkv_w': jax.random.normal(ks[4], (D, 3 * D), jnp.float32) * s, 'qkv_b': jnp.zeros((3 * D,), jnp.float32), 'attn_proj_w': jax.random.normal(ks[5], (D, D), jnp.float32) * s, 'attn_proj_b': jnp.zeros((D,), jnp.float32), 'ln3_g': jnp.ones((D,), jnp.float32), 'ln3_b': jnp.zeros((D,), jnp.float32), 'ffn1_w': jax.random.normal(ks[6], (D, HIDDEN), jnp.float32) * s, 'ffn1_b': jnp.zeros((HIDDEN,), jnp.float32), 'ffn2_w': jax.random.normal(ks[7], (HIDDEN, D), jnp.float32) * s, 'ffn2_b': jnp.zeros((D,), jnp.float32)}
        return inp
    _L1_attn_all = _L1_attn_setup()
    _L1_attn_in = {k: v for k, v in _L1_attn_all.items() if k in ('ln1_g', 'ln1_b', 'in_proj_w', 'conv_w', 'conv_b', 'out_proj_w', 'ln2_g', 'ln2_b', 'qkv_w', 'qkv_b', 'attn_proj_w', 'attn_proj_b', 'ln3_g', 'ln3_b', 'ffn1_w', 'ffn1_b', 'ffn2_w', 'ffn2_b')}
    del _L1_attn_all

    def _L1_ffn_setup():
        import jax, jax.numpy as jnp
        import numpy as np
        DECAY = 0.9
        EPS = 0.01
        TOP_K = 2
        key = jax.random.key(seed)
        k1, k2, k3, k4 = jax.random.split(key, 4)
        B, S, H, I, E = (4, 512, 192, 512, 8)
        return {'hidden_states': jax.random.normal(k1, (B, S, H), jnp.float32), 'router_w': jax.random.normal(k2, (E, H), jnp.float32) * 0.02, 'w1': jax.random.normal(k3, (E, I, H), jnp.float32) * 0.02, 'w2': jax.random.normal(k4, (E, H, I), jnp.float32) * 0.02}
    _L1_ffn_all = _L1_ffn_setup()
    _L1_ffn_in = {k: v for k, v in _L1_ffn_all.items() if k in ('router_w', 'w1', 'w2')}
    del _L1_ffn_all

    def _L2_attn_setup():
        import jax, jax.numpy as jnp
        import numpy as np
        import math
        B, N, DIM = (4, 512, 192)
        HEADS, DIM_HEAD = (12, 64)
        SCALE = math.sqrt(DIM_HEAD)

        def _split_heads(t):
            b, n, _ = t.shape
            return t.reshape(b, n, HEADS, DIM_HEAD).transpose(0, 2, 1, 3)
        key = jax.random.key(seed)
        ks = jax.random.split(key, 5)
        inner = HEADS * DIM_HEAD
        x = jax.random.normal(ks[0], (B, N, DIM), dtype=jnp.float32)
        w_q = jax.random.normal(ks[1], (DIM, inner), dtype=jnp.float32) * 0.02
        w_k = jax.random.normal(ks[2], (DIM, inner), dtype=jnp.float32) * 0.02
        w_v = jax.random.normal(ks[3], (DIM, inner), dtype=jnp.float32) * 0.02
        w_o = jax.random.normal(ks[4], (inner, DIM), dtype=jnp.float32) * 0.02
        b_o = jnp.zeros((DIM,), dtype=jnp.float32)
        return {'x': x, 'w_q': w_q, 'w_k': w_k, 'w_v': w_v, 'w_o': w_o, 'b_o': b_o}
    _L2_attn_all = _L2_attn_setup()
    _L2_attn_in = {k: v for k, v in _L2_attn_all.items() if k in ('w_q', 'w_k', 'w_v', 'w_o', 'b_o')}
    del _L2_attn_all

    def _L2_ffn_setup():
        import jax, jax.numpy as jnp
        import numpy as np
        B, S, D_IN, D_HID, D_OUT = (32, 128, 192, 768, 192)
        key = jax.random.key(seed)
        k1, k2, k3, k4 = jax.random.split(key, 4)
        init_k = float(np.sqrt(1.0 / D_IN))
        init_k2 = float(np.sqrt(1.0 / D_HID))
        x = jax.random.normal(k1, (B, S, D_IN), dtype=jnp.float32)
        in_weight = jax.random.uniform(k2, (D_HID, D_IN), dtype=jnp.float32, minval=-init_k, maxval=init_k)
        in_bias = jax.random.uniform(k3, (D_HID,), dtype=jnp.float32, minval=-init_k, maxval=init_k)
        out_weight = jax.random.uniform(k4, (D_HID, D_OUT), dtype=jnp.float32, minval=-init_k2, maxval=init_k2)
        return {'x': x, 'in_weight': in_weight, 'in_bias': in_bias, 'out_weight': out_weight}
    _L2_ffn_all = _L2_ffn_setup()
    _L2_ffn_in = {k: v for k, v in _L2_ffn_all.items() if k in ('in_weight', 'in_bias', 'out_weight')}
    del _L2_ffn_all

    def _L3_attn_setup():
        import jax, jax.numpy as jnp
        import numpy as np
        EMBED_DIM = 192
        SEQ_LEN = 256
        BATCH = 32
        ALPHA = 0.99

        def _decay_mask(sl: int, alpha: float) -> jnp.ndarray:
            i = jnp.arange(sl, dtype=jnp.float32)
            diff = i[:, None] - i[None, :]
            return jnp.where(diff >= 0, jnp.float32(alpha) ** diff, 0.0)
        key = jax.random.key(seed)
        k1, k2 = jax.random.split(key)
        x = jax.random.normal(k1, (BATCH, SEQ_LEN, EMBED_DIM), dtype=jnp.float32)
        W_qkv = jax.random.normal(k2, (EMBED_DIM, 3 * EMBED_DIM), dtype=jnp.float32) * EMBED_DIM ** (-0.5)
        b_qkv = jnp.zeros((3 * EMBED_DIM,), dtype=jnp.float32)
        return {'x': x, 'W_qkv': W_qkv, 'b_qkv': b_qkv}
    _L3_attn_all = _L3_attn_setup()
    _L3_attn_in = {k: v for k, v in _L3_attn_all.items() if k in ('W_qkv', 'b_qkv')}
    del _L3_attn_all

    def _L3_ffn_setup():
        import jax, jax.numpy as jnp
        import numpy as np
        E, C, F, K = (8, 192, 768, 2)
        key = jax.random.key(seed)
        k0, k1, k2, k3 = jax.random.split(key, 4)
        B, T = (8, 512)
        return {'x': jax.random.normal(k0, (B, T, C), jnp.float32), 'router_w': jax.random.normal(k1, (E, C), jnp.float32) * 0.02, 'w1': jax.random.normal(k2, (E, C, F), jnp.float32) * 0.02, 'b1': jnp.zeros((E, F), jnp.float32), 'w2': jax.random.normal(k3, (E, F, C), jnp.float32) * 0.02, 'b2': jnp.zeros((E, C), jnp.float32)}
    _L3_ffn_all = _L3_ffn_setup()
    _L3_ffn_in = {k: v for k, v in _L3_ffn_all.items() if k in ('router_w', 'w1', 'b1', 'w2', 'b2')}
    del _L3_ffn_all
    return {'x': x, 'x_txt': x_txt, 'L0_tok_conv_w': _L0_tok_in['conv_w'], 'L0_tok_conv_b': _L0_tok_in['conv_b'], 'L0_tok_pos_table': _L0_tok_in['pos_table'], 'L0_txt_token_embeddings': _L0_txt_in['token_embeddings'], 'L0_attn_position_embeds': _L0_attn_in['position_embeds'], 'L0_attn_Wq': _L0_attn_in['Wq'], 'L0_attn_Wk': _L0_attn_in['Wk'], 'L0_attn_bk': _L0_attn_in['bk'], 'L0_attn_Wv': _L0_attn_in['Wv'], 'L0_attn_bv': _L0_attn_in['bv'], 'L0_attn_r_kernel': _L0_attn_in['r_kernel'], 'L0_attn_r_w_bias': _L0_attn_in['r_w_bias'], 'L0_attn_r_r_bias': _L0_attn_in['r_r_bias'], 'L0_attn_Wo': _L0_attn_in['Wo'], 'L0_attn_bo': _L0_attn_in['bo'], 'L0_attn_gamma': _L0_attn_in['gamma'], 'L0_attn_beta': _L0_attn_in['beta'], 'L0_ffn_slots': _L0_ffn_in['slots'], 'L0_ffn_scale': _L0_ffn_in['scale'], 'L0_ffn_fc1_weight': _L0_ffn_in['fc1_weight'], 'L0_ffn_fc1_bias': _L0_ffn_in['fc1_bias'], 'L0_ffn_fc2_weight': _L0_ffn_in['fc2_weight'], 'L0_ffn_fc2_bias': _L0_ffn_in['fc2_bias'], 'L0_ffn_norm_weight': _L0_ffn_in['norm_weight'], 'L1_attn_ln1_g': _L1_attn_in['ln1_g'], 'L1_attn_ln1_b': _L1_attn_in['ln1_b'], 'L1_attn_in_proj_w': _L1_attn_in['in_proj_w'], 'L1_attn_conv_w': _L1_attn_in['conv_w'], 'L1_attn_conv_b': _L1_attn_in['conv_b'], 'L1_attn_out_proj_w': _L1_attn_in['out_proj_w'], 'L1_attn_ln2_g': _L1_attn_in['ln2_g'], 'L1_attn_ln2_b': _L1_attn_in['ln2_b'], 'L1_attn_qkv_w': _L1_attn_in['qkv_w'], 'L1_attn_qkv_b': _L1_attn_in['qkv_b'], 'L1_attn_attn_proj_w': _L1_attn_in['attn_proj_w'], 'L1_attn_attn_proj_b': _L1_attn_in['attn_proj_b'], 'L1_attn_ln3_g': _L1_attn_in['ln3_g'], 'L1_attn_ln3_b': _L1_attn_in['ln3_b'], 'L1_attn_ffn1_w': _L1_attn_in['ffn1_w'], 'L1_attn_ffn1_b': _L1_attn_in['ffn1_b'], 'L1_attn_ffn2_w': _L1_attn_in['ffn2_w'], 'L1_attn_ffn2_b': _L1_attn_in['ffn2_b'], 'L1_ffn_router_w': _L1_ffn_in['router_w'], 'L1_ffn_w1': _L1_ffn_in['w1'], 'L1_ffn_w2': _L1_ffn_in['w2'], 'L2_attn_w_q': _L2_attn_in['w_q'], 'L2_attn_w_k': _L2_attn_in['w_k'], 'L2_attn_w_v': _L2_attn_in['w_v'], 'L2_attn_w_o': _L2_attn_in['w_o'], 'L2_attn_b_o': _L2_attn_in['b_o'], 'L2_ffn_in_weight': _L2_ffn_in['in_weight'], 'L2_ffn_in_bias': _L2_ffn_in['in_bias'], 'L2_ffn_out_weight': _L2_ffn_in['out_weight'], 'L3_attn_W_qkv': _L3_attn_in['W_qkv'], 'L3_attn_b_qkv': _L3_attn_in['b_qkv'], 'L3_ffn_router_w': _L3_ffn_in['router_w'], 'L3_ffn_w1': _L3_ffn_in['w1'], 'L3_ffn_b1': _L3_ffn_in['b1'], 'L3_ffn_w2': _L3_ffn_in['w2'], 'L3_ffn_b2': _L3_ffn_in['b2']}

def reference(x, x_txt, L0_tok_conv_w, L0_tok_conv_b, L0_tok_pos_table, L0_txt_token_embeddings, L0_attn_position_embeds, L0_attn_Wq, L0_attn_Wk, L0_attn_bk, L0_attn_Wv, L0_attn_bv, L0_attn_r_kernel, L0_attn_r_w_bias, L0_attn_r_r_bias, L0_attn_Wo, L0_attn_bo, L0_attn_gamma, L0_attn_beta, L0_ffn_slots, L0_ffn_scale, L0_ffn_fc1_weight, L0_ffn_fc1_bias, L0_ffn_fc2_weight, L0_ffn_fc2_bias, L0_ffn_norm_weight, L1_attn_ln1_g, L1_attn_ln1_b, L1_attn_in_proj_w, L1_attn_conv_w, L1_attn_conv_b, L1_attn_out_proj_w, L1_attn_ln2_g, L1_attn_ln2_b, L1_attn_qkv_w, L1_attn_qkv_b, L1_attn_attn_proj_w, L1_attn_attn_proj_b, L1_attn_ln3_g, L1_attn_ln3_b, L1_attn_ffn1_w, L1_attn_ffn1_b, L1_attn_ffn2_w, L1_attn_ffn2_b, L1_ffn_router_w, L1_ffn_w1, L1_ffn_w2, L2_attn_w_q, L2_attn_w_k, L2_attn_w_v, L2_attn_w_o, L2_attn_b_o, L2_ffn_in_weight, L2_ffn_in_bias, L2_ffn_out_weight, L3_attn_W_qkv, L3_attn_b_qkv, L3_ffn_router_w, L3_ffn_w1, L3_ffn_b1, L3_ffn_w2, L3_ffn_b2):
    import jax
    import jax.numpy as jnp

    def _L0_tok_ref(pixel_values, conv_w, conv_b, pos_table):
        import jax, jax.numpy as jnp
        import numpy as np
        from jax import lax
        HIDDEN = 192
        C_IN = 3
        PATCH = 16
        SIDE = 32
        NUM_PATCHES = SIDE * SIDE

        def _position_ids(nb_h, nb_w):
            boundaries = np.arange(1.0 / SIDE, 1.0, 1.0 / SIDE, dtype=np.float32)
            frac_h = np.arange(0.0, 1.0 - 1e-06, 1.0 / nb_h, dtype=np.float32)
            frac_w = np.arange(0.0, 1.0 - 1e-06, 1.0 / nb_w, dtype=np.float32)
            bh = np.searchsorted(boundaries, frac_h, side='right')
            bw = np.searchsorted(boundaries, frac_w, side='right')
            return jnp.asarray((bh[:, None] * SIDE + bw).reshape(-1), dtype=jnp.int32)
        B, _, H, W = pixel_values.shape
        nb_h, nb_w = (H // PATCH, W // PATCH)
        patches = lax.conv_general_dilated(pixel_values, conv_w, window_strides=(PATCH, PATCH), padding='VALID', dimension_numbers=('NCHW', 'OIHW', 'NCHW'))
        patches = patches + conv_b[None, :, None, None]
        embeddings = patches.reshape(B, HIDDEN, nb_h * nb_w).transpose(0, 2, 1)
        pos_ids = _position_ids(nb_h, nb_w)
        pos_emb = pos_table[pos_ids]
        return embeddings + pos_emb[None, :, :]

    def _L0_txt_ref(input_ids, token_embeddings):
        import jax, jax.numpy as jnp
        import numpy as np
        VOCAB = 50257
        EMBED = 192
        one_hot = jax.nn.one_hot(input_ids, VOCAB, dtype=token_embeddings.dtype)
        return jnp.einsum('bsv,ve->bse', one_hot, token_embeddings)

    def _L0_attn_ref(query, position_embeds, Wq, Wk, bk, Wv, bv, r_kernel, r_w_bias, r_r_bias, Wo, bo, gamma, beta):
        import jax, jax.numpy as jnp
        import numpy as np
        B, S, D_MODEL, N_HEAD, D_HEAD, GROUPS = (2, 256, 192, 12, 64, 4)
        EPS = 1e-09
        SCALE = 1.0 / np.sqrt(D_HEAD).astype(np.float32)

        def grouped_proj(x, W, b=None):
            g = W.shape[0]
            b_, s_, d = x.shape
            y = jnp.einsum('bsgi,gio->bsgo', x.reshape(b_, s_, g, d // g), W).reshape(b_, s_, -1)
            return y if b is None else y + b

        def rel_shift_gather(pos_attn, context_len, shift):
            b, n, s, m = pos_attn.shape
            pos_attn = pos_attn.reshape(b, n, m, s)[:, :, shift:, :]
            pos_attn = pos_attn.reshape(b, n, s, m - shift)[..., :context_len]
            return pos_attn
        b, s, _ = query.shape
        q = grouped_proj(query, Wq).reshape(b, s, N_HEAD, D_HEAD) * SCALE
        k = grouped_proj(query, Wk, bk).reshape(b, s, N_HEAD, D_HEAD)
        v = grouped_proj(query, Wv, bv).reshape(b, s, N_HEAD, D_MODEL // N_HEAD)
        content_score = jnp.einsum('bind,bjnd->bnij', q + r_w_bias * SCALE, k)
        r_head = jnp.einsum('td,dnh->tnh', position_embeds, r_kernel)
        pos_score = jnp.einsum('bind,tnd->bnit', q + r_r_bias * SCALE, r_head)
        pos_score = rel_shift_gather(pos_score, s, shift=1)
        attn_prob = jax.nn.softmax(content_score + pos_score, axis=-1)
        attn_vec = jnp.einsum('bnij,bjnd->bind', attn_prob, v).reshape(b, s, D_MODEL)
        attn_out = attn_vec @ Wo + bo
        h = query + attn_out
        mu = jnp.mean(h, axis=-1, keepdims=True)
        var = jnp.mean(jnp.square(h - mu), axis=-1, keepdims=True)
        return (h - mu) * jax.lax.rsqrt(var + EPS) * gamma + beta

    def _L0_ffn_ref(x, slots, scale, fc1_weight, fc1_bias, fc2_weight, fc2_bias, norm_weight):
        import jax, jax.numpy as jnp
        import numpy as np
        EPS_NORM = 1e-05
        RMS_EPS = 1e-05

        def _l2_normalize(v):
            n = jnp.sqrt(jnp.sum(v * v, axis=-1, keepdims=True))
            return v / jnp.maximum(n, EPS_NORM)

        def _rms_norm(x, weight, eps):
            ms = jnp.mean(x * x, axis=-1, keepdims=True)
            return x * jax.lax.rsqrt(ms + eps) * weight
        xn = _rms_norm(x, norm_weight, RMS_EPS)
        tok = _l2_normalize(xn)
        sl = _l2_normalize(slots) * scale[:, None]
        logits = jnp.einsum('sd,btd->bst', sl, tok)
        dispatch_w = jax.nn.softmax(logits, axis=-1)
        combine_w = jax.nn.softmax(logits, axis=-2)
        y = jnp.einsum('btd,bst->bsd', xn, dispatch_w)
        y = jnp.einsum('sio,bsi->bso', fc1_weight, y) + fc1_bias
        y = jax.nn.gelu(y, approximate=False)
        y = jnp.einsum('sio,bsi->bso', fc2_weight, y) + fc2_bias
        out = jnp.einsum('bsd,bst->btd', y, combine_w)
        return out

    def _L1_attn_ref(x, ln1_g, ln1_b, in_proj_w, conv_w, conv_b, out_proj_w, ln2_g, ln2_b, qkv_w, qkv_b, attn_proj_w, attn_proj_b, ln3_g, ln3_b, ffn1_w, ffn1_b, ffn2_w, ffn2_b):
        import jax, jax.numpy as jnp
        import numpy as np
        D = 192
        H = 12
        D_INNER = 384
        K_CONV = 4
        HIDDEN = 768
        EPS = 1e-05

        def _ln(x, g, b):
            m = x.mean(-1, keepdims=True)
            v = ((x - m) ** 2).mean(-1, keepdims=True)
            return (x - m) * jax.lax.rsqrt(v + EPS) * g + b

        def _ssm(x, in_proj_w, conv_w, conv_b, out_proj_w):
            xz = x @ in_proj_w
            xb, z = jnp.split(xz, 2, axis=-1)
            lhs = xb.transpose(0, 2, 1)
            rhs = conv_w[:, None, :]
            y = jax.lax.conv_general_dilated(lhs, rhs, window_strides=(1,), padding=[(K_CONV - 1, 0)], dimension_numbers=('NCH', 'OIH', 'NCH'), feature_group_count=D_INNER)
            y = (y + conv_b[None, :, None]).transpose(0, 2, 1)
            y = jax.nn.silu(y) * jax.nn.silu(z)
            return y @ out_proj_w

        def _attn(x, qkv_w, qkv_b, num_heads):
            B, N, Dm = x.shape
            hd = Dm // num_heads
            qkv = (x @ qkv_w + qkv_b).reshape(B, N, 3, num_heads, hd)
            q, k, v = (qkv[:, :, 0], qkv[:, :, 1], qkv[:, :, 2])
            scale = hd ** (-0.5)
            scores = jnp.einsum('bqhd,bkhd->bhqk', q, k) * scale
            attn = jax.nn.softmax(scores, axis=-1)
            out = jnp.einsum('bhqk,bkhd->bqhd', attn, v)
            return out.reshape(B, N, Dm)
        x = x + _ssm(_ln(x, ln1_g, ln1_b), in_proj_w, conv_w, conv_b, out_proj_w)
        a = _attn(_ln(x, ln2_g, ln2_b), qkv_w, qkv_b, H)
        x = x + a @ attn_proj_w + attn_proj_b
        h = jax.nn.gelu(_ln(x, ln3_g, ln3_b) @ ffn1_w + ffn1_b, approximate=False)
        x = x + h @ ffn2_w + ffn2_b
        return x

    def _L1_ffn_ref(hidden_states, router_w, w1, w2):
        import jax, jax.numpy as jnp
        import numpy as np
        DECAY = 0.9
        EPS = 0.01
        TOP_K = 2
        B, S, H = hidden_states.shape
        E = router_w.shape[0]
        flat = hidden_states.reshape(B * S, H)
        logits = flat @ router_w.T
        probs = jax.nn.softmax(logits, axis=-1)
        topk_probs, topk_idx = jax.lax.top_k(probs, TOP_K)
        importance = jax.lax.stop_gradient(probs).sum(axis=0)
        running = jnp.ones((E,), dtype=flat.dtype)
        blended = running + (1.0 - DECAY) * (importance - running)
        running = blended + EPS
        balance = running[topk_idx]
        balanced = topk_probs / balance
        balanced = balanced / balanced.sum(axis=-1, keepdims=True)
        h = jnp.einsum('th,eih->tei', flat, w1)
        h = jax.nn.silu(h)
        outs = jnp.einsum('tei,ehi->teh', h, w2)
        sel = jnp.take_along_axis(outs, topk_idx[:, :, None], axis=1)
        combined = (sel * balanced[..., None]).sum(axis=1)
        return combined.reshape(B, S, H)

    def _L2_attn_ref(x, w_q, w_k, w_v, w_o, b_o):
        import jax, jax.numpy as jnp
        import numpy as np
        import math
        B, N, DIM = (4, 512, 192)
        HEADS, DIM_HEAD = (12, 64)
        SCALE = math.sqrt(DIM_HEAD)

        def _split_heads(t):
            b, n, _ = t.shape
            return t.reshape(b, n, HEADS, DIM_HEAD).transpose(0, 2, 1, 3)
        q = _split_heads(x @ w_q)
        k = _split_heads(x @ w_k)
        v = _split_heads(x @ w_v)
        scores = jnp.einsum('bhnd,bhmd->bhnm', q, k) / SCALE
        attn = jax.nn.softmax(scores, axis=-1)
        h = jnp.einsum('bhnm,bhmd->bhnd', attn, v)
        H = h.transpose(0, 2, 1, 3).reshape(x.shape[0], x.shape[1], HEADS * DIM_HEAD)
        out = H @ w_o + b_o
        return out

    def _L2_ffn_ref(x, in_weight, in_bias, out_weight):
        import jax, jax.numpy as jnp
        import numpy as np
        B, S, D_IN, D_HID, D_OUT = (32, 128, 192, 768, 192)
        lead = x.shape[:-1]
        xt = x.reshape(-1, in_weight.shape[1])
        h = jax.nn.gelu(jnp.einsum('td,hd->th', xt, in_weight) + in_bias, approximate=False)
        out = jnp.einsum('th,ho->to', h, out_weight)
        return out.reshape(*lead, out_weight.shape[1])

    def _L3_attn_ref(x, W_qkv, b_qkv):
        import jax, jax.numpy as jnp
        import numpy as np
        EMBED_DIM = 192
        SEQ_LEN = 256
        BATCH = 32
        ALPHA = 0.99

        def _decay_mask(sl: int, alpha: float) -> jnp.ndarray:
            i = jnp.arange(sl, dtype=jnp.float32)
            diff = i[:, None] - i[None, :]
            return jnp.where(diff >= 0, jnp.float32(alpha) ** diff, 0.0)
        bs, sl, d = x.shape
        qkv = x @ W_qkv + b_qkv
        q, k, v = jnp.split(qkv, 3, axis=-1)
        M = _decay_mask(sl, ALPHA)
        dim_sqrt = jnp.sqrt(jnp.float32(d))
        scores = jnp.einsum('bsd,btd->bst', q, k) / dim_sqrt * M
        return jnp.einsum('bst,btd->bsd', scores, v)

    def _L3_ffn_ref(x, router_w, w1, b1, w2, b2):
        import jax, jax.numpy as jnp
        import numpy as np
        E, C, F, K = (8, 192, 768, 2)
        B, T, Cc = x.shape
        flat = x.reshape(-1, Cc)
        logits = flat @ router_w.T
        probs = jax.nn.softmax(logits.astype(jnp.float32), axis=-1)
        top_w, top_i = jax.lax.top_k(probs, K)
        top_w = (top_w / top_w.sum(-1, keepdims=True)).astype(x.dtype)
        out = jnp.zeros_like(flat)
        for e in range(E):
            w_e = jnp.sum(top_w * (top_i == e), axis=-1)[:, None]
            h = jax.nn.gelu(flat @ w1[e] + b1[e], approximate=False)
            out = out + w_e * (h @ w2[e] + b2[e])
        return out.reshape(B, T, Cc)
    h = _L0_tok_ref(x, L0_tok_conv_w, L0_tok_conv_b, L0_tok_pos_table)
    h = jnp.concatenate([h, _L0_txt_ref(x_txt, L0_txt_token_embeddings)], axis=1)
    h = h + _L0_attn_ref(_layernorm(h, axis=-1), L0_attn_position_embeds, L0_attn_Wq, L0_attn_Wk, L0_attn_bk, L0_attn_Wv, L0_attn_bv, L0_attn_r_kernel, L0_attn_r_w_bias, L0_attn_r_r_bias, L0_attn_Wo, L0_attn_bo, L0_attn_gamma, L0_attn_beta)
    h = h + _L0_ffn_ref(_layernorm(h, axis=-1), L0_ffn_slots, L0_ffn_scale, L0_ffn_fc1_weight, L0_ffn_fc1_bias, L0_ffn_fc2_weight, L0_ffn_fc2_bias, L0_ffn_norm_weight)
    h = h + _L1_attn_ref(_layernorm(h, axis=-1), L1_attn_ln1_g, L1_attn_ln1_b, L1_attn_in_proj_w, L1_attn_conv_w, L1_attn_conv_b, L1_attn_out_proj_w, L1_attn_ln2_g, L1_attn_ln2_b, L1_attn_qkv_w, L1_attn_qkv_b, L1_attn_attn_proj_w, L1_attn_attn_proj_b, L1_attn_ln3_g, L1_attn_ln3_b, L1_attn_ffn1_w, L1_attn_ffn1_b, L1_attn_ffn2_w, L1_attn_ffn2_b)
    h = h + _L1_ffn_ref(_layernorm(h, axis=-1), L1_ffn_router_w, L1_ffn_w1, L1_ffn_w2)
    h = h + _L2_attn_ref(_layernorm(h, axis=-1), L2_attn_w_q, L2_attn_w_k, L2_attn_w_v, L2_attn_w_o, L2_attn_b_o)
    h = h + _L2_ffn_ref(_layernorm(h, axis=-1), L2_ffn_in_weight, L2_ffn_in_bias, L2_ffn_out_weight)
    h = h + _L3_attn_ref(_layernorm(h, axis=-1), L3_attn_W_qkv, L3_attn_b_qkv)
    h = h + _L3_ffn_ref(_layernorm(h, axis=-1), L3_ffn_router_w, L3_ffn_w1, L3_ffn_b1, L3_ffn_w2, L3_ffn_b2)
    return h

_drawn_inputs = setup_inputs


def setup_inputs(seed=0):
    import zlib

    import numpy as np

    out = dict(_drawn_inputs(seed))
    spreads = {'L0_tok_conv_b': (0.0, 0.1),
     'L0_attn_bk': (0.0, 2.0),
     'L0_attn_bv': (0.0, 0.273),
     'L0_attn_bo': (0.0, 0.1),
     'L0_attn_gamma': (1.0, 0.2),
     'L0_attn_beta': (0.0, 0.1),
     'L0_ffn_scale': (1.0, 0.6),
     'L0_ffn_fc1_bias': (0.0, 0.8),
     'L0_ffn_fc2_bias': (0.0, 0.681),
     'L0_ffn_norm_weight': (1.0, 0.6),
     'L1_attn_ln1_g': (1.0, 0.6),
     'L1_attn_ln1_b': (0.0, 0.8),
     'L1_attn_conv_b': (0.0, 0.8),
     'L1_attn_ln2_g': (1.0, 0.6),
     'L1_attn_ln2_b': (0.0, 0.8),
     'L1_attn_qkv_b': (0.0, 0.39),
     'L1_attn_attn_proj_b': (0.0, 0.1),
     'L1_attn_ln3_g': (1.0, 0.6),
     'L1_attn_ln3_b': (0.0, 0.8),
     'L1_attn_ffn1_b': (0.0, 0.426),
     'L1_attn_ffn2_b': (0.0, 0.1),
     'L2_attn_b_o': (0.0, 0.1),
     'L3_attn_b_qkv': (0.0, 0.1),
     'L3_ffn_b1': (0.0, 0.8),
     'L3_ffn_b2': (0.0, 0.8)}
    factors = {'L0_attn_position_embeds': 8.0,
     'L0_attn_Wq': 8.0,
     'L0_attn_Wk': 8.0,
     'L0_attn_Wv': 8.0,
     'L0_attn_r_kernel': 8.0,
     'L0_attn_r_w_bias': 21.654,
     'L0_attn_r_r_bias': 8.0,
     'L0_ffn_slots': 8.0,
     'L0_ffn_fc1_weight': 8.0,
     'L0_ffn_fc2_weight': 8.0,
     'L1_attn_in_proj_w': 8.0,
     'L1_attn_conv_w': 8.0,
     'L1_attn_out_proj_w': 8.0,
     'L1_attn_qkv_w': 6.381,
     'L1_attn_attn_proj_w': 2.7,
     'L1_ffn_router_w': 8.388,
     'L2_attn_w_q': 8.0,
     'L2_attn_w_k': 8.0,
     'L2_attn_w_v': 4.221,
     'L2_attn_w_o': 4.237,
     'L2_ffn_in_bias': 5.872,
     'L3_ffn_router_w': 4.821,
     'L3_ffn_w1': 6.93,
     'L3_ffn_w2': 6.412,
     'L1_ffn_w1': 2.733,
     'L1_ffn_w2': 2.953}
    for name, (base, spread) in spreads.items():
        noise = np.random.default_rng([zlib.crc32(name.encode()), seed]).standard_normal(out[name].shape)
        drawn = base * np.exp(spread * noise) if base else spread * noise
        out[name] = jnp.asarray(drawn.astype(out[name].dtype))
    for name, factor in factors.items():
        out[name] = (out[name] * factor).astype(out[name].dtype)
    return out
```

```python
from contextlib import ExitStack, contextmanager

import numpy as np

import concourse.bass as bass
from concourse import mybir

F32 = mybir.dt.float32
I32 = mybir.dt.int32
ACT = mybir.ActivationFunctionType
ALU = mybir.AluOpType
AX = mybir.AxisListType

NB = 16
T = 102
NPATCH = 25
D = 192
KD = 96
GB = 4
NG = NB // GB
TG = GB * T
HEADS = 12
HPU = 3
UPB = HEADS // HPU
TU = HPU * T
FF = 768
FT = FF // 128
NSLOT = 64
NE = 8
I1 = 512
INNER = 384
CT3 = INNER // 128
KCONV = 4
RING = 4
NREL = 2 * T - 1
VOCAB = 50257
KP = 768
EPS = 1e-5

POS_PAIRS = ((0, 1), (3, 4), (2, 6), (5, 9), (7, 8), (10, 11))

MARKS = tuple(range(8))

W0_LOADS = 16 * (12 + 3 + 7)
W1_LOADS = 6 + 8 + 8
W2_LOADS = 8 + 7

SBANKS, TBANKS, OBANKS, XBANKS, FBANKS = (0, 1), (2, 3), (4, 5), (6, 7), (2, 3, 6, 7)


class Count:

    def __init__(self, who, notes):
        self.who, self.notes = who, notes
        self.total, self.turn, self.per = {}, {}, {}
        self.i = None
        self.loops = 0
        self.turns_of_banks = {}

    def now(self, name):
        n = self.total.get(name, 0) + self.turn.get(name, 0)
        per = self.per.get(name, 0)
        return n + self.i * per if self.i is not None and per else n

    def one(self, name, by=1):
        self.turn[name] = self.turn.get(name, 0) + by
        return by

    def take(self, name, by=1):
        self.one(name, by)
        return self.now(name)

    def bank(self, banks):
        n = self.turns_of_banks.get(banks, 0)
        self.turns_of_banks[banks] = n + 1
        return banks[n % len(banks)]

    def _settle(self, times):
        for name, n in self.turn.items():
            self.total[name] = self.total.get(name, 0) + n * times
        self.turn, self.per, self.turns_of_banks = {}, {}, {}
        self.i = None

    @contextmanager
    def loop(self, engine, times):
        self._settle(1)
        key = (self.who, self.loops)
        self.loops += 1
        self.per = dict(self.notes.get(key, {}))
        with engine.Fori(0, times) as i:
            self.i = i
            yield i
            self.notes[key] = dict(self.turn)
        self._settle(times)


def build(nc, t, out, scratch, flat, notes):
    ctx = ExitStack()
    with ctx:
        def sb(name, shape, dt=F32):
            return ctx.enter_context(nc.sbuf_tensor(name, shape, dt))

        sem = {}

        def signal(*names):
            for name in names:
                sem[name] = ctx.enter_context(nc.semaphore(name))

        H = sb("H", [T, NB, D])
        XN = sb("XN", [T, GB, D])
        X1 = sb("X1", [T, GB, D])
        XT = sb("XT", [KD, 2, TG])
        QT = sb("QT", [128, 6, TG])
        KT = sb("KT", [128, 6, TG])
        PB = [sb(f"PB{j}", [T, 4, T]) for j in range(2)]
        PT = [sb(f"PT{j}", [T, 4, T]) for j in range(2)]
        V = sb("V", [T, GB * HEADS * 65])
        ON = [sb(f"ON{j}", [T, FF]) for j in range(2)]
        OT = [sb(f"OT{j}", [128, 6, T]) for j in range(2)]
        HT = sb("HT", [128, FT, TG])
        W1 = [sb(f"W1_{r}", [KD, 2, FF]) for r in range(RING)]
        W2 = [sb(f"W2_{r}", [128, FT, D]) for r in range(RING)]
        SLOTS = sb("SLOTS", [128, 2 * 2 * NSLOT * NB + NB * T])
        YT = SLOTS[0:KD, 0:2048].rearrange("p (k s b) -> p k s b", k=2, s=NSLOT)
        Y2T = SLOTS[0:KD, 2048:4096].rearrange("p (k s b) -> p k s b", k=2, s=NSLOT)
        CT = SLOTS[0:NSLOT, 4096:4096 + NB * T].rearrange("p (b t) -> p b t", b=NB)
        per_slot = lambda buf: buf[:].rearrange("p h t -> p (h t)")[:, 0:GB * NSLOT].rearrange(
            "p (b s) -> p b s", b=GB)
        LG4, CW, DW = per_slot(PT[0]), per_slot(PB[1]), per_slot(PT[1])
        DP = PB[0][0:NSLOT, :, :]
        Y2 = [ON[j][0:NSLOT, 0:D] for j in range(2)]
        SL, SL2 = ON[0][0:NSLOT, D:2 * D], ON[1][0:NSLOT, D:2 * D]
        ident = sb("ident", [128, 128])
        ones = sb("ones", [128, 128])
        marked = sb("marked", [1, 8])
        amarked = sb("amarked", [1, 8])
        expo = sb("expo", [128, 2, GB])
        ST = sb("ST", [T, GB, 6])
        MV = sb("MV", [T, GB, 2])
        VE = sb("VE", [T, GB])
        RS = sb("RS", [T, GB])
        MX = sb("MX", [T, GB])
        SM = sb("SM", [T, GB])
        RC = sb("RC", [T, GB])
        TS = sb("TS", [T, GB])
        IDS = sb("IDS", [T, NB], I32)
        LG = sb("LG", [T, NB, NE])
        E1 = [QT[0:T, j, 0:NB * NE].rearrange("p (b e) -> p b e", b=NB) for j in range(6)]
        E2 = [sb(f"E2_{j}", [T, NB]) for j in range(3)]
        RUN = sb("RUN", [T, NE])
        ORDER = sb("ORDER", [T, NB, NE])
        WT8 = KT[0:NE, 0:4, :].rearrange("p k (b t) -> p (k b) t", b=4)

        AREA = sb("AREA", [128, 13620])

        def area():
            at = [0]

            def piece(parts, *shape):
                n = int(np.prod(shape))
                ap = AREA[0:parts, at[0]:at[0] + n]
                at[0] += n
                assert at[0] <= 13620
                if len(shape) == 2:
                    ap = ap.rearrange("p (a b) -> p a b", a=shape[0])
                elif len(shape) == 3:
                    ap = ap.rearrange("p (a b c) -> p a b c", a=shape[0], b=shape[1])
                return ap
            return piece

        a0 = area()
        wq0, wk0, wv0 = a0(KD, 2, 384), a0(KD, 2, 384), a0(KD, 2, KD)
        rker, posT, RT = a0(KD, 2, FF), a0(KD, 2, NREL), a0(128, 6, NREL)
        wo0 = a0(KD, 2, D)
        rw0, rr0, bk0 = a0(128, 6), a0(128, 6), a0(128, 6)
        bv0, bo0, gamma0, beta0 = a0(T, D), a0(T, D), a0(T, D), a0(T, D)
        QR = a0(128, 6, TG)
        PR = a0(T, HEADS, NREL)
        POS = [a0(T, HEADS, T) for _ in range(2)]
        patchT = HT[:, :, 0:NB * NPATCH].rearrange("p k (b n) -> p k b n", b=NB)
        convT = KT[:, :, 0:D]
        posE = ON[0][0:NPATCH, 2 * D:4 * D].rearrange("p (a d) -> p a d", a=2)
        slS = sb("slS", [NSLOT, 1])
        slT = sb("slT", [KD, 2, NSLOT])
        nw0 = sb("nw0", [T, D])
        fb1 = sb("fb1", [128, NSLOT, FT])
        fb2 = sb("fb2", [KD, 2, NSLOT])

        a1 = area()
        XALL = a1(KD, 2, NB * T)
        win1, wout1 = a1(KD, 2, 2 * INNER), a1(128, CT3, D)
        cw1, cb1 = a1(128, CT3, KCONV), a1(128, CT3)
        g1 = a1(KD, 3, 2)
        b1 = a1(KD, 3, 2)
        wqkv1, wqk1 = a1(KD, 2, 3 * D), a1(KD, 2, 2 * 384)
        bqk1, bv1 = a1(128, 6), a1(T, D)
        wp1, bp1 = a1(KD, 2, D), a1(T, D)
        wf1, bf1, wf2, bf2 = a1(KD, 2, FF), a1(128, FT), a1(128, FT, D), a1(T, D)
        rt1 = sb("rt1", [KD, 2, NE])

        a2 = area()
        a2(KD, 2, NB * T)
        wq2, wk2, wv2 = a2(KD, 2, FF), a2(KD, 2, FF), a2(KD, 2, FF)
        wo2, bo2 = a2(128, 6, D), a2(T, D)
        wi2, bi2, wu2 = a2(KD, 2, FF), a2(128, FT), a2(128, FT, D)
        wqkv3, bqk3, bv3 = a2(KD, 2, 3 * D), a2(KD, 4), a2(T, D)
        decay = a2(T, T)
        rt3, bb1, bb2 = a2(KD, 2, NE), a2(128, NE, FT), a2(NE, D)

        psum = [ctx.enter_context(nc.psum_tensor(f"bank{k}", [128, 512], F32)) for k in range(8)]

        for k in range(8):
            signal(f"bank_full{k}", f"bank_free{k}")
        for r in range(RING):
            signal(f"w1_loaded{r}", f"w1_used{r}", f"w2_loaded{r}", f"w2_used{r}")
        signal("patches_loaded", "ids_loaded", "words_loaded", "w0_loaded", "w1_loaded", "w2_loaded",
               "slots_loaded",
               "constants_ready", "area_cleared", "w0_cleared", "padded",
               "vector_step", "pool_step",
               "vector_passed", "tensor_passed",
               "power_in", "power_out",
               "xn_ready",
               "xt_ready",
               "xt_copied",
               "scores_ready",
               "probs_in", "probs_ready",
               "exp_ready",
               "pr_ready", "pr_stored", "pos_loaded0", "pos_loaded1", "pos_used",
               "conv_ready", "gate_ready", "gated",
               "slot_in", "yt_ready",
               "attn0_done", "attn1_done",
               "router_ready", "out_ready", "out_stored")

        block = ctx.enter_context(nc.Block())

        def head(buf, h, per_tile, dk, cols):
            unit, j = h // HPU, h % HPU
            p = (unit % per_tile) * (128 // per_tile)
            return buf[p:p + dk, (unit // per_tile) * HPU + j, cols]

        def cols(bb):
            return slice(bb * T, (bb + 1) * T)

        UNITS = GB * UPB
        STEPS = UNITS + 4

        def last_of(step):
            return step // UPB if 0 <= step < UNITS and step % UPB == UPB - 1 else None

        @block.sync
        def _(sp):
            at = Count("sp", notes)

            def load(dst, src, name):
                sp.dma_start(dst, src).then_inc(sem[name], at.one(name, 16))

            sp.sem_inc(sem["pr_stored"], at.one("pr_stored", 16))
            at.one("pos_used")

            load(patchT, t["patchT"], "patches_loaded")
            load(convT, t["convT"], "patches_loaded")
            load(posE[:, 0, :], t["pos_rows"], "patches_loaded")
            load(posE[:, 1, :], t["conv_b"], "patches_loaded")
            sp.wait_ge(sem["w0_cleared"], 3)
            for g in range(4):
                rows = slice((g % 2) * 48, (g % 2) * 48 + 48)
                for w, name in ((wq0, "Wq"), (wk0, "Wk")):
                    tiles = w[rows, g // 2, :].rearrange("p (j two d) -> p j two d", j=HPU, two=2)
                    load(tiles[:, :, g % 2, :], t[name][g].rearrange("i (j d) -> i j d", j=HPU), "w0_loaded")
                load(wv0[rows, g // 2, (g % 2) * 48:(g % 2) * 48 + 48], t["Wv"][g], "w0_loaded")
            load(rker, t["r_kernel"].rearrange("(k p) n -> p k n", p=KD), "w0_loaded")
            load(posT, t["posT"].rearrange("(k p) n -> p k n", p=KD), "w0_loaded")
            load(wo0, t["Wo"].rearrange("(k p) n -> p k n", p=KD), "w0_loaded")
            for dst, name in ((rw0, "r_w_bias"), (rr0, "r_r_bias"), (bk0, "bk"), (bv0, "bv"), (bo0, "bo"),
                              (gamma0, "gamma"), (beta0, "beta")):
                load(dst, t[name], "w0_loaded")
            for dst, name in ((SL, "slots"), (slS, "slot_scale"), (nw0, "norm_weight"), (fb1, "fc1_bias"),
                              (fb2, "fc2_bias"), (rt1, "router1")):
                load(dst if name == "slots" else dst[:], t[name], "slots_loaded")

            def fill(r, w1, w2, rounds=1):
                sp.wait_ge(sem[f"w1_used{r}"], at.now(f"w1_used{r}"))
                at.one(f"w1_used{r}", rounds)
                sp.dma_start(W1[r][:, :, 0:w1.shape[1]], w1.rearrange("(k p) f -> p k f", p=KD)
                             ).then_inc(sem[f"w1_loaded{r}"], 16)
                sp.wait_ge(sem[f"w2_used{r}"], at.now(f"w2_used{r}"))
                at.one(f"w2_used{r}")
                k2 = w2.shape[0] // 128
                sp.dma_start(W2[r][:, 0:k2, :], w2.rearrange("(k p) o -> p k o", p=128)
                             ).then_inc(sem[f"w2_loaded{r}"], 16)

            for r in range(RING):
                fill(r, t["fc1"][r], t["fc2"][r])

            with at.loop(sp, NG) as g:
                for bb in range(GB):
                    here = scratch[bass.ds(g * GB + bb, 1)].rearrange("o t n -> (o t) n")
                    sp.wait_ge(sem["pr_ready"], at.take("pr_ready"))
                    sp.dma_start(here, PR.rearrange("p h n -> p (h n)")
                                 ).then_inc(sem["pr_stored"], at.one("pr_stored", 16))
                    sp.wait_ge(sem["pr_stored"], at.now("pr_stored"))
                    if bb < 2:
                        sp.wait_ge(sem["pos_used"], at.now("pos_used"))
                    else:
                        sp.wait_ge(sem["pos_used"], at.take("pos_used"))
                    row = HEADS * NREL
                    shifted = bass.AP(tensor=flat.tensor, offset=(g * GB + bb) * (T * row) + (T - 1),
                                      ap=[[row - 1, T], [NREL, HEADS], [1, T]])
                    sp.dma_start(POS[bb % 2], shifted).then_inc(sem[f"pos_loaded{bb % 2}"], 16)
                for _ in range(2):
                    at.one("pos_used")

            with at.loop(sp, NSLOT // RING - 1) as j:
                for r in range(RING):
                    s = bass.ds(j * RING + RING + r, 1)
                    fill(r, t["fc1"][s].rearrange("o i f -> (o i) f"), t["fc2"][s].rearrange("o i f -> (o i) f"))
            for e in range(NE):
                fill(e % RING, t["m1w1"][e], t["m1w2"][e], NG)
            for e in range(NE):
                fill(e % RING, t["m3w1"][e], t["m3w2"][e], NG)

            with at.loop(sp, NG) as g:
                sp.wait_ge(sem["out_ready"], at.take("out_ready"))
                sp.dma_start(out[:, bass.ds(g * GB, GB), :], H[:, bass.ds(g * GB, GB), :]
                             ).then_inc(sem["out_stored"], at.one("out_stored", 16))
            sp.wait_ge(sem["out_stored"], 16 * NG)

        @block.gpsimd
        def _(pool):
            at = Count("pool", notes)

            def step(ins):
                ins.then_inc(sem["pool_step"], at.one("pool_step"))
                pool.wait_ge(sem["pool_step"], at.now("pool_step"))

            pool.dma_start(IDS[:], t["ids"]).then_inc(sem["ids_loaded"], 16)
            for w in (wq0, wk0, wv0):
                pool.memset(w, 0.0).then_inc(sem["w0_cleared"], 1)
            step(pool.memset(H[:], 0.0))
            pool.wait_ge(sem["ids_loaded"], 16)
            for b in range(NB):
                pool.indirect_dma_start(H[:, b, :], None, t["words"],
                                        bass.IndirectOffsetOnAxis(ap=IDS[:, b:b + 1], axis=0),
                                        bounds_check=VOCAB - 1, oob_is_err=False
                                        ).then_inc(sem["words_loaded"], 16)
            step(pool.memset(ident[:], 0.0))
            step(pool.affine_select(out=ident[:], in_=ident[:], compare_op=ALU.not_equal, fill=1.0, base=0,
                                    pattern=[[-1, 128]], channel_multiplier=1))
            pool.memset(ones[:], 1.0)
            pool.memset(expo[:, 0, :], -0.5)
            pool.memset(expo[:, 1, :], 0.5)
            pool.memset(V[:], 1.0)
            for e in range(NE):
                last = pool.memset(ORDER[:, :, e:e + 1], float(NE - e))
            last.then_inc(sem["constants_ready"], 1)

            def power(half, rows=T, width=GB):
                pool.wait_ge(sem["power_in"], at.take("power_in"))
                pool.tensor_tensor(RS[0:rows, 0:width], VE[0:rows, 0:width], expo[0:rows, half, 0:width],
                                   ALU.pow).then_inc(sem["power_out"], at.one("power_out"))

            power(1, NSLOT, 1)
            with at.loop(pool, NG):
                power(0)
                power(0)

            pool.wait_ge(sem["attn0_done"], 1)
            step(pool.memset(wqk1, 0.0))
            step(pool.memset(bqk1, 0.0))

            def load(dst, src, name):
                pool.dma_start(dst, src).then_inc(sem[name], at.one(name, 16))

            for dst, name, p in ((win1, "in_proj", KD), (wout1, "out_proj", 128), (wqkv1, "qkv1", KD),
                                 (wp1, "proj1", KD), (wf1, "ffn1", KD), (wf2, "ffn2", 128)):
                load(dst, t[name].rearrange("(k p) n -> p k n", p=p), "w1_loaded")
            for dst, name in ((cw1, "conv1_w"), (cb1, "conv1_b"), (g1, "ln_g"), (b1, "ln_b"), (bv1, "v1_b"),
                              (bp1, "proj1_b"), (bf1, "ffn1_b"), (bf2, "ffn2_b")):
                load(dst, t[name], "w1_loaded")
            for q in range(2):
                for u in range(UPB):
                    load(bqk1[32 * u:32 * u + 16, 3 * q:3 * q + 3], t["qk1_b"][q, u], "w1_loaded")
            pool.wait_ge(sem["w1_loaded"], at.now("w1_loaded"))
            for k in range(2):
                for q in range(2):
                    dst = wqk1[:, k, q * 384:(q + 1) * 384].rearrange("p (j u d) -> p u j d", j=HPU, d=32)
                    src = wqkv1[:, k, q * D:(q + 1) * D].rearrange("p (u j d) -> p u j d", j=HPU, d=16)
                    last = pool.tensor_copy(dst[:, :, :, 0:16], src)
            last.then_inc(sem["padded"], 1)

            with at.loop(pool, NG):
                power(0)
                power(0)
                power(1)
            with at.loop(pool, NG):
                power(0)
                power(0)
                for c in range(CT3):
                    pool.wait_ge(sem["gate_ready"], at.take("gate_ready"))
                    pool.tensor_tensor(QT[:, c, :], HT[:, c, :], HT[:, 3 + c, :], ALU.mult
                                       ).then_inc(sem["gated"], at.one("gated"))
                power(0)
                power(0)

            def router_copies():
                with at.loop(pool, NG) as g:
                    power(0)
                    pool.wait_ge(sem["xt_ready"], at.take("xt_ready"))
                    pool.tensor_copy(XALL[:, :, bass.ds(g * TG, TG)], XT[:]
                                     ).then_inc(sem["xt_copied"], at.one("xt_copied"))

            pool.wait_ge(sem["attn1_done"], 1)
            for dst, name, p in ((wq2, "q2", KD), (wk2, "k2", KD), (wv2, "v2", KD), (wo2, "o2", 128),
                                 (wi2, "in2", KD), (wu2, "up2", 128), (wqkv3, "qkv3", KD), (rt3, "router3", KD)):
                load(dst, t[name].rearrange("(k p) n -> p k n", p=p), "w2_loaded")
            for dst, name in ((bo2, "o2_b"), (bi2, "in2_b"), (bqk3, "qk3_b"), (bv3, "v3_b"), (decay, "decay"),
                              (bb1, "m3b1"), (bb2, "m3b2")):
                load(dst, t[name], "w2_loaded")
            pool.memset(V[:], 1.0).then_inc(sem["constants_ready"], 1)
            router_copies()
            with at.loop(pool, NG):
                power(0)
            with at.loop(pool, NG):
                power(0)
                power(0)
            router_copies()

        @block.vector
        def _(dve):
            at = Count("dve", notes)
            at.one("yt_ready")
            tt, ts, stt = dve.tensor_tensor, dve.tensor_scalar, dve.scalar_tensor_tensor

            def step(ins):
                ins.then_inc(sem["vector_step"], at.one("vector_step"))
                dve.wait_ge(sem["vector_step"], at.now("vector_step"))

            def give(ins, name):
                ins.then_inc(sem[name], at.one(name))

            def full(k):
                dve.wait_ge(sem[f"bank_full{k}"], at.take(f"bank_full{k}"))
                return psum[k]

            def mark(name):
                n = at.bank(MARKS)
                give(dve.memset(marked[:, n:n + 1], 0.0), name)

            def free(ins, k):
                ins.then_inc(sem[f"bank_free{k}"], at.one(f"bank_free{k}"))
                dve.wait_ge(sem[f"bank_free{k}"], at.now(f"bank_free{k}"))

            def power(ins):
                give(ins, "power_in")
                dve.wait_ge(sem["power_out"], at.take("power_out"))

            def wide(ap, n):
                return ap.unsqueeze(2).to_broadcast([ap.shape[0], ap.shape[1], n])

            def layernorm(src, dst, eps=EPS, name=None):
                dve.sem_inc(sem["vector_passed"], 1)
                for bb in range(GB):
                    last = dve.bn_stats(ST[:, bb, :], src(bb))
                step(last)
                dve.sem_inc(sem["vector_passed"], 1)
                for bb in range(GB):
                    last = dve.bn_aggr(MV[:, bb, :], ST[:, bb, :])
                step(last)
                power(ts(VE[:], MV[:, :, 1], eps, None, ALU.add))
                for bb in range(GB):
                    last = ts(dst(bb), src(bb), MV[:, bb, 0:1], RS[:, bb:bb + 1], ALU.subtract, ALU.mult)
                if name:
                    give(last, name)
                    dve.wait_ge(sem[name], at.now(name))
                else:
                    step(last)

            xn = lambda bb: XN[:, bb, :]
            x1 = lambda bb: X1[:, bb, :]

            def h_of(g):
                return lambda bb: H[:, bass.ds(g * GB + bb, 1), :].rearrange("p o d -> p (o d)")

            def softmax_unit(n, pos):
                k = at.bank(SBANKS)
                dve.wait_ge(sem["scores_ready"], at.take("scores_ready"))
                scores = psum[k][0:T, 0:TU].rearrange("p (h t) -> p h t", h=HPU)
                p = PB[n % 2][:, 0:HPU, :]
                bb, unit = n // UPB, n % UPB
                if pos:
                    if unit == 0:
                        dve.wait_ge(sem[f"pos_loaded{bb % 2}"], at.take(f"pos_loaded{bb % 2}", 16))
                    ins = tt(p, scores, POS[bb % 2][:, HPU * unit:HPU * unit + HPU, :], ALU.add)
                    if unit == UPB - 1:
                        give(ins, "pos_used")
                        dve.wait_ge(sem["pos_used"], at.now("pos_used"))
                    else:
                        step(ins)
                    scores = p
                step(dve.tensor_reduce(MX[:, 0:HPU], scores, AX.X, ALU.max))
                give(tt(p, scores, wide(MX[:, 0:HPU], T), ALU.subtract), "probs_in")
                dve.wait_ge(sem["probs_in"], at.now("probs_in"))

            def norm_unit(n, dv):
                bb, unit = n // UPB, n % UPB
                k = at.bank(OBANKS)
                o = full(k)[0:T, 0:HPU * (dv + 1)].rearrange("p (h d) -> p h d", h=HPU)
                step(dve.reciprocal(RC[:, 0:HPU], o[:, :, dv]))
                on = ON[bb % 2][:, 0:HEADS * dv].rearrange("p (h d) -> p h d", d=dv)
                free(tt(on[:, HPU * unit:HPU * unit + HPU, :], o[:, :, 0:dv], wide(RC[:, 0:HPU], dv), ALU.mult), k)

            def attention(dv, pos, finish):
                for s in range(STEPS):
                    if s < UNITS:
                        softmax_unit(s, pos)
                    if 0 <= s - 2 < UNITS:
                        norm_unit(s - 2, dv)
                    if last_of(s - 4) is not None:
                        bb = last_of(s - 4)
                        k = at.bank(OBANKS)
                        finish(bb, full(k)[0:T, 0:D], k)

            def values(v, dv, bias):
                per = 2 * D // dv
                v5 = V[:, 0:GB * HEADS * (dv + 1)].rearrange("p (h d) -> p h d", d=dv + 1)
                for first in range(0, GB * HEADS, per):
                    k = at.bank(OBANKS)
                    src = full(k)[0:T, 0:per * dv].rearrange("p (h d) -> p h d", d=dv)
                    if bias is None:
                        last = dve.tensor_copy(v5[:, first:first + per, 0:dv], src)
                    else:
                        for j in range(per // HEADS):
                            last = tt(v5[:, first + j * HEADS:first + (j + 1) * HEADS, 0:dv],
                                      src[:, j * HEADS:(j + 1) * HEADS, :],
                                      bias.rearrange("p (h d) -> p h d", d=dv), ALU.add)
                    free(last, k)

            def pairs(consume):
                for first in range(0, GB, 2):
                    k = at.bank(OBANKS)
                    o = full(k)
                    last = None
                    for bb in (first, first + 1):
                        last = consume(bb, o[0:T, (bb - first) * D:(bb - first + 1) * D])
                    free(last, k)

            for k in SBANKS + OBANKS:
                dve.sem_inc(sem[f"bank_free{k}"], at.one(f"bank_free{k}"))
            dve.sem_inc(sem["pos_used"], at.one("pos_used"))

            dve.wait_ge(sem["slots_loaded"], 16 * 6)
            dve.wait_ge(sem["constants_ready"], 1)
            step(dve.tensor_tensor_reduce(out=SL2, in0=SL, in1=SL, scale=1.0, scalar=0.0,
                                          op0=ALU.mult, op1=ALU.add, accum_out=SM[0:NSLOT, 0:1]))
            power(ts(VE[0:NSLOT, 0:1], SM[0:NSLOT, 0:1], 1.0, None, ALU.mult))
            step(ts(MX[0:NSLOT, 0:1], RS[0:NSLOT, 0:1], EPS, None, ALU.max))
            step(dve.reciprocal(RC[0:NSLOT, 0:1], MX[0:NSLOT, 0:1]))
            give(ts(SL2, SL, RC[0:NSLOT, 0:1], slS[:, 0:1], ALU.mult, ALU.mult), "xn_ready")

            dve.wait_ge(sem["patches_loaded"], 64)
            dve.wait_ge(sem["words_loaded"], 16 * NB)
            step(tt(posE[:, 0, :], posE[:, 0, :], posE[:, 1, :], ALU.add))
            for first in range(0, NB, 2):
                k = at.bank(OBANKS)
                o = full(k)[0:NPATCH, 0:2 * D].rearrange("p (b d) -> p b d", b=2)
                for j in range(2):
                    last = tt(H[0:NPATCH, first + j, :], o[:, j, :], posE[:, 0, :], ALU.add)
                free(last, k)

            dve.wait_ge(sem["w0_loaded"], W0_LOADS)
            with at.loop(dve, NG) as g:
                h = h_of(g)
                layernorm(h, xn, name="xn_ready")
                values(V, 16, bv0)

                def finish(bb, o, k):
                    free(tt(X1[:, bb, :], o, XN[:, bb, :], ALU.add), k)
                    step(tt(X1[:, bb, :], X1[:, bb, :], bo0, ALU.add))

                attention(16, True, finish)
                layernorm(x1, x1, eps=1e-9)
                for bb in range(GB):
                    step(tt(X1[:, bb, :], X1[:, bb, :], gamma0, ALU.mult))
                    step(tt(X1[:, bb, :], X1[:, bb, :], beta0, ALU.add))
                    step(tt(h(bb), h(bb), x1(bb), ALU.add))
            mark("attn0_done")

            with at.loop(dve, NG) as g:
                layernorm(h_of(g), x1)
                dve.wait_ge(sem["yt_ready"], at.now("yt_ready"))
                at.one("yt_ready")
                for bb in range(GB):
                    last = dve.tensor_tensor_reduce(out=XN[:, bb, :], in0=X1[:, bb, :], in1=X1[:, bb, :],
                                                    scale=1.0 / D, scalar=0.0, op0=ALU.mult, op1=ALU.add,
                                                    accum_out=SM[:, bb:bb + 1])
                step(last)
                power(ts(VE[:], SM[:], EPS, None, ALU.add))
                for bb in range(GB):
                    last = stt(XN[:, bb, :], X1[:, bb, :], RS[:, bb:bb + 1], nw0[:], ALU.mult, ALU.mult)
                give(last, "xn_ready")
                dve.wait_ge(sem["xn_ready"], at.now("xn_ready"))
                for bb in range(GB):
                    last = dve.tensor_tensor_reduce(out=X1[:, bb, :], in0=XN[:, bb, :], in1=XN[:, bb, :],
                                                    scale=1.0, scalar=0.0, op0=ALU.mult, op1=ALU.add,
                                                    accum_out=SM[:, bb:bb + 1])
                step(last)
                power(ts(VE[:], SM[:], 1.0, None, ALU.mult))
                step(ts(TS[:], RS[:], EPS, None, ALU.max))
                step(dve.reciprocal(TS[:], TS[:]))
                k = at.bank(OBANKS)
                o = full(k)[0:T, 0:GB * NSLOT].rearrange("p (b s) -> p b s", b=GB)
                free(tt(LG4, o, wide(TS[:], NSLOT), ALU.mult), k)
                give(dve.tensor_reduce(MX[:], LG4, AX.X, ALU.max), "slot_in")
                dve.wait_ge(sem["slot_in"], at.now("slot_in"))
                give(tt(CW, LG4, wide(MX[:], NSLOT), ALU.subtract), "probs_in")
                dve.wait_ge(sem["probs_in"], at.now("probs_in"))
                k = at.bank(SBANKS)
                dve.wait_ge(sem["scores_ready"], at.take("scores_ready"))
                o = psum[k][0:NSLOT, 0:TG].rearrange("p (b t) -> p b t", b=GB)
                step(dve.tensor_reduce(MX[0:NSLOT, :], o, AX.X, ALU.max))
                give(tt(DP, o, wide(MX[0:NSLOT, :], T), ALU.subtract), "probs_in")
                dve.wait_ge(sem["exp_ready"], at.take("exp_ready"))
                step(dve.tensor_reduce(SM[:], CW, AX.X, ALU.add))
                step(dve.reciprocal(RC[:], SM[:]))
                give(tt(CW, CW, wide(RC[:], NSLOT), ALU.mult), "slot_in")
                dve.wait_ge(sem["exp_ready"], at.take("exp_ready"))
                step(dve.tensor_reduce(SM[0:NSLOT, :], DP, AX.X, ALU.add))
                step(dve.reciprocal(RC[0:NSLOT, :], SM[0:NSLOT, :]))
                give(tt(DP, DP, wide(RC[0:NSLOT, :], T), ALU.mult), "slot_in")

            with at.loop(dve, NSLOT // RING) as j:
                for half in range(2):
                    k = at.bank(SBANKS)
                    dve.wait_ge(sem["scores_ready"], at.take("scores_ready"))
                    o = psum[k][:, 0:2 * FT * NB].rearrange("p (a b) -> p a b", b=NB)
                    bias = fb1[:, bass.ds(j * RING + 2 * half, 2), :].rearrange("p s k -> p (s k)")
                    dst = HT[:, half, 0:2 * FT * NB].rearrange("p (a b) -> p a b", b=NB)
                    give(tt(dst, o, wide(bias, NB), ALU.add), "probs_in")
                for half in range(2):
                    k = at.bank(OBANKS)
                    o = full(k)[0:KD, 0:4 * NB].rearrange("p (s m b) -> p s m b", s=2, m=2)
                    for m in range(2):
                        where = bass.ds(j * RING + 2 * half, 2)
                        last = tt(Y2T[:, m, where, :], o[:, :, m, :], wide(fb2[:, m, where], NB), ALU.add)
                    free(last, k)
                    mark(f"w2_used{2 * half}")
                    mark(f"w2_used{2 * half + 1}")

            for first in range(0, NB, 2):
                k = at.bank(OBANKS)
                o = full(k)[0:T, 0:2 * D].rearrange("p (b d) -> p b d", b=2)
                free(tt(H[:, first:first + 2, :], H[:, first:first + 2, :], o, ALU.add), k)

            dve.wait_ge(sem["padded"], 1)
            with at.loop(dve, NG) as g:
                h = h_of(g)
                layernorm(h, x1)
                layernorm(x1, xn, name="xn_ready")
                for c in range(CT3):
                    k = at.bank(SBANKS)
                    src = full(k)[:, 0:TG].rearrange("p (b t) -> p b t", b=GB)
                    y = HT[:, c, :].rearrange("p (b t) -> p b t", b=GB)
                    step(ts(y, src, cw1[:, c, 3:4], cb1[:, c:c + 1], ALU.mult, ALU.add))
                    for lag in (1, 2):
                        step(stt(y[:, :, lag:], src[:, :, :T - lag], cw1[:, c, 3 - lag:4 - lag],
                                 y[:, :, lag:], ALU.mult, ALU.add))
                    give(stt(y[:, :, 3:], src[:, :, :T - 3], cw1[:, c, 0:1], y[:, :, 3:],
                             ALU.mult, ALU.add), "conv_ready")
                    mark(f"bank_free{k}")
                pairs(lambda bb, o: tt(X1[:, bb, :], X1[:, bb, :], o, ALU.add))
                layernorm(x1, xn, name="xn_ready")
                values(V, 16, bv1)

                def finish(bb, o, k):
                    free(tt(X1[:, bb, :], X1[:, bb, :], o, ALU.add), k)
                    step(tt(X1[:, bb, :], X1[:, bb, :], bp1, ALU.add))

                attention(16, False, finish)
                layernorm(x1, xn, name="xn_ready")
                pairs(lambda bb, o: tt(X1[:, bb, :], X1[:, bb, :], o, ALU.add))
                for bb in range(GB):
                    step(tt(X1[:, bb, :], X1[:, bb, :], bf2, ALU.add))
                    step(tt(h(bb), h(bb), x1(bb), ALU.add))
            mark("attn1_done")

            def router_inputs():
                with at.loop(dve, NG) as g:
                    layernorm(h_of(g), xn, name="xn_ready")
                    k = at.bank(OBANKS)
                    o = full(k)[0:T, 0:GB * NE].rearrange("p (b e) -> p b e", b=GB)
                    free(dve.tensor_copy(LG[:, bass.ds(g * GB, GB), :], o), k)

            def probabilities():
                step(dve.tensor_reduce(E2[0][:], LG[:], AX.X, ALU.max))
                give(tt(E1[0], LG[:], wide(E2[0][:], NE), ALU.subtract), "probs_in")
                dve.wait_ge(sem["exp_ready"], at.take("exp_ready"))
                step(dve.tensor_reduce(E2[0][:], E1[0], AX.X, ALU.add))
                step(dve.reciprocal(E2[1][:], E2[0][:]))
                step(tt(E1[0], E1[0], wide(E2[1][:], NE), ALU.mult))

            def best_two():
                step(dve.tensor_copy(E1[2], E1[0]))
                for n in range(2):
                    step(dve.tensor_reduce(E2[0][:], E1[2], AX.X, ALU.max))
                    step(tt(E1[3], E1[2], wide(E2[0][:], NE), ALU.is_equal))
                    step(tt(E1[3], E1[3], ORDER[:], ALU.mult))
                    step(dve.tensor_reduce(E2[1][:], E1[3], AX.X, ALU.max))
                    step(tt(E1[4 + n], ORDER[:], wide(E2[1][:], NE), ALU.is_equal))
                    if n == 0:
                        step(stt(E1[2], E1[4], -2.0, E1[2], ALU.mult, ALU.add))
                step(tt(E1[4], E1[4], E1[5], ALU.add))
                step(tt(E1[1], E1[0], E1[4], ALU.mult))

            def share():
                step(dve.tensor_reduce(E2[0][:], E1[1], AX.X, ALU.add))
                step(dve.reciprocal(E2[1][:], E2[0][:]))
                step(tt(E1[1], E1[1], wide(E2[1][:], NE), ALU.mult))

            def experts():
                for e in range(NE):
                    with at.loop(dve, NG) as g:
                        for bb0 in range(0, GB, 2):
                            k = at.bank(OBANKS)
                            o = full(k)
                            for j in range(2):
                                w = E1[1][:, bass.ds(g * GB + bb0 + j, 1), e]
                                hh = h_of(g)(bb0 + j)
                                last = stt(hh, o[0:T, j * D:(j + 1) * D], w, hh, ALU.mult, ALU.add)
                            free(last, k)
                    mark(f"w2_used{e % RING}")

            router_inputs()
            probabilities()
            mark("router_ready")
            best_two()
            k = at.bank(OBANKS)
            o = full(k)[0:T, 0:NB * NE].rearrange("p (b e) -> p e b", e=NE)
            free(dve.tensor_reduce(RUN[:], o, AX.X, ALU.add), k)
            step(ts(RUN[:], RUN[:], -1.0, 1.0 - 0.9, ALU.add, ALU.mult))
            step(ts(RUN[:], RUN[:], 1.0, 0.01, ALU.add, ALU.add))
            step(dve.reciprocal(RUN[:], RUN[:]))
            step(tt(E1[1], E1[1], RUN[:].unsqueeze(1).to_broadcast([T, NB, NE]), ALU.mult))
            share()
            experts()

            dve.wait_ge(sem["w2_loaded"], 16 * W2_LOADS)
            dve.wait_ge(sem["constants_ready"], 2)
            with at.loop(dve, NG) as g:
                h = h_of(g)
                layernorm(h, xn, name="xn_ready")
                values(V, 64, None)

                def finish(bb, o, k):
                    free(tt(h(bb), h(bb), o, ALU.add), k)
                    step(tt(h(bb), h(bb), bo2, ALU.add))

                attention(64, False, finish)

            with at.loop(dve, NG) as g:
                h = h_of(g)
                layernorm(h, xn, name="xn_ready")
                pairs(lambda bb, o: tt(h(bb), h(bb), o, ALU.add))
                layernorm(h, xn, name="xn_ready")
                for first in range(0, GB, 2):
                    k = at.bank(OBANKS)
                    o = full(k)
                    for bb in (first, first + 1):
                        last = tt(V[:, bb * D:(bb + 1) * D], o[0:T, (bb - first) * D:(bb - first + 1) * D],
                                  bv3, ALU.add)
                    free(last, k)
                k = at.bank(SBANKS)
                o = full(k)[0:T, 0:TG].rearrange("p (b t) -> p b t", b=GB)
                free(stt(PT[0][:], o, float(np.float32(1) / np.sqrt(np.float32(D))),
                         decay.unsqueeze(1).to_broadcast([T, GB, T]), ALU.mult, ALU.mult), k)
                pairs(lambda bb, o: tt(h(bb), h(bb), o, ALU.add))

            router_inputs()
            probabilities()
            best_two()
            share()
            mark("router_ready")
            for first in range(0, NB, 2):
                k = at.bank(OBANKS)
                o = full(k)[0:T, 0:2 * D].rearrange("p (b d) -> p b d", b=2)
                free(tt(H[:, first:first + 2, :], H[:, first:first + 2, :], o, ALU.add), k)
            experts()
            for _ in range(NG):
                mark("out_ready")

        @block.scalar
        def _(act):
            at = Count("act", notes)
            activation = act.activation

            def give(ins, name):
                ins.then_inc(sem[name], at.one(name))

            def full(k):
                act.wait_ge(sem[f"bank_full{k}"], at.take(f"bank_full{k}"))
                return psum[k]

            def free(ins, k):
                give(ins, f"bank_free{k}")

            def mark(name):
                n = at.bank(MARKS)
                give(activation(amarked[:, n:n + 1], ident[0:1, 0:1], ACT.Copy), name)

            def turned(dst, scale=None, bias=None):
                for part in range(2):
                    k = at.bank(XBANKS)
                    src = full(k)[0:KD, 0:TG]
                    if scale is None:
                        free(activation(dst[:, part, :], src, ACT.Copy), k)
                    else:
                        free(activation(dst[:, part, :], src, ACT.Identity, scale=scale[:, part:part + 1],
                                        bias=bias[:, part:part + 1]), k)

            def hidden(tiles, func, bias, src_ready=None):
                for m in range(tiles):
                    k = at.bank(FBANKS)
                    src = full(k)[:, 0:TG]
                    free(activation(HT[:, m, :], src, func, bias=0.0 if bias is None else bias(m)), k)

            def exponentials(buf, scale=1.0, name="probs_ready"):
                act.wait_ge(sem["probs_in"], at.take("probs_in"))
                give(activation(buf, buf, ACT.Exp, scale=scale), name)

            def attention(dv, scale, pos=None):
                for s in range(STEPS):
                    if s < UNITS:
                        exponentials(PB[s % 2][:, 0:HPU, :], scale)
                    if 0 <= s - 1 < UNITS:
                        k = at.bank(TBANKS)
                        src = full(k)[0:T, 0:TU].rearrange("p (h t) -> p h t", h=HPU)
                        free(activation(PT[(s - 1) % 2][:, 0:HPU, :], src, ACT.Copy), k)
                    if last_of(s - 3) is not None:
                        ot = OT[last_of(s - 3) % 2]
                        rows, tiles = (KD, 2) if dv == 16 else (128, 3)
                        for first in range(0, HEADS * dv // rows, tiles):
                            k = at.bank(XBANKS)
                            src = full(k)[0:rows, 0:tiles * T].rearrange("p (k t) -> p k t", k=tiles)
                            free(activation(ot[0:rows, first:first + tiles, :], src, ACT.Copy), k)
                    if pos and s in (UPB, 2 * UPB):
                        pos()

            for k in TBANKS + XBANKS:
                act.sem_inc(sem[f"bank_free{k}"], 1)
            act.sem_inc(sem["yt_ready"], 1)

            act.wait_ge(sem["constants_ready"], 1)
            k = at.bank(XBANKS)
            src = full(k)[0:KD, 0:2 * NSLOT].rearrange("p (k s) -> p k s", k=2)
            free(activation(slT[:], src, ACT.Copy), k)

            act.wait_ge(sem["w0_loaded"], W0_LOADS)
            for p in range(6):
                k = at.bank(TBANKS)
                free(activation(RT[:, p, :], full(k)[:, 0:NREL], ACT.Copy), k)
            with at.loop(act, NG) as g:
                turned(XT)
                for p in range(6):
                    k = at.bank(XBANKS)
                    src = full(k)[:, 0:TG]
                    activation(QT[:, p, :], src, ACT.Identity, bias=rw0[:, p:p + 1])
                    free(activation(QR[:, p, :], src, ACT.Identity, bias=rr0[:, p:p + 1]), k)
                for p in range(6):
                    k = at.bank(XBANKS)
                    free(activation(KT[:, p, :], full(k)[:, 0:TG], ACT.Identity, bias=bk0[:, p:p + 1]), k)

                def pos_rows():
                    act.wait_ge(sem["pr_stored"], at.now("pr_ready") * 16 + 16)
                    for h0, h1 in POS_PAIRS:
                        k = at.bank(XBANKS)
                        src = full(k)[0:T, 0:2 * NREL].rearrange("p (h n) -> p h n", h=2)
                        free(activation(PR[:, h0:h1 + 1:h1 - h0, 0:NREL], src, ACT.Copy), k)
                    mark("pr_ready")

                pos_rows()
                pos_rows()
                attention(16, 0.125, pos_rows)

            with at.loop(act, NG) as g:
                turned(XT)
                exponentials(CW, name="exp_ready")
                exponentials(DP, name="exp_ready")
                k = at.bank(TBANKS)
                src = full(k)[0:NSLOT, 0:TG].rearrange("p (b t) -> p b t", b=GB)
                free(activation(CT[:, bass.ds(g * GB, GB), :], src, ACT.Copy), k)
                k = at.bank(TBANKS)
                src = full(k)[0:T, 0:GB * NSLOT].rearrange("p (b s) -> p b s", b=GB)
                free(activation(DW, src, ACT.Copy), k)
                k = at.bank(XBANKS)
                src = full(k)[0:KD, :].rearrange("p (k b s) -> p k s b", k=2, b=GB)
                activation(YT[:, 0, :, bass.ds(g * GB, GB)], src[:, 0], ACT.Copy)
                free(activation(YT[:, 1, :, bass.ds(g * GB, GB)], src[:, 1], ACT.Copy), k)
                mark("yt_ready")
            with at.loop(act, NSLOT // RING) as j:
                for half in range(2):
                    act.wait_ge(sem["probs_in"], at.take("probs_in"))
                    h = HT[:, half, 0:2 * FT * NB]
                    give(activation(h, h, ACT.Gelu), "probs_ready")
            for b in range(NB):
                k = at.bank(XBANKS)
                free(activation(Y2[b % 2], full(k)[0:NSLOT, 0:D], ACT.Copy), k)

            act.wait_ge(sem["w1_loaded"], 16 * W1_LOADS)
            act.wait_ge(sem["padded"], 1)
            with at.loop(act, NG) as g:
                turned(XT, g1[:, 0, :], b1[:, 0, :])
                for c in range(CT3):
                    k = at.bank(TBANKS)
                    free(activation(HT[:, 3 + c, :], full(k)[:, 0:TG], ACT.Silu), k)
                    act.wait_ge(sem["conv_ready"], at.take("conv_ready"))
                    give(activation(HT[:, c, :], HT[:, c, :], ACT.Silu), "gate_ready")
                turned(XT, g1[:, 1, :], b1[:, 1, :])
                for dst in range(6):
                    k = at.bank(XBANKS)
                    free(activation((QT, KT)[dst // 3][:, dst % 3, :], full(k)[:, 0:TG], ACT.Identity,
                                    bias=bqk1[:, dst:dst + 1]), k)
                attention(16, 0.25)
                turned(XT, g1[:, 2, :], b1[:, 2, :])
                hidden(FT, ACT.Gelu, lambda m: bf1[:, m:m + 1])

            def router_inputs():
                with at.loop(act, NG) as g:
                    turned(XT)
                    mark("xt_ready")

            router_inputs()
            exponentials(E1[0], name="exp_ready")
            for e in range(NE):
                with at.loop(act, NG) as g:
                    hidden(I1 // 128, ACT.Silu, None)

            act.wait_ge(sem["w2_loaded"], 16 * W2_LOADS)
            with at.loop(act, NG) as g:
                turned(XT)
                for buf in (QT, KT):
                    for p in range(6):
                        k = at.bank(XBANKS)
                        free(activation(buf[:, p, :], full(k)[:, 0:TG], ACT.Copy), k)
                attention(64, 0.125)

            with at.loop(act, NG) as g:
                turned(XT)
                hidden(FT, ACT.Gelu, lambda m: bi2[:, m:m + 1])
                turned(XT)
                for dst in range(4):
                    k = at.bank(XBANKS)
                    free(activation((QT, KT)[dst // 2][0:KD, dst % 2, :], full(k)[0:KD, 0:TG], ACT.Identity,
                                    bias=bqk3[:, dst:dst + 1]), k)

            router_inputs()
            exponentials(E1[0], name="exp_ready")
            for first in range(0, NB, 4):
                k = at.bank(TBANKS)
                src = full(k)[0:NE, 0:TG].rearrange("p (b t) -> p b t", b=4)
                free(activation(WT8[:, first:first + 4, :], src, ACT.Copy), k)
            for e in range(NE):
                with at.loop(act, NG) as g:
                    hidden(FT, ACT.Gelu, lambda m: bb1[:, e, m:m + 1])

        @block.tensor
        def _(pe):
            at = Count("pe", notes)

            def claim(banks):
                k = at.bank(banks)
                pe.wait_ge(sem[f"bank_free{k}"], at.now(f"bank_full{k}") + 1)
                return k, psum[k]

            def filled(ins, k):
                ins.then_inc(sem[f"bank_full{k}"], at.one(f"bank_full{k}"))
                return k, at.now(f"bank_full{k}")

            def moved(*fillings):
                for k, n in fillings:
                    pe.wait_ge(sem[f"bank_free{k}"], n + 1)

            def product(dst, pieces):
                for n, (lhsT, rhs) in enumerate(pieces):
                    last = pe.matmul(dst, lhsT, rhs, start=n == 0, stop=n == len(pieces) - 1)
                return last

            def turn_group(src):
                out = []
                for part in range(2):
                    k, p = claim(XBANKS)
                    for bb in range(GB):
                        last = pe.transpose(p[0:KD, cols(bb)], src[:, bb, part * KD:(part + 1) * KD],
                                            ident[0:T, 0:T])
                    out.append(filled(last, k))
                return out

            def xt():
                pe.wait_ge(sem["xn_ready"], at.take("xn_ready"))
                moved(*turn_group(XN))

            def two(w, n0, n1, x=XT):
                return [(w[:, part, n0:n1], x[:, part, :]) for part in range(2)]

            def token_rows(x, bb, w, n0=0, n1=D):
                return [(x[:, part, cols(bb)], w[:, part, n0:n1]) for part in range(w.shape[1])]

            def pairs(pieces):
                out = []
                for first in range(0, GB, 2):
                    k, p = claim(OBANKS)
                    for bb in (first, first + 1):
                        last = product(p[0:T, (bb - first) * D:(bb - first + 1) * D], pieces(bb))
                    out.append(filled(last, k))
                return out

            def mlp(tiles, w1, x, w2, w1_used=None):
                tokens = []
                for m in range(tiles):
                    k, p = claim(FBANKS)
                    last = product(p[:, 0:TG], [(w1[:, part, m * 128:(m + 1) * 128], x(part)) for part in range(2)])
                    tokens.append(filled(last, k))
                for first in range(0, GB, 2):
                    k, p = claim(OBANKS)
                    for bb in (first, first + 1):
                        for m in range(tiles):
                            if bb == 0:
                                moved(tokens[m])
                            last = pe.matmul(p[0:T, (bb - first) * D:(bb - first + 1) * D], HT[:, m, cols(bb)],
                                             w2[:, m, 0:D], start=m == 0, stop=m == tiles - 1)
                            if bb == 0 and m == 0 and w1_used:
                                last.then_inc(sem[w1_used], at.one(w1_used))
                    filled(last, k)

            def attention(dk, per_tile, dv, wo, pos=None):
                v5 = V[:, 0:GB * HEADS * (dv + 1)].rearrange("p (h d) -> p h d", d=dv + 1)
                pt_moved, on_moved, ot_moved = {}, {}, {}
                for s in range(STEPS):
                    if s < UNITS:
                        bb, unit = s // UPB, s % UPB
                        k = at.bank(SBANKS)
                        if s < 2:
                            pe.wait_ge(sem[f"bank_free{k}"], at.now(f"bank_full{k}") + 1)
                        for j in range(HPU):
                            h = HPU * unit + j
                            last = pe.matmul(psum[k][0:T, cols(j)], head(QT, h, per_tile, dk, cols(bb)),
                                             head(KT, h, per_tile, dk, cols(bb)), start=True, stop=True)
                        last.then_inc(sem["scores_ready"], at.one("scores_ready"))
                    if 0 <= s - 1 < UNITS:
                        pe.wait_ge(sem["probs_ready"], at.take("probs_ready"))
                        k, p = claim(TBANKS)
                        for j in range(HPU):
                            last = pe.transpose(p[0:T, cols(j)], PB[(s - 1) % 2][:, j, :], ident[0:T, 0:T])
                        pt_moved[s - 1] = filled(last, k)
                    if 0 <= s - 2 < UNITS:
                        bb, unit = (s - 2) // UPB, (s - 2) % UPB
                        moved(pt_moved[s - 2])
                        k, p = claim(OBANKS)
                        for j in range(HPU):
                            last = pe.matmul(p[0:T, j * (dv + 1):(j + 1) * (dv + 1)], PT[s % 2][:, j, :],
                                             v5[:, bb * HEADS + HPU * unit + j, :], start=True, stop=True)
                        on_moved[bb] = filled(last, k)
                    bb = last_of(s - 3)
                    if bb is not None:
                        moved(on_moved[bb])
                        rows, tiles = (KD, 2) if dv == 16 else (128, 3)
                        for first in range(0, HEADS * dv // rows, tiles):
                            k, p = claim(XBANKS)
                            for j in range(tiles):
                                c = (first + j) * rows
                                last = pe.transpose(p[0:rows, cols(j)], ON[bb % 2][:, c:c + rows], ident[0:T, 0:T])
                            ot_moved[bb] = filled(last, k)
                            ot_moved[bb, first] = ot_moved[bb]
                    if pos and s in (UPB, 2 * UPB):
                        pos(2 if s == UPB else 3)
                    bb = last_of(s - 4)
                    if bb is not None:
                        rows = KD if dv == 16 else 128
                        moved(*[f for key, f in ot_moved.items() if isinstance(key, tuple) and key[0] == bb])
                        k, p = claim(OBANKS)
                        filled(product(p[0:T, 0:D], [(OT[bb % 2][0:rows, n, :], wo[0:rows, n, :])
                                                     for n in range(HEADS * dv // rows)]), k)

            pe.wait_ge(sem["constants_ready"], 1)
            pe.wait_ge(sem["xn_ready"], at.take("xn_ready"))
            k, p = claim(XBANKS)
            for part in range(2):
                last = pe.transpose(p[0:KD, part * NSLOT:(part + 1) * NSLOT], SL2[:, part * KD:(part + 1) * KD],
                                    ident[0:NSLOT, 0:NSLOT])
            filled(last, k)

            pe.wait_ge(sem["patches_loaded"], 64)
            for first in range(0, NB, 2):
                k, p = claim(OBANKS)
                for j in range(2):
                    last = product(p[0:NPATCH, j * D:(j + 1) * D],
                                   [(patchT[:, n, first + j, :], convT[:, n, :]) for n in range(KP // 128)])
                f = filled(last, k)
            moved(f)

            pe.wait_ge(sem["w0_loaded"], W0_LOADS)
            r_moved = []
            for p6 in range(6):
                k, p = claim(TBANKS)
                r_moved.append(filled(product(p[:, 0:NREL], [(rker[:, part, p6 * 128:(p6 + 1) * 128],
                                                              posT[:, part, :]) for part in range(2)]), k))
            moved(*r_moved[-2:])
            with at.loop(pe, NG) as g:
                xt()
                qk = []
                for w in (wq0, wk0):
                    for p6 in range(6):
                        k, p = claim(XBANKS)
                        part, c = p6 // 3, (p6 % 3) * 128
                        qk.append(filled(pe.matmul(p[:, 0:TG], w[:, part, c:c + 128], XT[:, part, :],
                                                   start=True, stop=True), k))
                v_moved = []
                for first in range(0, GB, 2):
                    k, p = claim(OBANKS)
                    for bb in (first, first + 1):
                        for part in range(2):
                            c = (bb - first) * D + part * KD
                            last = pe.matmul(p[0:T, c:c + KD], XT[:, part, cols(bb)], wv0[:, part, :],
                                             start=True, stop=True)
                    v_moved.append(filled(last, k))
                moved(*qk[-2:], *v_moved)

                def pos(bb):
                    for pair in POS_PAIRS:
                        k, p = claim(XBANKS)
                        for j, h in enumerate(pair):
                            last = pe.matmul(p[0:T, j * NREL:(j + 1) * NREL], head(QR, h, 2, 64, cols(bb)),
                                             head(RT, h, 2, 64, slice(0, NREL)), start=True, stop=True)
                        filled(last, k)

                pos(0)
                pos(1)
                attention(64, 2, 16, wo0, pos)

            with at.loop(pe, NG) as g:
                xt()
                k, p = claim(OBANKS)
                for bb in range(GB):
                    last = product(p[0:T, bb * NSLOT:(bb + 1) * NSLOT], token_rows(XT, bb, slT, 0, NSLOT))
                filled(last, k)
                pe.wait_ge(sem["slot_in"], at.take("slot_in"))
                k = at.bank(SBANKS)
                pe.wait_ge(sem[f"bank_free{k}"], at.now(f"bank_full{k}") + 1)
                pe.sem_inc(sem["tensor_passed"], 1)
                for bb in range(GB):
                    last = pe.transpose(psum[k][0:NSLOT, cols(bb)], LG4[:, bb, :], ident[0:T, 0:T])
                last.then_inc(sem["scores_ready"], at.one("scores_ready"))
                pe.wait_ge(sem["slot_in"], at.take("slot_in"))
                k, p = claim(TBANKS)
                pe.sem_inc(sem["tensor_passed"], 1)
                for bb in range(GB):
                    last = pe.transpose(p[0:NSLOT, cols(bb)], CW[:, bb, :], ident[0:T, 0:T])
                filled(last, k)
                pe.wait_ge(sem["slot_in"], at.take("slot_in"))
                k, p = claim(TBANKS)
                pe.sem_inc(sem["tensor_passed"], 1)
                for bb in range(GB):
                    last = pe.transpose(p[0:T, bb * NSLOT:(bb + 1) * NSLOT], DP[:, bb, :], ident[0:NSLOT, 0:NSLOT])
                moved(filled(last, k))
                k, p = claim(XBANKS)
                for part in range(2):
                    for bb in range(GB):
                        c = (part * GB + bb) * NSLOT
                        last = pe.matmul(p[0:KD, c:c + NSLOT], XN[:, bb, part * KD:(part + 1) * KD], DW[:, bb, :],
                                         start=True, stop=True)
                y_moved = filled(last, k)
            last_bank = y_moved[0]
            pe.wait_ge(sem[f"bank_free{last_bank}"], at.now(f"bank_full{last_bank}") + 1)

            with at.loop(pe, NSLOT // RING) as j:
                for half in range(2):
                    k = at.bank(SBANKS)
                    for n in range(2):
                        r = 2 * half + n
                        pe.wait_ge(sem[f"w1_loaded{r}"], at.take(f"w1_loaded{r}", 16))
                        for m in range(FT):
                            c = (n * FT + m) * NB
                            last = product(psum[k][:, c:c + NB],
                                           [(W1[r][:, part, m * 128:(m + 1) * 128],
                                             YT[:, part, bass.ds(j * RING + r, 1), :].rearrange("p o b -> p (o b)"))
                                            for part in range(2)])
                    last.then_inc(sem["scores_ready"], at.one("scores_ready"))
                for half in range(2):
                    k, p = claim(OBANKS)
                    pe.wait_ge(sem["probs_ready"], at.take("probs_ready"))
                    for n in range(2):
                        r = 2 * half + n
                        pe.wait_ge(sem[f"w2_loaded{r}"], at.take(f"w2_loaded{r}", 16))
                        for m in range(2):
                            for f in range(FT):
                                c = (n * FT + f) * NB
                                last = pe.matmul(p[0:KD, (n * 2 + m) * NB:(n * 2 + m + 1) * NB],
                                                 W2[r][:, f, m * KD:(m + 1) * KD], HT[:, half, c:c + NB],
                                                 start=f == 0, stop=f == FT - 1)
                                if m == 0 and f == 0:
                                    last.then_inc(sem[f"w1_used{r}"], at.one(f"w1_used{r}"))
                    o_moved = filled(last, k)
            pe.wait_ge(sem[f"bank_free{o_moved[0]}"], at.now(f"bank_full{o_moved[0]}") + 1)

            y2 = {}
            for s in range(NB + 1):
                if s < NB:
                    k, p = claim(XBANKS)
                    for part in range(2):
                        last = pe.transpose(p[0:NSLOT, part * KD:(part + 1) * KD], Y2T[:, part, :, s],
                                            ident[0:KD, 0:KD])
                    y2[s] = filled(last, k)
                if s >= 1:
                    b = s - 1
                    moved(y2[b])
                    if b % 2 == 0:
                        k, p = claim(OBANKS)
                        kk = k
                    last = pe.matmul(psum[kk][0:T, (b % 2) * D:(b % 2 + 1) * D], CT[:, b, :], Y2[b % 2],
                                     start=True, stop=True)
                    if b % 2:
                        filled(last, kk)

            pe.wait_ge(sem["w1_loaded"], 16 * W1_LOADS)
            pe.wait_ge(sem["padded"], 1)
            with at.loop(pe, NG) as g:
                xt()
                for c in range(CT3):
                    k, p = claim(SBANKS)
                    filled(product(p[:, 0:TG], two(win1, c * 128, (c + 1) * 128)), k)
                    k, p = claim(TBANKS)
                    filled(product(p[:, 0:TG], two(win1, INNER + c * 128, INNER + (c + 1) * 128)), k)
                pe.wait_ge(sem["gated"], at.take("gated", CT3))
                pairs(lambda bb: token_rows(QT[:, 0:CT3, :], bb, wout1))
                xt()
                qk = []
                for dst in range(6):
                    k, p = claim(XBANKS)
                    qk.append(filled(product(p[:, 0:TG], two(wqk1, dst * 128, (dst + 1) * 128)), k))
                v_moved = pairs(lambda bb: token_rows(XT, bb, wqkv1, 2 * D, 3 * D))
                moved(*qk[-2:], *v_moved)
                attention(16, 4, 16, wp1)
                xt()
                mlp(FT, wf1, lambda part: XT[:, part, :], wf2)

            def router_inputs(w):
                with at.loop(pe, NG) as g:
                    xt()
                    k, p = claim(OBANKS)
                    for bb in range(GB):
                        last = product(p[0:T, bb * NE:(bb + 1) * NE], token_rows(XT, bb, w, 0, NE))
                    filled(last, k)
                    at.take("xt_copied")
                pe.wait_ge(sem["xt_copied"], at.now("xt_copied"))

            def experts(tiles):
                for e in range(NE):
                    r = e % RING
                    pe.wait_ge(sem[f"w1_loaded{r}"], at.take(f"w1_loaded{r}", 16))
                    pe.wait_ge(sem[f"w2_loaded{r}"], at.take(f"w2_loaded{r}", 16))
                    with at.loop(pe, NG) as g:
                        mlp(tiles, W1[r], lambda part: XALL[:, part, bass.ds(g * TG, TG)], W2[r], f"w1_used{r}")

            router_inputs(rt1)
            pe.wait_ge(sem["router_ready"], at.take("router_ready"))
            k, p = claim(OBANKS)
            filled(pe.matmul(p[0:T, 0:NB * NE], ones[0:T, 0:T], E1[0].rearrange("p b e -> p (b e)"),
                             start=True, stop=True), k)
            experts(I1 // 128)

            pe.wait_ge(sem["w2_loaded"], 16 * W2_LOADS)
            with at.loop(pe, NG) as g:
                xt()
                qk = []
                for w in (wq2, wk2):
                    for p6 in range(6):
                        k, p = claim(XBANKS)
                        qk.append(filled(product(p[:, 0:TG], two(w, p6 * 128, (p6 + 1) * 128)), k))
                v_moved = []
                for bb in range(GB):
                    for c in range(0, FF, 2 * D):
                        k, p = claim(OBANKS)
                        v_moved.append(filled(product(p[0:T, 0:2 * D], token_rows(XT, bb, wv2, c, c + 2 * D)), k))
                moved(*qk[-2:], *v_moved[-2:])
                attention(64, 2, 64, wo2)

            with at.loop(pe, NG) as g:
                xt()
                mlp(FT, wi2, lambda part: XT[:, part, :], wu2)
                xt()
                qk = []
                for dst in range(4):
                    k, p = claim(XBANKS)
                    qk.append(filled(product(p[0:KD, 0:TG], two(wqkv3, dst * KD, (dst + 1) * KD)), k))
                v_moved = pairs(lambda bb: token_rows(XT, bb, wqkv3, 2 * D, 3 * D))
                moved(*qk[-2:])
                k, p = claim(SBANKS)
                for bb in range(GB):
                    last = product(p[0:T, cols(bb)], [(KT[0:KD, part, cols(bb)], QT[0:KD, part, cols(bb)])
                                                      for part in range(2)])
                moved(*v_moved, filled(last, k))
                pairs(lambda bb: [(PT[0][:, bb, :], V[:, bb * D:(bb + 1) * D])])

            router_inputs(rt3)
            pe.wait_ge(sem["router_ready"], at.take("router_ready"))
            w_moved = []
            for first in range(0, NB, 4):
                k, p = claim(TBANKS)
                for j in range(4):
                    last = pe.transpose(p[0:NE, cols(j)], E1[1][:, first + j, :], ident[0:T, 0:T])
                w_moved.append(filled(last, k))
            moved(*w_moved[-2:])
            for first in range(0, NB, 2):
                k, p = claim(OBANKS)
                for j in range(2):
                    last = pe.matmul(p[0:T, j * D:(j + 1) * D], WT8[:, first + j, :], bb2, start=True, stop=True)
                filled(last, k)
            experts(FT)


def laid_out(i):
    a = {k: np.asarray(v) for k, v in i.items()}
    rows = lambda v, n=T: np.ascontiguousarray(np.broadcast_to(v, (n,) + v.shape))
    per128 = lambda v: v.reshape(-1, 128).T
    side = 32
    n5 = 5
    frac = np.arange(0.0, 1.0 - 1e-06, 1.0 / n5, dtype=np.float32)
    bins = np.searchsorted(np.arange(1.0 / side, 1.0, 1.0 / side, dtype=np.float32), frac, side="right")
    pos_ids = (bins[:, None] * side + bins).reshape(-1)
    x = a["x"][:, :, :80, :80].reshape(NB, 3, n5, 16, n5, 16)
    patches = x.transpose(1, 3, 5, 0, 2, 4).reshape(KP // 128, 128, NB, NPATCH).transpose(1, 0, 2, 3)
    ids = np.zeros((T, NB), np.int32)
    ids[NPATCH:] = a["x_txt"].T
    qkv_b = a["L1_attn_qkv_b"]
    far = np.arange(T)[None, :] - np.arange(T)[:, None]
    decay = np.where(far >= 0, np.float32(0.99) ** far.astype(np.float32), np.float32(0)).astype(np.float32)
    tiled = lambda v: v.reshape(-1, 2, 2, HPU, 64).transpose(0, 1, 3, 2, 4).reshape(v.shape)
    t = {
        "patchT": patches,
        "convT": a["L0_tok_conv_w"].reshape(D, KP).T.reshape(KP // 128, 128, D).transpose(1, 0, 2),
        "pos_rows": a["L0_tok_pos_table"][pos_ids], "conv_b": rows(a["L0_tok_conv_b"], NPATCH),
        "ids": ids, "words": a["L0_txt_token_embeddings"],
        "Wq": a["L0_attn_Wq"], "Wk": a["L0_attn_Wk"], "Wv": a["L0_attn_Wv"],
        "r_kernel": tiled(a["L0_attn_r_kernel"].reshape(D, FF)),
        "posT": a["L0_attn_position_embeds"][1:1 + NREL].T, "Wo": a["L0_attn_Wo"],
        "r_w_bias": per128(tiled(a["L0_attn_r_w_bias"].reshape(1, -1))), "r_r_bias": per128(tiled(a["L0_attn_r_r_bias"].reshape(1, -1))),
        "bk": per128(tiled(a["L0_attn_bk"][None])), "bv": rows(a["L0_attn_bv"]), "bo": rows(a["L0_attn_bo"]),
        "gamma": rows(a["L0_attn_gamma"]), "beta": rows(a["L0_attn_beta"]),
        "slots": a["L0_ffn_slots"], "slot_scale": a["L0_ffn_scale"][:, None],
        "norm_weight": rows(a["L0_ffn_norm_weight"]),
        "fc1_bias": a["L0_ffn_fc1_bias"].reshape(NSLOT, FT, 128).transpose(2, 0, 1),
        "fc2_bias": a["L0_ffn_fc2_bias"].reshape(NSLOT, 2, KD).transpose(2, 1, 0),
        "fc1": a["L0_ffn_fc1_weight"], "fc2": a["L0_ffn_fc2_weight"],
        "in_proj": a["L1_attn_in_proj_w"], "out_proj": a["L1_attn_out_proj_w"], "qkv1": a["L1_attn_qkv_w"],
        "proj1": a["L1_attn_attn_proj_w"], "ffn1": a["L1_attn_ffn1_w"], "ffn2": a["L1_attn_ffn2_w"],
        "conv1_w": a["L1_attn_conv_w"].reshape(CT3, 128, KCONV).transpose(1, 0, 2),
        "conv1_b": per128(a["L1_attn_conv_b"]),
        "ln_g": np.stack([a[f"L1_attn_ln{n}_g"].reshape(2, KD) for n in (1, 2, 3)]).transpose(2, 0, 1),
        "ln_b": np.stack([a[f"L1_attn_ln{n}_b"].reshape(2, KD) for n in (1, 2, 3)]).transpose(2, 0, 1),
        "qk1_b": qkv_b[:2 * D].reshape(2, UPB, HPU, 16).transpose(0, 1, 3, 2),
        "v1_b": rows(qkv_b[2 * D:]), "proj1_b": rows(a["L1_attn_attn_proj_b"]),
        "ffn1_b": per128(a["L1_attn_ffn1_b"]), "ffn2_b": rows(a["L1_attn_ffn2_b"]),
        "router1": a["L1_ffn_router_w"].T.reshape(2, KD, NE).transpose(1, 0, 2),
        "m1w1": a["L1_ffn_w1"].transpose(0, 2, 1), "m1w2": a["L1_ffn_w2"].transpose(0, 2, 1),
        "q2": tiled(a["L2_attn_w_q"]), "k2": tiled(a["L2_attn_w_k"]), "v2": a["L2_attn_w_v"], "o2": a["L2_attn_w_o"],
        "o2_b": rows(a["L2_attn_b_o"]), "in2": a["L2_ffn_in_weight"].T, "in2_b": per128(a["L2_ffn_in_bias"]),
        "up2": a["L2_ffn_out_weight"],
        "qkv3": a["L3_attn_W_qkv"], "qk3_b": a["L3_attn_b_qkv"][:2 * D].reshape(4, KD).T,
        "v3_b": rows(a["L3_attn_b_qkv"][2 * D:]), "decay": decay,
        "router3": a["L3_ffn_router_w"].T, "m3w1": a["L3_ffn_w1"], "m3w2": a["L3_ffn_w2"],
        "m3b1": a["L3_ffn_b1"].reshape(NE, FT, 128).transpose(2, 0, 1), "m3b2": a["L3_ffn_b2"],
    }
    return {k: np.ascontiguousarray(v) for k, v in t.items()}


def program(nc, shapes, notes):
    t = {name: nc.dram_tensor(f"in_{name}", shape, dt, kind="ExternalInput").ap()
         for name, (shape, dt) in shapes.items()}
    out = nc.dram_tensor("out_h", (T, NB, D), F32, kind="ExternalOutput").ap()
    row = HEADS * NREL
    scratch = nc.dram_tensor("pos_scratch", (NB, T, row), F32, kind="Internal").ap()
    flat = scratch.rearrange("b t n -> (b t n)")
    build(nc, t, out, scratch, flat, notes)


def kernel(**inputs):
    import concourse.bacc as _bacc
    from concourse.bass_utils import run_bass_kernel_spmd as _run

    t = laid_out(inputs)
    shapes = {k: (v.shape, mybir.dt.from_np(v.dtype)) for k, v in t.items()}
    notes = {}
    program(_bacc.Bacc("TRN2", target_bir_lowering=False, num_devices=1), shapes, notes)
    nc = _bacc.Bacc("TRN2", target_bir_lowering=False, num_devices=1)
    program(nc, shapes, notes)
    r = _run(nc, [{f"in_{k}": v for k, v in t.items()}], core_ids=[0])
    return np.ascontiguousarray(r.results[0]["out_h"].transpose(1, 0, 2))
```

```python
from contextlib import ExitStack, contextmanager

import numpy as np

import concourse.bass as bass
from concourse import mybir

F32 = mybir.dt.float32
F32R = mybir.dt.float32r
I32 = mybir.dt.int32
ACT = mybir.ActivationFunctionType
ALU = mybir.AluOpType
AX = mybir.AxisListType

NB = 16
T = 102
NPATCH = 25
D = 192
KD = 96
GB = 4
NG = NB // GB
TG = GB * T
HEADS = 12
HPU = 3
UPB = HEADS // HPU
TU = HPU * T
FF = 768
FT = FF // 128
NSLOT = 64
NE = 8
I1 = 512
INNER = 384
CT3 = INNER // 128
KCONV = 4
RING = 4
NREL = 2 * T - 1
VOCAB = 50257
KP = 768
EPS = 1e-5

POS_PAIRS = ((0, 1), (3, 4), (2, 6), (5, 9), (7, 8), (10, 11))

MARKS = tuple(range(8))

W0_LOADS = 16 * (12 + 3 + 7)
W1_LOADS = 6 + 8 + 8
W2_LOADS = 8 + 7

SBANKS, TBANKS, OBANKS, XBANKS, FBANKS = (0, 1), (2, 3), (4, 5), (6, 7), (2, 3, 6, 7)


class Count:

    def __init__(self, who, notes):
        self.who, self.notes = who, notes
        self.total, self.turn, self.per = {}, {}, {}
        self.i = None
        self.loops = 0
        self.turns_of_banks = {}

    def now(self, name):
        n = self.total.get(name, 0) + self.turn.get(name, 0)
        per = self.per.get(name, 0)
        return n + self.i * per if self.i is not None and per else n

    def one(self, name, by=1):
        self.turn[name] = self.turn.get(name, 0) + by
        return by

    def take(self, name, by=1):
        self.one(name, by)
        return self.now(name)

    def bank(self, banks):
        n = self.turns_of_banks.get(banks, 0)
        self.turns_of_banks[banks] = n + 1
        return banks[n % len(banks)]

    def first_banks(self):
        self.turns_of_banks = {}

    def _settle(self, times):
        for name, n in self.turn.items():
            self.total[name] = self.total.get(name, 0) + n * times
        self.turn, self.per, self.turns_of_banks = {}, {}, {}
        self.i = None

    @contextmanager
    def loop(self, engine, times):
        self._settle(1)
        key = (self.who, self.loops)
        self.loops += 1
        self.per = dict(self.notes.get(key, {}))
        with engine.Fori(0, times) as i:
            self.i = i
            yield i
            self.notes[key] = dict(self.turn)
        self._settle(times)


def build(nc, t, out, scratch, flat, notes):
    ctx = ExitStack()
    with ctx:
        def sb(name, shape, dt=F32):
            return ctx.enter_context(nc.sbuf_tensor(name, shape, dt))

        sem = {}

        def signal(*names):
            for name in names:
                sem[name] = ctx.enter_context(nc.semaphore(name))

        shapes = {"KT": [128, 6, TG],
                  "V": [T, GB * HEADS * 65],
                  "HT": [128, FT, TG],
                  **{f"W1_{r}": [KD + 1, 2, FF] for r in range(RING)},
                  **{f"W2_{r}": [128, FT, D] for r in range(RING)},
                  "SLOTS": [128, 2 * 2 * NSLOT * NB + NB * T],
                  "AREA": [128, 13620]}
        with ExitStack() as first:
            whole = {name: first.enter_context(nc.sbuf_tensor(name, shape, F32)) for name, shape in shapes.items()}
        rounded = {name: sb(f"{name}_R", shape, F32R) for name, shape in shapes.items()}
        KT, V, HT, SLOTS, AREA = (whole[n] for n in ("KT", "V", "HT", "SLOTS", "AREA"))
        W1B, W2 = ([whole[f"W{n}_{r}"] for r in range(RING)] for n in (1, 2))
        H = sb("H", [T, NB, D])
        XN = sb("XN", [T, GB, D])
        X1 = sb("X1", [T, GB, D])
        XT = sb("XT", [KD, 2, TG])
        QT = sb("QT", [128, 6, TG])
        PB = [sb(f"PB{j}", [T, 4, T]) for j in range(2)]
        PT = [sb(f"PT{j}", [T, 4, T]) for j in range(2)]
        ON = [sb(f"ON{j}", [T, FF]) for j in range(2)]
        OT = [sb(f"OT{j}", [128, 6, T]) for j in range(2)]
        W1 = [w[0:KD] for w in W1B]
        YT = SLOTS[0:KD, 0:2048].rearrange("p (k s b) -> p k s b", k=2, s=NSLOT)
        Y2T = SLOTS[0:KD, 2048:4096].rearrange("p (k s b) -> p k s b", k=2, s=NSLOT)
        XA = SLOTS[0:T, 0:NB * D].rearrange("p (b d) -> p b d", b=NB)
        CT = SLOTS[0:NSLOT, 4096:4096 + NB * T].rearrange("p (b t) -> p b t", b=NB)
        per_slot = lambda buf: buf[:].rearrange("p h t -> p (h t)")[:, 0:GB * NSLOT].rearrange(
            "p (b s) -> p b s", b=GB)
        LG4, CW, DW = per_slot(PT[0]), per_slot(PB[1]), per_slot(PT[1])
        DP = PB[0][0:NSLOT, :, :]
        Y2 = [ON[j][0:NSLOT, 0:D] for j in range(2)]
        flat_of = lambda buf, parts, c0, c1: buf[0:parts].rearrange("p k t -> p (k t)")[:, c0:c1]
        XS = flat_of(KT, KD + 1, 0, 2 * 128).rearrange("p (k s b) -> p k s b", k=2, s=RING)
        HR = flat_of(QT, 128, 0, FF)
        YR = flat_of(QT, 128, FF, FF + D)
        HS = HT[:, :, 0:128]
        def twice(name, view):
            return view(whole[name]), view(rounded[name])

        by_k = lambda ap: ap.rearrange("p (k t) -> p k t", k=2)
        XALL_H, XALL_HR = twice("SLOTS", lambda b: by_k(b[0:KD, 0:2 * NB * T]))
        XALL_LR = by_k(rounded["AREA"][0:KD, 0:2 * NB * T])
        HT_H, HT_HR = twice("KT", lambda b: b)
        HT_LR = rounded["HT"]
        W1_H, W1_HR = zip(*[twice("V", lambda b: by_k(b[0:KD, j * 2 * FF:(j + 1) * 2 * FF])) for j in range(2)])
        W1_LR = [rounded[f"W1_{r}"][0:KD] for r in range(RING)]
        after = 2 * NB * T
        W2_H, W2_HR = zip(*[twice("SLOTS", lambda b: b[:, after + j * FT * D:after + (j + 1) * FT * D].rearrange(
            "p (f d) -> p f d", f=FT)) for j in range(2)])
        W2_LR = [rounded[f"W2_{r}"] for r in range(RING)]
        SL, SL2 = ON[0][0:NSLOT, D:2 * D], ON[1][0:NSLOT, D:2 * D]
        ident = sb("ident", [128, 128])
        ones = sb("ones", [128, 128])
        marked = sb("marked", [1, 8])
        amarked = sb("amarked", [1, 8])
        expo = sb("expo", [128, 2, GB])
        ST = sb("ST", [T, GB, 6])
        MV = sb("MV", [T, GB, 2])
        VE = sb("VE", [T, GB])
        RS = sb("RS", [T, GB])
        MX = sb("MX", [T, GB])
        SM = sb("SM", [T, GB])
        RC = sb("RC", [T, GB])
        TS = sb("TS", [T, GB])
        IDS = sb("IDS", [T, NB], I32)
        LG = sb("LG", [T, NB, NE])
        E1 = [QT[0:T, j, 0:NB * NE].rearrange("p (b e) -> p b e", b=NB) for j in range(6)]
        E2 = [sb(f"E2_{j}", [T, NB]) for j in range(3)]
        RUN = sb("RUN", [T, NE])
        ORDER = sb("ORDER", [T, NB, NE])
        WT8 = KT[0:NE, 0:4, :].rearrange("p k (b t) -> p (k b) t", b=4)


        def area():
            at = [0]

            def piece(parts, *shape):
                n = int(np.prod(shape))
                ap = AREA[0:parts, at[0]:at[0] + n]
                at[0] += n
                assert at[0] <= 13620
                if len(shape) == 2:
                    ap = ap.rearrange("p (a b) -> p a b", a=shape[0])
                elif len(shape) == 3:
                    ap = ap.rearrange("p (a b c) -> p a b c", a=shape[0], b=shape[1])
                return ap
            return piece

        a0 = area()
        wq0, wk0, wv0 = a0(KD, 2, 384), a0(KD, 2, 384), a0(KD, 2, KD)
        rker, posT, RT = a0(KD, 2, FF), a0(KD, 2, NREL), a0(128, 6, NREL)
        wo0 = a0(KD, 2, D)
        rw0, rr0, bk0 = a0(128, 6), a0(128, 6), a0(128, 6)
        bv0, bo0, gamma0, beta0 = a0(T, D), a0(T, D), a0(T, D), a0(T, D)
        QR = a0(128, 6, TG)
        PR = a0(T, HEADS, NREL)
        POS = [a0(T, HEADS, T) for _ in range(2)]
        patchT = HT[:, :, 0:NB * NPATCH].rearrange("p k (b n) -> p k b n", b=NB)
        convT = KT[:, :, 0:D]
        posE = ON[0][0:NPATCH, 2 * D:4 * D].rearrange("p (a d) -> p a d", a=2)
        slS = sb("slS", [NSLOT, 1])
        slT = sb("slT", [KD, 2, NSLOT])
        nw0 = sb("nw0", [T, D])
        fb2 = sb("fb2", [KD, 2, NSLOT])

        a1 = area()
        XALL = a1(KD, 2, NB * T)
        win1, wout1 = a1(KD, 2, 2 * INNER), a1(128, CT3, D)
        cw1, cb1 = a1(128, CT3, KCONV), a1(128, CT3)
        g1 = a1(KD, 3, 2)
        b1 = a1(KD, 3, 2)
        wqkv1, wqk1 = a1(KD, 2, 3 * D), a1(KD, 2, 2 * 384)
        bqk1, bv1 = a1(128, 6), a1(T, D)
        wp1, bp1 = a1(KD, 2, D), a1(T, D)
        wf1, bf1, wf2, bf2 = a1(KD, 2, FF), a1(128, FT), a1(128, FT, D), a1(T, D)
        rt1 = sb("rt1", [KD, 2, NE])

        a2 = area()
        a2(KD, 2, NB * T)
        wq2, wk2, wv2 = a2(KD, 2, FF), a2(KD, 2, FF), a2(KD, 2, FF)
        wo2, bo2 = a2(128, 6, D), a2(T, D)
        wi2, bi2, wu2 = a2(KD, 2, FF), a2(128, FT), a2(128, FT, D)
        wqkv3, bqk3, bv3 = a2(KD, 2, 3 * D), a2(KD, 4), a2(T, D)
        decay = a2(T, T)
        rt3, bb1, bb2 = a2(KD, 2, NE), a2(128, NE, FT), a2(NE, D)

        psum = [ctx.enter_context(nc.psum_tensor(f"bank{k}", [128, 512], F32)) for k in range(8)]

        for k in range(8):
            signal(f"bank_full{k}", f"bank_free{k}")
        for r in range(RING):
            signal(f"w1_loaded{r}", f"w1_used{r}", f"w2_loaded{r}", f"w2_used{r}")
        signal("patches_loaded", "ids_loaded", "words_loaded", "w0_loaded", "w1_loaded", "w2_loaded",
               "slots_loaded",
               "constants_ready", "area_cleared", "w0_cleared", "padded",
               "vector_step", "pool_step",
               "vector_passed", "tensor_passed",
               "power_in", "power_out",
               "xn_ready", "xn_taken",
               "xt_ready",
               "xt_copied",
               "scores_ready",
               "probs_in", "probs_ready",
               "exp_ready",
               "pr_ready", "pr_stored", "pos_loaded0", "pos_loaded1", "pos_used",
               "conv_ready", "gate_ready", "gated",
               "slot_in", "yt_ready", "slot_rows",
               "w1_split", "w2_split",
               "hidden_ready", "hidden_split",

               "attn0_done", "attn1_done",
               "router_ready", "out_ready", "out_stored")

        block = ctx.enter_context(nc.Block())

        def head(buf, h, per_tile, dk, cols):
            unit, j = h // HPU, h % HPU
            p = (unit % per_tile) * (128 // per_tile)
            return buf[p:p + dk, (unit // per_tile) * HPU + j, cols]

        def cols(bb):
            return slice(bb * T, (bb + 1) * T)

        UNITS = GB * UPB
        STEPS = UNITS + 4

        def last_of(step):
            return step // UPB if 0 <= step < UNITS and step % UPB == UPB - 1 else None

        @block.sync
        def _(sp):
            at = Count("sp", notes)

            def load(dst, src, name):
                sp.dma_start(dst, src).then_inc(sem[name], at.one(name, 16))

            sp.sem_inc(sem["pr_stored"], at.one("pr_stored", 16))
            at.one("pos_used")

            load(patchT, t["patchT"], "patches_loaded")
            load(convT, t["convT"], "patches_loaded")
            load(posE[:, 0, :], t["pos_rows"], "patches_loaded")
            load(posE[:, 1, :], t["conv_b"], "patches_loaded")
            sp.wait_ge(sem["w0_cleared"], 3)
            for g in range(4):
                rows = slice((g % 2) * 48, (g % 2) * 48 + 48)
                for w, name in ((wq0, "Wq"), (wk0, "Wk")):
                    tiles = w[rows, g // 2, :].rearrange("p (j two d) -> p j two d", j=HPU, two=2)
                    load(tiles[:, :, g % 2, :], t[name][g].rearrange("i (j d) -> i j d", j=HPU), "w0_loaded")
                load(wv0[rows, g // 2, (g % 2) * 48:(g % 2) * 48 + 48], t["Wv"][g], "w0_loaded")
            load(rker, t["r_kernel"].rearrange("(k p) n -> p k n", p=KD), "w0_loaded")
            load(posT, t["posT"].rearrange("(k p) n -> p k n", p=KD), "w0_loaded")
            load(wo0, t["Wo"].rearrange("(k p) n -> p k n", p=KD), "w0_loaded")
            for dst, name in ((rw0, "r_w_bias"), (rr0, "r_r_bias"), (bk0, "bk"), (bv0, "bv"), (bo0, "bo"),
                              (gamma0, "gamma"), (beta0, "beta")):
                load(dst, t[name], "w0_loaded")
            for dst, name in ((SL, "slots"), (slS, "slot_scale"), (nw0, "norm_weight"), (fb2, "fc2_bias"), (rt1, "router1")):
                load(dst if name == "slots" else dst[:], t[name], "slots_loaded")

            def fill_w1(r, w1, rounds=1):
                sp.wait_ge(sem[f"w1_used{r}"], at.now(f"w1_used{r}"))
                at.one(f"w1_used{r}", rounds)
                sp.dma_start(W1B[r][0:w1.shape[0], :, 0:w1.shape[2]], w1).then_inc(sem[f"w1_loaded{r}"], 16)

            def fill_w2(r, w2):
                sp.wait_ge(sem[f"w2_used{r}"], at.now(f"w2_used{r}"))
                at.one(f"w2_used{r}")
                sp.dma_start(W2[r][:, 0:w2.shape[1], :], w2).then_inc(sem[f"w2_loaded{r}"], 16)

            def fill(r, w1, w2):
                fill_w1(r, w1, NG)
                fill_w2(r, w2)

            def fill_slots(first):
                for r in range(RING):
                    fill_w1(r, t["fc1"][bass.ds(first + r, 1)].rearrange("o p k f -> (o p) k f"))
                for r in range(RING):
                    fill_w2(r, t["fc2"][bass.ds(first + r, 1)].rearrange("o p k f -> (o p) k f"))

            fill_slots(0)

            with at.loop(sp, NG) as g:
                for bb in range(GB):
                    here = scratch[bass.ds(g * GB + bb, 1)].rearrange("o t n -> (o t) n")
                    sp.wait_ge(sem["pr_ready"], at.take("pr_ready"))
                    sp.dma_start(here, PR.rearrange("p h n -> p (h n)")
                                 ).then_inc(sem["pr_stored"], at.one("pr_stored", 16))
                    sp.wait_ge(sem["pr_stored"], at.now("pr_stored"))
                    if bb < 2:
                        sp.wait_ge(sem["pos_used"], at.now("pos_used"))
                    else:
                        sp.wait_ge(sem["pos_used"], at.take("pos_used"))
                    row = HEADS * NREL
                    shifted = bass.AP(tensor=flat.tensor, offset=(g * GB + bb) * (T * row) + (T - 1),
                                      ap=[[row - 1, T], [NREL, HEADS], [1, T]])
                    sp.dma_start(POS[bb % 2], shifted).then_inc(sem[f"pos_loaded{bb % 2}"], 16)
                for _ in range(2):
                    at.one("pos_used")

            def load_area(pieces, name):
                for dst, src, p in pieces:
                    load(dst, t[src].rearrange("(k p) n -> p k n", p=p) if p else t[src], name)

            sp.wait_ge(sem["attn0_done"], 1)
            sp.wait_ge(sem["area_cleared"], 1)
            load_area(((win1, "in_proj", KD), (wout1, "out_proj", 128), (wqkv1, "qkv1", KD), (wp1, "proj1", KD),
                       (wf1, "ffn1", KD), (wf2, "ffn2", 128), (cw1, "conv1_w", 0), (cb1, "conv1_b", 0),
                       (g1, "ln_g", 0), (b1, "ln_b", 0), (bv1, "v1_b", 0), (bp1, "proj1_b", 0),
                       (bf1, "ffn1_b", 0), (bf2, "ffn2_b", 0)), "w1_loaded")
            for q in range(2):
                for u in range(UPB):
                    load(bqk1[32 * u:32 * u + 16, 3 * q:3 * q + 3], t["qk1_b"][q, u], "w1_loaded")

            with at.loop(sp, NSLOT // RING - 1) as j:
                fill_slots(j * RING + RING)
            for e in range(NE):
                if e == RING:
                    sp.wait_ge(sem["attn1_done"], 1)
                    load_area(((wq2, "q2", KD), (wk2, "k2", KD), (wv2, "v2", KD), (wo2, "o2", 128),
                               (wi2, "in2", KD), (wu2, "up2", 128), (wqkv3, "qkv3", KD), (rt3, "router3", KD),
                               (bo2, "o2_b", 0), (bi2, "in2_b", 0), (bqk3, "qk3_b", 0), (bv3, "v3_b", 0),
                               (decay, "decay", 0), (bb1, "m3b1", 0), (bb2, "m3b2", 0)), "w2_loaded")
                fill(e % RING, t["m1w1"][e], t["m1w2"][e])
            for e in range(NE):
                fill(e % RING, t["m3w1"][e], t["m3w2"][e])

            with at.loop(sp, NG) as g:
                sp.wait_ge(sem["out_ready"], at.take("out_ready"))
                sp.dma_start(out[:, bass.ds(g * GB, GB), :], H[:, bass.ds(g * GB, GB), :]
                             ).then_inc(sem["out_stored"], at.one("out_stored", 16))
            sp.wait_ge(sem["out_stored"], 16 * NG)

        @block.gpsimd
        def _(pool):
            at = Count("pool", notes)

            def step(ins):
                ins.then_inc(sem["pool_step"], at.one("pool_step"))
                pool.wait_ge(sem["pool_step"], at.now("pool_step"))

            pool.dma_start(IDS[:], t["ids"]).then_inc(sem["ids_loaded"], 16)
            for w in (wq0, wk0, wv0):
                pool.memset(w, 0.0).then_inc(sem["w0_cleared"], 1)
            step(pool.memset(H[:], 0.0))
            pool.wait_ge(sem["ids_loaded"], 16)
            for b in range(NB):
                pool.indirect_dma_start(H[:, b, :], None, t["words"],
                                        bass.IndirectOffsetOnAxis(ap=IDS[:, b:b + 1], axis=0),
                                        bounds_check=VOCAB - 1, oob_is_err=False
                                        ).then_inc(sem["words_loaded"], 16)
            step(pool.memset(ident[:], 0.0))
            step(pool.affine_select(out=ident[:], in_=ident[:], compare_op=ALU.not_equal, fill=1.0, base=0,
                                    pattern=[[-1, 128]], channel_multiplier=1))
            pool.memset(ones[:], 1.0)
            pool.memset(expo[:, 0, :], -0.5)
            pool.memset(expo[:, 1, :], 0.5)
            pool.memset(V[:], 1.0)
            for e in range(NE):
                last = pool.memset(ORDER[:, :, e:e + 1], float(NE - e))
            last.then_inc(sem["constants_ready"], 1)

            def power(half, rows=T, width=GB):
                pool.wait_ge(sem["power_in"], at.take("power_in"))
                pool.tensor_tensor(RS[0:rows, 0:width], VE[0:rows, 0:width], expo[0:rows, half, 0:width],
                                   ALU.pow).then_inc(sem["power_out"], at.one("power_out"))

            power(1, NSLOT, 1)
            def powers(n):
                for _ in range(n):
                    power(0)

            powers(1)
            with at.loop(pool, NG - 1):
                powers(2)
            powers(1)

            pool.wait_ge(sem["attn0_done"], 1)
            pool.memset(bqk1, 0.0).then_inc(sem["area_cleared"], 1)
            pool.wait_ge(sem["area_cleared"], 1)
            step(pool.memset(XS[0:KD], 0.0))
            step(pool.memset(XS[KD:KD + 1], 1.0))
            with at.loop(pool, NG):
                powers(2)
                power(1)
            pool.wait_ge(sem["yt_ready"], 1 + NG)
            with at.loop(pool, NSLOT // RING) as j:
                for r in range(RING):
                    pool.wait_ge(sem[f"w1_used{r}"], at.now(f"w1_used{r}"))
                    at.one(f"w1_used{r}")
                pool.tensor_copy(XS[0:KD, :, :, 0:NB], YT[:, :, bass.ds(j * RING, RING), :]
                                 ).then_inc(sem["slot_rows"], at.one("slot_rows"))
            step(pool.memset(wqk1, 0.0))
            pool.wait_ge(sem["w1_loaded"], 16 * W1_LOADS)
            for k in range(2):
                for q in range(2):
                    dst = wqk1[:, k, q * 384:(q + 1) * 384].rearrange("p (j u d) -> p u j d", j=HPU, d=32)
                    src = wqkv1[:, k, q * D:(q + 1) * D].rearrange("p (u j d) -> p u j d", j=HPU, d=16)
                    last = pool.tensor_copy(dst[:, :, :, 0:16], src)
            last.then_inc(sem["padded"], 1)

            def gate():
                for c in range(CT3):
                    pool.wait_ge(sem["gate_ready"], at.take("gate_ready"))
                    pool.tensor_tensor(QT[:, c, :], HT[:, c, :], HT[:, 3 + c, :], ALU.mult
                                       ).then_inc(sem["gated"], at.one("gated"))

            powers(2)
            with at.loop(pool, NG - 1):
                powers(2)
                gate()
            powers(1)
            gate()
            with at.loop(pool, 2 * NG - 1):
                powers(1)

            def router_copies():
                def copy(g):
                    pool.wait_ge(sem["xt_ready"], at.take("xt_ready"))
                    here = (slice(None), slice(None), bass.ds(g * TG, TG))
                    pool.tensor_tensor(XALL_LR[here], XT[:], XALL_HR[here], ALU.subtract
                                       ).then_inc(sem["xt_copied"], at.one("xt_copied"))
                powers(1)
                with at.loop(pool, NG - 1) as g:
                    powers(1)
                    copy(g)
                copy(NG - 1)

            def split_weights(w1_cols, tiles):
                def used(e):
                    pool.wait_ge(sem[f"w1_used{e % RING}"], at.take(f"w1_used{e % RING}", NG))
                    pool.wait_ge(sem[f"w2_used{e % RING}"], at.take(f"w2_used{e % RING}"))

                for e in range(NE):
                    r = e % RING
                    if e >= 2:
                        used(e - 2)
                    c, f = (slice(None), slice(None), slice(0, w1_cols)), (slice(None), slice(0, tiles))
                    for src, high, high_r, low_r, name in (
                            (W1[r][c], W1_H[e % 2][c], W1_HR[e % 2][c], W1_LR[r][c], "w1"),
                            (W2[r][f], W2_H[e % 2][f], W2_HR[e % 2][f], W2_LR[r][f], "w2")):
                        pool.wait_ge(sem[f"{name}_loaded{r}"], at.take(f"{name}_loaded{r}", 16))
                        step(pool.tensor_copy(high_r, src))
                        pool.tensor_tensor(low_r, src, high_r, ALU.subtract
                                           ).then_inc(sem[f"{name}_split"], at.one(f"{name}_split"))
                used(NE - 2)
                used(NE - 1)

            for r in range(RING):
                for name in ("w1_loaded", "w2_loaded"):
                    at.one(f"{name}{r}", 16 * (NSLOT // RING))
                at.one(f"w2_used{r}", NSLOT // RING)
            router_copies()
            split_weights(I1, I1 // 128)
            pool.memset(V[:], 1.0).then_inc(sem["constants_ready"], 1)
            with at.loop(pool, 3 * NG):
                powers(1)
            router_copies()
            split_weights(FF, FT)

        @block.vector
        def _(dve):
            at = Count("dve", notes)
            at.one("yt_ready")
            tt, ts, stt = dve.tensor_tensor, dve.tensor_scalar, dve.scalar_tensor_tensor

            def step(ins):
                ins.then_inc(sem["vector_step"], at.one("vector_step"))
                dve.wait_ge(sem["vector_step"], at.now("vector_step"))

            def give(ins, name):
                ins.then_inc(sem[name], at.one(name))

            def full(k):
                dve.wait_ge(sem[f"bank_full{k}"], at.take(f"bank_full{k}"))
                return psum[k]

            def mark(name):
                n = at.bank(MARKS)
                give(dve.memset(marked[:, n:n + 1], 0.0), name)

            def free(ins, k):
                ins.then_inc(sem[f"bank_free{k}"], at.one(f"bank_free{k}"))
                dve.wait_ge(sem[f"bank_free{k}"], at.now(f"bank_free{k}"))

            def power(ins):
                give(ins, "power_in")
                dve.wait_ge(sem["power_out"], at.take("power_out"))

            def wide(ap, n):
                return ap.unsqueeze(2).to_broadcast([ap.shape[0], ap.shape[1], n])

            def layernorm(src, dst, eps=EPS, name=None):
                dve.sem_inc(sem["vector_passed"], 1)
                for bb in range(GB):
                    last = dve.bn_stats(ST[:, bb, :], src(bb))
                step(last)
                dve.sem_inc(sem["vector_passed"], 1)
                for bb in range(GB):
                    last = dve.bn_aggr(MV[:, bb, :], ST[:, bb, :])
                step(last)
                power(ts(VE[:], MV[:, :, 1], eps, None, ALU.add))
                if name:
                    dve.wait_ge(sem["xn_taken"], at.now(name))
                for bb in range(GB):
                    last = ts(dst(bb), src(bb), MV[:, bb, 0:1], RS[:, bb:bb + 1], ALU.subtract, ALU.mult)
                if name:
                    give(last, name)
                    dve.wait_ge(sem[name], at.now(name))
                else:
                    step(last)

            xn = lambda bb: XN[:, bb, :]
            x1 = lambda bb: X1[:, bb, :]

            def group(buf, g):
                return buf[:, bass.ds(g * GB, GB), :]

            def spread(v):
                return v.unsqueeze(1).to_broadcast([T, GB, D])

            def in_turns(prepare, consume, then):
                with at.loop(dve, NG - 1) as g:
                    prepare(g + 1)
                    consume(g)
                then()
                consume(NG - 1)
                at.first_banks()

            def a_of(g):
                return lambda bb: XA[:, bass.ds(g * GB + bb, 1), :].rearrange("p o d -> p (o d)")

            def h_of(g):
                return lambda bb: H[:, bass.ds(g * GB + bb, 1), :].rearrange("p o d -> p (o d)")

            def softmax_unit(n, pos):
                k = at.bank(SBANKS)
                dve.wait_ge(sem["scores_ready"], at.take("scores_ready"))
                scores = psum[k][0:T, 0:TU].rearrange("p (h t) -> p h t", h=HPU)
                p = PB[n % 2][:, 0:HPU, :]
                bb, unit = n // UPB, n % UPB
                if pos:
                    if unit == 0:
                        dve.wait_ge(sem[f"pos_loaded{bb % 2}"], at.take(f"pos_loaded{bb % 2}", 16))
                    ins = tt(p, scores, POS[bb % 2][:, HPU * unit:HPU * unit + HPU, :], ALU.add)
                    if unit == UPB - 1:
                        give(ins, "pos_used")
                        dve.wait_ge(sem["pos_used"], at.now("pos_used"))
                    else:
                        step(ins)
                    scores = p
                step(dve.tensor_reduce(MX[:, 0:HPU], scores, AX.X, ALU.max))
                give(tt(p, scores, wide(MX[:, 0:HPU], T), ALU.subtract), "probs_in")
                dve.wait_ge(sem["probs_in"], at.now("probs_in"))

            def norm_unit(n, dv):
                bb, unit = n // UPB, n % UPB
                k = at.bank(OBANKS)
                o = full(k)[0:T, 0:HPU * (dv + 1)].rearrange("p (h d) -> p h d", h=HPU)
                step(dve.reciprocal(RC[:, 0:HPU], o[:, :, dv]))
                on = ON[bb % 2][:, 0:HEADS * dv].rearrange("p (h d) -> p h d", d=dv)
                free(tt(on[:, HPU * unit:HPU * unit + HPU, :], o[:, :, 0:dv], wide(RC[:, 0:HPU], dv), ALU.mult), k)

            def attention(dv, pos, finish):
                for s in range(STEPS):
                    if s < UNITS:
                        softmax_unit(s, pos)
                    if 0 <= s - 2 < UNITS:
                        norm_unit(s - 2, dv)
                    if last_of(s - 4) is not None:
                        bb = last_of(s - 4)
                        k = at.bank(OBANKS)
                        finish(bb, full(k)[0:T, 0:D], k)

            def values(v, dv, bias):
                per = 2 * D // dv
                v5 = V[:, 0:GB * HEADS * (dv + 1)].rearrange("p (h d) -> p h d", d=dv + 1)
                for first in range(0, GB * HEADS, per):
                    k = at.bank(OBANKS)
                    src = full(k)[0:T, 0:per * dv].rearrange("p (h d) -> p h d", d=dv)
                    if bias is None:
                        last = dve.tensor_copy(v5[:, first:first + per, 0:dv], src)
                    else:
                        for j in range(per // HEADS):
                            last = tt(v5[:, first + j * HEADS:first + (j + 1) * HEADS, 0:dv],
                                      src[:, j * HEADS:(j + 1) * HEADS, :],
                                      bias.rearrange("p (h d) -> p h d", d=dv), ALU.add)
                    free(last, k)

            def pairs(consume):
                for first in range(0, GB, 2):
                    k = at.bank(OBANKS)
                    o = full(k)
                    last = None
                    for bb in (first, first + 1):
                        last = consume(bb, o[0:T, (bb - first) * D:(bb - first + 1) * D])
                    free(last, k)

            for k in SBANKS + OBANKS:
                dve.sem_inc(sem[f"bank_free{k}"], at.one(f"bank_free{k}"))
            dve.sem_inc(sem["pos_used"], at.one("pos_used"))

            dve.wait_ge(sem["slots_loaded"], 16 * 5)
            dve.wait_ge(sem["constants_ready"], 1)
            step(dve.tensor_tensor_reduce(out=SL2, in0=SL, in1=SL, scale=1.0, scalar=0.0,
                                          op0=ALU.mult, op1=ALU.add, accum_out=SM[0:NSLOT, 0:1]))
            power(ts(VE[0:NSLOT, 0:1], SM[0:NSLOT, 0:1], 1.0, None, ALU.mult))
            step(ts(MX[0:NSLOT, 0:1], RS[0:NSLOT, 0:1], EPS, None, ALU.max))
            step(dve.reciprocal(RC[0:NSLOT, 0:1], MX[0:NSLOT, 0:1]))
            give(ts(SL2, SL, RC[0:NSLOT, 0:1], slS[:, 0:1], ALU.mult, ALU.mult), "xn_ready")

            dve.wait_ge(sem["patches_loaded"], 64)
            dve.wait_ge(sem["words_loaded"], 16 * NB)
            step(tt(posE[:, 0, :], posE[:, 0, :], posE[:, 1, :], ALU.add))
            for first in range(0, NB, 2):
                k = at.bank(OBANKS)
                o = full(k)[0:NPATCH, 0:2 * D].rearrange("p (b d) -> p b d", b=2)
                for j in range(2):
                    last = tt(H[0:NPATCH, first + j, :], o[:, j, :], posE[:, 0, :], ALU.add)
                free(last, k)

            dve.wait_ge(sem["w0_loaded"], W0_LOADS)
            def prepare_a0(g):
                layernorm(h_of(g), xn, name="xn_ready")
                step(tt(group(XA, g), XN[:], spread(bo0), ALU.add))

            def attend_0(g):
                values(V, 16, bv0)
                attention(16, True, lambda bb, o, k: free(tt(a_of(g)(bb), o, a_of(g)(bb), ALU.add), k))
                layernorm(a_of(g), a_of(g), eps=1e-9)
                step(tt(group(XA, g), group(XA, g), spread(gamma0), ALU.mult))
                step(tt(group(XA, g), group(XA, g), spread(beta0), ALU.add))
                step(tt(group(H, g), group(H, g), group(XA, g), ALU.add))

            prepare_a0(0)
            in_turns(prepare_a0, attend_0, lambda: None)
            mark("attn0_done")

            with at.loop(dve, NG) as g:
                layernorm(h_of(g), x1)
                dve.wait_ge(sem["yt_ready"], at.now("yt_ready"))
                at.one("yt_ready")
                for bb in range(GB):
                    last = dve.tensor_tensor_reduce(out=XN[:, bb, :], in0=X1[:, bb, :], in1=X1[:, bb, :],
                                                    scale=1.0 / D, scalar=0.0, op0=ALU.mult, op1=ALU.add,
                                                    accum_out=SM[:, bb:bb + 1])
                step(last)
                power(ts(VE[:], SM[:], EPS, None, ALU.add))
                for bb in range(GB):
                    last = stt(XN[:, bb, :], X1[:, bb, :], RS[:, bb:bb + 1], nw0[:], ALU.mult, ALU.mult)
                give(last, "xn_ready")
                dve.wait_ge(sem["xn_ready"], at.now("xn_ready"))
                for bb in range(GB):
                    last = dve.tensor_tensor_reduce(out=X1[:, bb, :], in0=XN[:, bb, :], in1=XN[:, bb, :],
                                                    scale=1.0, scalar=0.0, op0=ALU.mult, op1=ALU.add,
                                                    accum_out=SM[:, bb:bb + 1])
                step(last)
                power(ts(VE[:], SM[:], 1.0, None, ALU.mult))
                step(ts(TS[:], RS[:], EPS, None, ALU.max))
                step(dve.reciprocal(TS[:], TS[:]))
                k = at.bank(OBANKS)
                o = full(k)[0:T, 0:GB * NSLOT].rearrange("p (b s) -> p b s", b=GB)
                free(tt(LG4, o, wide(TS[:], NSLOT), ALU.mult), k)
                give(dve.tensor_reduce(MX[:], LG4, AX.X, ALU.max), "slot_in")
                dve.wait_ge(sem["slot_in"], at.now("slot_in"))
                give(tt(CW, LG4, wide(MX[:], NSLOT), ALU.subtract), "probs_in")
                dve.wait_ge(sem["probs_in"], at.now("probs_in"))
                k = at.bank(SBANKS)
                dve.wait_ge(sem["scores_ready"], at.take("scores_ready"))
                o = psum[k][0:NSLOT, 0:TG].rearrange("p (b t) -> p b t", b=GB)
                step(dve.tensor_reduce(MX[0:NSLOT, :], o, AX.X, ALU.max))
                give(tt(DP, o, wide(MX[0:NSLOT, :], T), ALU.subtract), "probs_in")
                dve.wait_ge(sem["exp_ready"], at.take("exp_ready"))
                step(dve.tensor_reduce(SM[:], CW, AX.X, ALU.add))
                step(dve.reciprocal(RC[:], SM[:]))
                give(tt(CW, CW, wide(RC[:], NSLOT), ALU.mult), "slot_in")
                dve.wait_ge(sem["exp_ready"], at.take("exp_ready"))
                step(dve.tensor_reduce(SM[0:NSLOT, :], DP, AX.X, ALU.add))
                step(dve.reciprocal(RC[0:NSLOT, :], SM[0:NSLOT, :]))
                give(tt(DP, DP, wide(RC[0:NSLOT, :], T), ALU.mult), "slot_in")

            with at.loop(dve, NSLOT // RING) as j:
                for half in range(2):
                    k = at.bank(SBANKS)
                    src = full(k)[:, 0:3 * 128].rearrange("p (f c) -> p f c", f=3)
                    free(dve.tensor_copy(HS[:, 3 * half:3 * half + 3, :], src), k)
                k = at.bank(OBANKS)
                free(dve.tensor_copy(YR, full(k)[:, 0:D]), k)
                k = at.bank(OBANKS)
                o = full(k)[0:KD, 0:2 * 128].rearrange("p (m s b) -> p m s b", m=2, s=RING)
                for m in range(2):
                    s = bass.ds(j * RING, RING)
                    last = tt(Y2T[:, m, s, :], o[:, m, :, 0:NB], wide(fb2[:, m, s], NB), ALU.add)
                free(last, k)

            for first in range(0, NB, 2):
                k = at.bank(OBANKS)
                o = full(k)[0:T, 0:2 * D].rearrange("p (b d) -> p b d", b=2)
                free(tt(H[:, first:first + 2, :], H[:, first:first + 2, :], o, ALU.add), k)

            dve.wait_ge(sem["padded"], 1)
            def prepare_c1(g):
                layernorm(h_of(g), a_of(g))
                layernorm(a_of(g), xn, name="xn_ready")

            def convolve(g):
                for c in range(CT3):
                    k = at.bank(SBANKS)
                    src = full(k)[:, 0:TG].rearrange("p (b t) -> p b t", b=GB)
                    y = HT[:, c, :].rearrange("p (b t) -> p b t", b=GB)
                    step(ts(y, src, cw1[:, c, 3:4], cb1[:, c:c + 1], ALU.mult, ALU.add))
                    for lag in (1, 2):
                        step(stt(y[:, :, lag:], src[:, :, :T - lag], cw1[:, c, 3 - lag:4 - lag],
                                 y[:, :, lag:], ALU.mult, ALU.add))
                    give(stt(y[:, :, 3:], src[:, :, :T - 3], cw1[:, c, 0:1], y[:, :, 3:],
                             ALU.mult, ALU.add), "conv_ready")
                    mark(f"bank_free{k}")
                pairs(lambda bb, o: tt(a_of(g)(bb), a_of(g)(bb), o, ALU.add))

            def prepare_a1(g):
                layernorm(a_of(g), xn, name="xn_ready")
                step(tt(group(XA, g), group(XA, g), spread(bp1), ALU.add))

            def attend_1(g):
                values(V, 16, bv1)
                attention(16, False, lambda bb, o, k: free(tt(a_of(g)(bb), a_of(g)(bb), o, ALU.add), k))

            def prepare_f1(g):
                layernorm(a_of(g), xn, name="xn_ready")
                step(tt(group(XA, g), group(XA, g), spread(bf2), ALU.add))

            def mlp_1(g):
                pairs(lambda bb, o: tt(a_of(g)(bb), a_of(g)(bb), o, ALU.add))
                step(tt(group(H, g), group(H, g), group(XA, g), ALU.add))

            def prepare_h(g):
                layernorm(h_of(g), xn, name="xn_ready")

            prepare_c1(0)
            in_turns(prepare_c1, convolve, lambda: prepare_a1(0))
            in_turns(prepare_a1, attend_1, lambda: prepare_f1(0))
            in_turns(prepare_f1, mlp_1, lambda: prepare_h(0))
            mark("attn1_done")

            def logits(g):
                k = at.bank(OBANKS)
                o = full(k)[0:T, 0:GB * NE].rearrange("p (b e) -> p b e", b=GB)
                free(dve.tensor_copy(LG[:, bass.ds(g * GB, GB), :], o), k)

            def probabilities():
                step(dve.tensor_reduce(E2[0][:], LG[:], AX.X, ALU.max))
                give(tt(E1[0], LG[:], wide(E2[0][:], NE), ALU.subtract), "probs_in")
                dve.wait_ge(sem["exp_ready"], at.take("exp_ready"))
                step(dve.tensor_reduce(E2[0][:], E1[0], AX.X, ALU.add))
                step(dve.reciprocal(E2[1][:], E2[0][:]))
                step(tt(E1[0], E1[0], wide(E2[1][:], NE), ALU.mult))

            def best_two():
                step(dve.tensor_copy(E1[2], E1[0]))
                for n in range(2):
                    step(dve.tensor_reduce(E2[0][:], E1[2], AX.X, ALU.max))
                    step(tt(E1[3], E1[2], wide(E2[0][:], NE), ALU.is_equal))
                    step(tt(E1[3], E1[3], ORDER[:], ALU.mult))
                    step(dve.tensor_reduce(E2[1][:], E1[3], AX.X, ALU.max))
                    step(tt(E1[4 + n], ORDER[:], wide(E2[1][:], NE), ALU.is_equal))
                    if n == 0:
                        step(stt(E1[2], E1[4], -2.0, E1[2], ALU.mult, ALU.add))
                step(tt(E1[4], E1[4], E1[5], ALU.add))
                step(tt(E1[1], E1[0], E1[4], ALU.mult))

            def share():
                step(dve.tensor_reduce(E2[0][:], E1[1], AX.X, ALU.add))
                step(dve.reciprocal(E2[1][:], E2[0][:]))
                step(tt(E1[1], E1[1], wide(E2[1][:], NE), ALU.mult))

            def experts(tiles):
                for e in range(NE):
                    with at.loop(dve, NG) as g:
                        for m in range(tiles):
                            dve.wait_ge(sem["hidden_ready"], at.take("hidden_ready"))
                            give(tt(HT_LR[:, m, :], HT[:, m, :], HT_HR[:, m, :], ALU.subtract), "hidden_split")
                        for bb in range(GB):
                            k = at.bank(SBANKS if bb < 2 else OBANKS)
                            h = h_of(g)(bb)
                            free(stt(h, full(k)[0:T, 0:D], E1[1][:, bass.ds(g * GB + bb, 1), e], h,
                                     ALU.mult, ALU.add), k)
                    mark(f"w2_used{e % RING}")

            in_turns(prepare_h, logits, lambda: None)
            probabilities()
            mark("router_ready")
            best_two()
            k = at.bank(OBANKS)
            o = full(k)[0:T, 0:NB * NE].rearrange("p (b e) -> p e b", e=NE)
            free(dve.tensor_reduce(RUN[:], o, AX.X, ALU.add), k)
            step(ts(RUN[:], RUN[:], -1.0, 1.0 - 0.9, ALU.add, ALU.mult))
            step(ts(RUN[:], RUN[:], 1.0, 0.01, ALU.add, ALU.add))
            step(dve.reciprocal(RUN[:], RUN[:]))
            step(tt(E1[1], E1[1], RUN[:].unsqueeze(1).to_broadcast([T, NB, NE]), ALU.mult))
            share()
            experts(I1 // 128)

            dve.wait_ge(sem["w2_loaded"], 16 * W2_LOADS)
            dve.wait_ge(sem["constants_ready"], 2)
            def prepare_a2(g):
                layernorm(h_of(g), xn, name="xn_ready")
                step(tt(group(H, g), group(H, g), spread(bo2), ALU.add))

            def attend_2(g):
                values(V, 64, None)
                attention(64, False, lambda bb, o, k: free(tt(h_of(g)(bb), h_of(g)(bb), o, ALU.add), k))

            def mlp_2(g):
                pairs(lambda bb, o: tt(h_of(g)(bb), h_of(g)(bb), o, ALU.add))

            def attend_3(g):
                for first in range(0, GB, 2):
                    k = at.bank(OBANKS)
                    o = full(k)
                    for bb in (first, first + 1):
                        last = tt(V[:, bb * D:(bb + 1) * D], o[0:T, (bb - first) * D:(bb - first + 1) * D],
                                  bv3, ALU.add)
                    free(last, k)
                k = at.bank(SBANKS)
                o = full(k)[0:T, 0:TG].rearrange("p (b t) -> p b t", b=GB)
                free(stt(PT[0][:], o, float(np.float32(1) / np.sqrt(np.float32(D))),
                         decay.unsqueeze(1).to_broadcast([T, GB, T]), ALU.mult, ALU.mult), k)
                mlp_2(g)

            prepare_a2(0)
            in_turns(prepare_a2, attend_2, lambda: prepare_h(0))

            in_turns(prepare_h, mlp_2, lambda: prepare_h(0))
            in_turns(prepare_h, attend_3, lambda: prepare_h(0))

            in_turns(prepare_h, logits, lambda: None)
            probabilities()
            best_two()
            share()
            mark("router_ready")
            for first in range(0, NB, 2):
                k = at.bank(OBANKS)
                o = full(k)[0:T, 0:2 * D].rearrange("p (b d) -> p b d", b=2)
                free(tt(H[:, first:first + 2, :], H[:, first:first + 2, :], o, ALU.add), k)
            experts(FT)
            for _ in range(NG):
                mark("out_ready")

        @block.scalar
        def _(act):
            at = Count("act", notes)
            activation = act.activation

            def give(ins, name):
                ins.then_inc(sem[name], at.one(name))

            def full(k):
                act.wait_ge(sem[f"bank_full{k}"], at.take(f"bank_full{k}"))
                return psum[k]

            def free(ins, k):
                give(ins, f"bank_free{k}")

            def mark(name):
                n = at.bank(MARKS)
                give(activation(amarked[:, n:n + 1], ident[0:1, 0:1], ACT.Copy), name)

            def turned(dst, scale=None, bias=None):
                for part in range(2):
                    k = at.bank(XBANKS)
                    src = full(k)[0:KD, 0:TG]
                    if scale is None:
                        free(activation(dst[:, part, :], src, ACT.Copy), k)
                    else:
                        free(activation(dst[:, part, :], src, ACT.Identity, scale=scale[:, part:part + 1],
                                        bias=bias[:, part:part + 1]), k)

            def hidden(tiles, func, bias, src_ready=None):
                for m in range(tiles):
                    k = at.bank(FBANKS)
                    src = full(k)[:, 0:TG]
                    free(activation(HT[:, m, :], src, func, bias=0.0 if bias is None else bias(m)), k)

            def hidden_parts(tiles, func, bias):
                def high(m, k, n):
                    act.wait_ge(sem[f"bank_free{k}"], n)
                    give(activation(HT_HR[:, m, :], HT[:, m, :], ACT.Copy), "hidden_ready")

                last = None
                for m in range(tiles):
                    k = at.bank(FBANKS)
                    free(activation(HT[:, m, :], full(k)[:, 0:TG], func, bias=0.0 if bias is None else bias(m)), k)
                    if last:
                        high(*last)
                    last = m, k, at.now(f"bank_free{k}") + 1
                high(*last)

            def exponentials(buf, scale=1.0, name="probs_ready"):
                act.wait_ge(sem["probs_in"], at.take("probs_in"))
                give(activation(buf, buf, ACT.Exp, scale=scale), name)

            def attention(dv, scale, pos=None):
                for s in range(STEPS):
                    if s < UNITS:
                        exponentials(PB[s % 2][:, 0:HPU, :], scale)
                    if 0 <= s - 1 < UNITS:
                        k = at.bank(TBANKS)
                        src = full(k)[0:T, 0:TU].rearrange("p (h t) -> p h t", h=HPU)
                        free(activation(PT[(s - 1) % 2][:, 0:HPU, :], src, ACT.Copy), k)
                    if last_of(s - 3) is not None:
                        ot = OT[last_of(s - 3) % 2]
                        rows, tiles = (KD, 2) if dv == 16 else (128, 3)
                        for first in range(0, HEADS * dv // rows, tiles):
                            k = at.bank(XBANKS)
                            src = full(k)[0:rows, 0:tiles * T].rearrange("p (k t) -> p k t", k=tiles)
                            free(activation(ot[0:rows, first:first + tiles, :], src, ACT.Copy), k)
                    if pos and s in (UPB, 2 * UPB):
                        pos()

            for k in TBANKS + XBANKS:
                act.sem_inc(sem[f"bank_free{k}"], 1)
            act.sem_inc(sem["yt_ready"], 1)

            act.wait_ge(sem["constants_ready"], 1)
            k = at.bank(XBANKS)
            src = full(k)[0:KD, 0:2 * NSLOT].rearrange("p (k s) -> p k s", k=2)
            free(activation(slT[:], src, ACT.Copy), k)

            act.wait_ge(sem["w0_loaded"], W0_LOADS)
            for p in range(6):
                k = at.bank(TBANKS)
                free(activation(RT[:, p, :], full(k)[:, 0:NREL], ACT.Copy), k)
            with at.loop(act, NG) as g:
                turned(XT)
                for p in range(6):
                    k = at.bank(XBANKS)
                    src = full(k)[:, 0:TG]
                    activation(QT[:, p, :], src, ACT.Identity, bias=rw0[:, p:p + 1])
                    free(activation(QR[:, p, :], src, ACT.Identity, bias=rr0[:, p:p + 1]), k)
                for p in range(6):
                    k = at.bank(XBANKS)
                    free(activation(KT[:, p, :], full(k)[:, 0:TG], ACT.Identity, bias=bk0[:, p:p + 1]), k)

                def pos_rows():
                    act.wait_ge(sem["pr_stored"], at.now("pr_ready") * 16 + 16)
                    for h0, h1 in POS_PAIRS:
                        k = at.bank(XBANKS)
                        src = full(k)[0:T, 0:2 * NREL].rearrange("p (h n) -> p h n", h=2)
                        free(activation(PR[:, h0:h1 + 1:h1 - h0, 0:NREL], src, ACT.Copy), k)
                    mark("pr_ready")

                pos_rows()
                pos_rows()
                attention(16, 0.125, pos_rows)

            with at.loop(act, NG) as g:
                turned(XT)
                exponentials(CW, name="exp_ready")
                exponentials(DP, name="exp_ready")
                k = at.bank(TBANKS)
                src = full(k)[0:NSLOT, 0:TG].rearrange("p (b t) -> p b t", b=GB)
                free(activation(CT[:, bass.ds(g * GB, GB), :], src, ACT.Copy), k)
                k = at.bank(TBANKS)
                src = full(k)[0:T, 0:GB * NSLOT].rearrange("p (b s) -> p b s", b=GB)
                free(activation(DW, src, ACT.Copy), k)
                k = at.bank(XBANKS)
                src = full(k)[0:KD, :].rearrange("p (k b s) -> p k s b", k=2, b=GB)
                activation(YT[:, 0, :, bass.ds(g * GB, GB)], src[:, 0], ACT.Copy)
                free(activation(YT[:, 1, :, bass.ds(g * GB, GB)], src[:, 1], ACT.Copy), k)
                mark("yt_ready")
            with at.loop(act, NSLOT // RING) as j:
                for c0, c1 in ((0, 512), (512, FF)):
                    k = at.bank(TBANKS)
                    free(activation(HR[:, c0:c1], full(k)[:, 0:c1 - c0], ACT.Gelu), k)
            for b in range(NB):
                k = at.bank(XBANKS)
                free(activation(Y2[b % 2], full(k)[0:NSLOT, 0:D], ACT.Copy), k)

            act.wait_ge(sem["w1_loaded"], 16 * W1_LOADS)
            act.wait_ge(sem["padded"], 1)
            with at.loop(act, NG) as g:
                turned(XT, g1[:, 0, :], b1[:, 0, :])
                for c in range(CT3):
                    k = at.bank(TBANKS)
                    free(activation(HT[:, 3 + c, :], full(k)[:, 0:TG], ACT.Silu), k)
                    act.wait_ge(sem["conv_ready"], at.take("conv_ready"))
                    give(activation(HT[:, c, :], HT[:, c, :], ACT.Silu), "gate_ready")
            with at.loop(act, NG) as g:
                turned(XT, g1[:, 1, :], b1[:, 1, :])
                for dst in range(6):
                    k = at.bank(XBANKS)
                    free(activation((QT, KT)[dst // 3][:, dst % 3, :], full(k)[:, 0:TG], ACT.Identity,
                                    bias=bqk1[:, dst:dst + 1]), k)
                attention(16, 0.25)
            with at.loop(act, NG) as g:
                turned(XT, g1[:, 2, :], b1[:, 2, :])
                hidden(FT, ACT.Gelu, lambda m: bf1[:, m:m + 1])

            def router_inputs():
                with at.loop(act, NG) as g:
                    for part in range(2):
                        k = at.bank(XBANKS)
                        src = full(k)[0:KD, 0:TG]
                        activation(XT[:, part, :], src, ACT.Copy)
                        free(activation(XALL_HR[:, part, bass.ds(g * TG, TG)], src, ACT.Copy), k)
                    mark("xt_ready")

            act.wait_ge(sem["attn1_done"], 1)
            router_inputs()
            exponentials(E1[0], name="exp_ready")
            for e in range(NE):
                with at.loop(act, NG) as g:
                    hidden_parts(I1 // 128, ACT.Silu, None)

            act.wait_ge(sem["w2_loaded"], 16 * W2_LOADS)
            with at.loop(act, NG) as g:
                turned(XT)
                for buf in (QT, KT):
                    for p in range(6):
                        k = at.bank(XBANKS)
                        free(activation(buf[:, p, :], full(k)[:, 0:TG], ACT.Copy), k)
                attention(64, 0.125)

            with at.loop(act, NG) as g:
                turned(XT)
                hidden(FT, ACT.Gelu, lambda m: bi2[:, m:m + 1])
            with at.loop(act, NG) as g:
                turned(XT)
                for dst in range(4):
                    k = at.bank(XBANKS)
                    free(activation((QT, KT)[dst // 2][0:KD, dst % 2, :], full(k)[0:KD, 0:TG], ACT.Identity,
                                    bias=bqk3[:, dst:dst + 1]), k)

            router_inputs()
            exponentials(E1[0], name="exp_ready")
            for first in range(0, NB, 4):
                k = at.bank(TBANKS)
                src = full(k)[0:NE, 0:TG].rearrange("p (b t) -> p b t", b=4)
                free(activation(WT8[:, first:first + 4, :], src, ACT.Copy), k)
            for e in range(NE):
                with at.loop(act, NG) as g:
                    hidden_parts(FT, ACT.Gelu, lambda m: bb1[:, e, m:m + 1])

        @block.tensor
        def _(pe):
            at = Count("pe", notes)

            def claim(banks):
                k = at.bank(banks)
                pe.wait_ge(sem[f"bank_free{k}"], at.now(f"bank_full{k}") + 1)
                return k, psum[k]

            def filled(ins, k):
                ins.then_inc(sem[f"bank_full{k}"], at.one(f"bank_full{k}"))
                return k, at.now(f"bank_full{k}")

            def moved(*fillings):
                for k, n in fillings:
                    pe.wait_ge(sem[f"bank_free{k}"], n + 1)

            def product(dst, pieces):
                for n, (lhsT, rhs) in enumerate(pieces):
                    last = pe.matmul(dst, lhsT, rhs, start=n == 0, stop=n == len(pieces) - 1)
                    if n == 0 and len(pieces) > 1:
                        say_taken(last)
                return last

            fresh = []

            def say_taken(ins):
                if fresh:
                    fresh.clear()
                    ins.then_inc(sem["xn_taken"], 1)

            def turn_group(src):
                out = []
                for part in range(2):
                    k, p = claim(XBANKS)
                    for bb in range(GB):
                        last = pe.transpose(p[0:KD, cols(bb)], src[:, bb, part * KD:(part + 1) * KD],
                                            ident[0:T, 0:T])
                    out.append(filled(last, k))
                return out

            def xt():
                pe.wait_ge(sem["xn_ready"], at.take("xn_ready"))
                moved(*turn_group(XN))
                fresh.append(True)

            def two(w, n0, n1, x=XT):
                return [(w[:, part, n0:n1], x[:, part, :]) for part in range(2)]

            def token_rows(x, bb, w, n0=0, n1=D):
                return [(x[:, part, cols(bb)], w[:, part, n0:n1]) for part in range(w.shape[1])]

            def pairs(pieces):
                out = []
                for first in range(0, GB, 2):
                    k, p = claim(OBANKS)
                    for bb in (first, first + 1):
                        last = product(p[0:T, (bb - first) * D:(bb - first + 1) * D], pieces(bb))
                    out.append(filled(last, k))
                return out

            def mlp(tiles, w1, x, w2, w1_used=None):
                tokens = []
                for m in range(tiles):
                    k, p = claim(FBANKS)
                    last = product(p[:, 0:TG], [(w1[:, part, m * 128:(m + 1) * 128], x(part)) for part in range(2)])
                    tokens.append(filled(last, k))
                for first in range(0, GB, 2):
                    k, p = claim(OBANKS)
                    for bb in (first, first + 1):
                        for m in range(tiles):
                            if bb == 0:
                                moved(tokens[m])
                            last = pe.matmul(p[0:T, (bb - first) * D:(bb - first + 1) * D], HT[:, m, cols(bb)],
                                             w2[:, m, 0:D], start=m == 0, stop=m == tiles - 1)
                            if bb == 0 and m == 0 and w1_used:
                                last.then_inc(sem[w1_used], at.one(w1_used))
                    filled(last, k)

            def attention(dk, per_tile, dv, wo, pos=None):
                v5 = V[:, 0:GB * HEADS * (dv + 1)].rearrange("p (h d) -> p h d", d=dv + 1)
                pt_moved, on_moved, ot_moved = {}, {}, {}
                for s in range(STEPS):
                    if s < UNITS:
                        bb, unit = s // UPB, s % UPB
                        k = at.bank(SBANKS)
                        if s < 2:
                            pe.wait_ge(sem[f"bank_free{k}"], at.now(f"bank_full{k}") + 1)
                        for j in range(HPU):
                            h = HPU * unit + j
                            last = pe.matmul(psum[k][0:T, cols(j)], head(QT, h, per_tile, dk, cols(bb)),
                                             head(KT, h, per_tile, dk, cols(bb)), start=True, stop=True)
                        last.then_inc(sem["scores_ready"], at.one("scores_ready"))
                    if 0 <= s - 1 < UNITS:
                        pe.wait_ge(sem["probs_ready"], at.take("probs_ready"))
                        k, p = claim(TBANKS)
                        for j in range(HPU):
                            last = pe.transpose(p[0:T, cols(j)], PB[(s - 1) % 2][:, j, :], ident[0:T, 0:T])
                        pt_moved[s - 1] = filled(last, k)
                    if 0 <= s - 2 < UNITS:
                        bb, unit = (s - 2) // UPB, (s - 2) % UPB
                        moved(pt_moved[s - 2])
                        k, p = claim(OBANKS)
                        for j in range(HPU):
                            last = pe.matmul(p[0:T, j * (dv + 1):(j + 1) * (dv + 1)], PT[s % 2][:, j, :],
                                             v5[:, bb * HEADS + HPU * unit + j, :], start=True, stop=True)
                        on_moved[bb] = filled(last, k)
                    bb = last_of(s - 3)
                    if bb is not None:
                        moved(on_moved[bb])
                        rows, tiles = (KD, 2) if dv == 16 else (128, 3)
                        for first in range(0, HEADS * dv // rows, tiles):
                            k, p = claim(XBANKS)
                            for j in range(tiles):
                                c = (first + j) * rows
                                last = pe.transpose(p[0:rows, cols(j)], ON[bb % 2][:, c:c + rows], ident[0:T, 0:T])
                            ot_moved[bb] = filled(last, k)
                            ot_moved[bb, first] = ot_moved[bb]
                    if pos and s in (UPB, 2 * UPB):
                        pos(2 if s == UPB else 3)
                    bb = last_of(s - 4)
                    if bb is not None:
                        rows = KD if dv == 16 else 128
                        moved(*[f for key, f in ot_moved.items() if isinstance(key, tuple) and key[0] == bb])
                        k, p = claim(OBANKS)
                        filled(product(p[0:T, 0:D], [(OT[bb % 2][0:rows, n, :], wo[0:rows, n, :])
                                                     for n in range(HEADS * dv // rows)]), k)

            pe.wait_ge(sem["constants_ready"], 1)
            pe.wait_ge(sem["xn_ready"], at.take("xn_ready"))
            k, p = claim(XBANKS)
            for part in range(2):
                last = pe.transpose(p[0:KD, part * NSLOT:(part + 1) * NSLOT], SL2[:, part * KD:(part + 1) * KD],
                                    ident[0:NSLOT, 0:NSLOT])
            filled(last, k)
            fresh.append(True)

            pe.wait_ge(sem["patches_loaded"], 64)
            for first in range(0, NB, 2):
                k, p = claim(OBANKS)
                for j in range(2):
                    last = product(p[0:NPATCH, j * D:(j + 1) * D],
                                   [(patchT[:, n, first + j, :], convT[:, n, :]) for n in range(KP // 128)])
                f = filled(last, k)
            moved(f)

            pe.wait_ge(sem["w0_loaded"], W0_LOADS)
            r_moved = []
            for p6 in range(6):
                k, p = claim(TBANKS)
                r_moved.append(filled(product(p[:, 0:NREL], [(rker[:, part, p6 * 128:(p6 + 1) * 128],
                                                              posT[:, part, :]) for part in range(2)]), k))
            moved(*r_moved[-2:])
            with at.loop(pe, NG) as g:
                xt()
                v_moved = []
                for first in range(0, GB, 2):
                    k, p = claim(OBANKS)
                    for bb in (first, first + 1):
                        for part in range(2):
                            c = (bb - first) * D + part * KD
                            last = pe.matmul(p[0:T, c:c + KD], XT[:, part, cols(bb)], wv0[:, part, :],
                                             start=True, stop=True)
                            say_taken(last)
                    v_moved.append(filled(last, k))
                qk = []
                for w in (wq0, wk0):
                    for p6 in range(6):
                        k, p = claim(XBANKS)
                        part, c = p6 // 3, (p6 % 3) * 128
                        qk.append(filled(pe.matmul(p[:, 0:TG], w[:, part, c:c + 128], XT[:, part, :],
                                                   start=True, stop=True), k))
                moved(*qk[-2:], *v_moved)

                def pos(bb):
                    for pair in POS_PAIRS:
                        k, p = claim(XBANKS)
                        for j, h in enumerate(pair):
                            last = pe.matmul(p[0:T, j * NREL:(j + 1) * NREL], head(QR, h, 2, 64, cols(bb)),
                                             head(RT, h, 2, 64, slice(0, NREL)), start=True, stop=True)
                        filled(last, k)

                pos(0)
                pos(1)
                attention(64, 2, 16, wo0, pos)

            with at.loop(pe, NG) as g:
                xt()
                k, p = claim(OBANKS)
                for bb in range(GB):
                    last = product(p[0:T, bb * NSLOT:(bb + 1) * NSLOT], token_rows(XT, bb, slT, 0, NSLOT))
                filled(last, k)
                pe.wait_ge(sem["slot_in"], at.take("slot_in"))
                k = at.bank(SBANKS)
                pe.wait_ge(sem[f"bank_free{k}"], at.now(f"bank_full{k}") + 1)
                pe.sem_inc(sem["tensor_passed"], 1)
                for bb in range(GB):
                    last = pe.transpose(psum[k][0:NSLOT, cols(bb)], LG4[:, bb, :], ident[0:T, 0:T])
                last.then_inc(sem["scores_ready"], at.one("scores_ready"))
                pe.wait_ge(sem["slot_in"], at.take("slot_in"))
                k, p = claim(TBANKS)
                pe.sem_inc(sem["tensor_passed"], 1)
                for bb in range(GB):
                    last = pe.transpose(p[0:NSLOT, cols(bb)], CW[:, bb, :], ident[0:T, 0:T])
                filled(last, k)
                pe.wait_ge(sem["slot_in"], at.take("slot_in"))
                k, p = claim(TBANKS)
                pe.sem_inc(sem["tensor_passed"], 1)
                for bb in range(GB):
                    last = pe.transpose(p[0:T, bb * NSLOT:(bb + 1) * NSLOT], DP[:, bb, :], ident[0:NSLOT, 0:NSLOT])
                moved(filled(last, k))
                k, p = claim(XBANKS)
                for part in range(2):
                    for bb in range(GB):
                        c = (part * GB + bb) * NSLOT
                        last = pe.matmul(p[0:KD, c:c + NSLOT], XN[:, bb, part * KD:(part + 1) * KD], DW[:, bb, :],
                                         start=True, stop=True)
                y_moved = filled(last, k)
            last_bank = y_moved[0]
            pe.wait_ge(sem[f"bank_free{last_bank}"], at.now(f"bank_full{last_bank}") + 1)

            def slots_product(o, n, piece, used=None):
                for m in range(n):
                    for r in range(RING):
                        last = pe.matmul(o[32 * r:32 * r + 32, :], *piece(r, m), start=m == 0, stop=m == n - 1)
                        if used and m == n - 1 and r < RING - 1:
                            last.then_inc(sem[f"{used}{r}"], at.one(f"{used}{r}"))
                return last

            with at.loop(pe, NSLOT // RING) as j:
                pe.wait_ge(sem["slot_rows"], at.take("slot_rows"))
                for r in range(RING):
                    pe.wait_ge(sem[f"w1_loaded{r}"], at.take(f"w1_loaded{r}", 16))
                rows = (KD + 1, KD)
                hidden_moved = []
                for c0, c1 in ((0, 512), (512, FF)):
                    k, p = claim(TBANKS)
                    hidden_moved.append(filled(slots_product(p[:, 0:c1 - c0], 2, lambda r, m: (
                        XS[0:rows[m], m, r, :], W1B[r][0:rows[m], m, c0:c1])), k))
                moved(*hidden_moved)
                turned = []
                for half in range(2):
                    k, p = claim(SBANKS)
                    for f in range(3):
                        last = pe.transpose(p[:, f * 128:(f + 1) * 128],
                                            HR[:, (3 * half + f) * 128:(3 * half + f + 1) * 128], ident[:])
                        if f < RING // 2:
                            last.then_inc(sem[f"w1_used{2 * half + f}"], at.one(f"w1_used{2 * half + f}"))
                    turned.append(filled(last, k))
                for r in range(RING):
                    pe.wait_ge(sem[f"w2_loaded{r}"], at.take(f"w2_loaded{r}", 16))
                moved(*turned)
                k, p = claim(OBANKS)
                moved(filled(slots_product(p[:, 0:D], FT, lambda r, f: (
                    HS[:, f, 32 * r:32 * r + 32], W2[r][:, f, :]), "w2_used"), k))
                k, p = claim(OBANKS)
                for part in range(2):
                    last = pe.transpose(p[0:KD, part * 128:(part + 1) * 128], YR[:, part * KD:(part + 1) * KD],
                                        ident[:])
                    if part == 0:
                        last.then_inc(sem[f"w2_used{RING - 1}"], at.one(f"w2_used{RING - 1}"))
                y_moved = filled(last, k)
            pe.wait_ge(sem[f"bank_free{y_moved[0]}"], at.now(f"bank_full{y_moved[0]}") + 1)

            y2 = {}
            for s in range(NB + 1):
                if s < NB:
                    k, p = claim(XBANKS)
                    for part in range(2):
                        last = pe.transpose(p[0:NSLOT, part * KD:(part + 1) * KD], Y2T[:, part, :, s],
                                            ident[0:KD, 0:KD])
                    y2[s] = filled(last, k)
                if s >= 1:
                    b = s - 1
                    moved(y2[b])
                    if b % 2 == 0:
                        k, p = claim(OBANKS)
                        kk = k
                    last = pe.matmul(psum[kk][0:T, (b % 2) * D:(b % 2 + 1) * D], CT[:, b, :], Y2[b % 2],
                                     start=True, stop=True)
                    if b % 2:
                        filled(last, kk)

            pe.wait_ge(sem["w1_loaded"], 16 * W1_LOADS)
            pe.wait_ge(sem["padded"], 1)
            with at.loop(pe, NG) as g:
                xt()
                for c in range(CT3):
                    k, p = claim(SBANKS)
                    filled(product(p[:, 0:TG], two(win1, c * 128, (c + 1) * 128)), k)
                    k, p = claim(TBANKS)
                    filled(product(p[:, 0:TG], two(win1, INNER + c * 128, INNER + (c + 1) * 128)), k)
                pe.wait_ge(sem["gated"], at.take("gated", CT3))
                pairs(lambda bb: token_rows(QT[:, 0:CT3, :], bb, wout1))
            with at.loop(pe, NG) as g:
                xt()
                qk = []
                for dst in range(6):
                    k, p = claim(XBANKS)
                    qk.append(filled(product(p[:, 0:TG], two(wqk1, dst * 128, (dst + 1) * 128)), k))
                v_moved = pairs(lambda bb: token_rows(XT, bb, wqkv1, 2 * D, 3 * D))
                moved(*qk[-2:], *v_moved)
                attention(16, 4, 16, wp1)
            with at.loop(pe, NG) as g:
                xt()
                mlp(FT, wf1, lambda part: XT[:, part, :], wf2)

            def router_inputs(w):
                with at.loop(pe, NG) as g:
                    xt()
                    k, p = claim(OBANKS)
                    for bb in range(GB):
                        last = product(p[0:T, bb * NE:(bb + 1) * NE], token_rows(XT, bb, w, 0, NE))
                    filled(last, k)
                    pe.wait_ge(sem["xt_copied"], at.take("xt_copied"))

            def by_parts(stationary, moving):
                (s_high, s_low), (m_high, m_low) = stationary, moving
                return [(s_high, m_high), (s_high, m_low), (s_low, m_high)]

            def experts(tiles):
                for e in range(NE):
                    r = e % RING
                    pe.wait_ge(sem["w1_split"], at.take("w1_split"))
                    pe.wait_ge(sem["w2_split"], at.take("w2_split"))
                    with at.loop(pe, NG) as g:
                        for m in range(tiles):
                            k, p = claim(FBANKS)
                            c = slice(m * 128, (m + 1) * 128)
                            pieces = []
                            for part in range(2):
                                pieces += by_parts([w[:, part, c] for w in (W1_HR[e % 2], W1_LR[r])],
                                                   [x[:, part, bass.ds(g * TG, TG)] for x in (XALL_HR, XALL_LR)])
                            filled(product(p[:, 0:TG], pieces), k)
                        banks = [claim(SBANKS if bb < 2 else OBANKS) for bb in range(GB)]
                        for m in range(tiles):
                            pe.wait_ge(sem["hidden_split"], at.take("hidden_split"))
                            for bb, (k, p) in enumerate(banks):
                                for n, (lhsT, rhs) in enumerate(by_parts(
                                        [h[:, m, cols(bb)] for h in (HT_HR, HT_LR)],
                                        [w[:, m, :] for w in (W2_HR[e % 2], W2_LR[r])])):
                                    last = pe.matmul(p[0:T, 0:D], lhsT, rhs, start=m == 0 and n == 0,
                                                     stop=m == tiles - 1 and n == 2)
                                    if bb == 0 and m == 0 and n == 0:
                                        last.then_inc(sem[f"w1_used{r}"], at.one(f"w1_used{r}"))
                                if m == tiles - 1:
                                    filled(last, k)

            router_inputs(rt1)
            pe.wait_ge(sem["router_ready"], at.take("router_ready"))
            k, p = claim(OBANKS)
            filled(pe.matmul(p[0:T, 0:NB * NE], ones[0:T, 0:T], E1[0].rearrange("p b e -> p (b e)"),
                             start=True, stop=True), k)
            experts(I1 // 128)

            pe.wait_ge(sem["w2_loaded"], 16 * W2_LOADS)
            with at.loop(pe, NG) as g:
                xt()
                qk = []
                for w in (wq2, wk2):
                    for p6 in range(6):
                        k, p = claim(XBANKS)
                        qk.append(filled(product(p[:, 0:TG], two(w, p6 * 128, (p6 + 1) * 128)), k))
                v_moved = []
                for bb in range(GB):
                    for c in range(0, FF, 2 * D):
                        k, p = claim(OBANKS)
                        v_moved.append(filled(product(p[0:T, 0:2 * D], token_rows(XT, bb, wv2, c, c + 2 * D)), k))
                moved(*qk[-2:], *v_moved[-2:])
                attention(64, 2, 64, wo2)

            with at.loop(pe, NG) as g:
                xt()
                mlp(FT, wi2, lambda part: XT[:, part, :], wu2)
            with at.loop(pe, NG) as g:
                xt()
                qk = []
                for dst in range(4):
                    k, p = claim(XBANKS)
                    qk.append(filled(product(p[0:KD, 0:TG], two(wqkv3, dst * KD, (dst + 1) * KD)), k))
                v_moved = pairs(lambda bb: token_rows(XT, bb, wqkv3, 2 * D, 3 * D))
                moved(*qk[-2:])
                k, p = claim(SBANKS)
                for bb in range(GB):
                    last = product(p[0:T, cols(bb)], [(KT[0:KD, part, cols(bb)], QT[0:KD, part, cols(bb)])
                                                      for part in range(2)])
                moved(*v_moved, filled(last, k))
                pairs(lambda bb: [(PT[0][:, bb, :], V[:, bb * D:(bb + 1) * D])])

            router_inputs(rt3)
            pe.wait_ge(sem["router_ready"], at.take("router_ready"))
            w_moved = []
            for first in range(0, NB, 4):
                k, p = claim(TBANKS)
                for j in range(4):
                    last = pe.transpose(p[0:NE, cols(j)], E1[1][:, first + j, :], ident[0:T, 0:T])
                w_moved.append(filled(last, k))
            moved(*w_moved[-2:])
            for first in range(0, NB, 2):
                k, p = claim(OBANKS)
                for j in range(2):
                    last = pe.matmul(p[0:T, j * D:(j + 1) * D], WT8[:, first + j, :], bb2, start=True, stop=True)
                filled(last, k)
            experts(FT)


def laid_out(i):
    a = {k: np.asarray(v) for k, v in i.items()}
    rows = lambda v, n=T: np.ascontiguousarray(np.broadcast_to(v, (n,) + v.shape))
    per128 = lambda v: v.reshape(-1, 128).T
    side = 32
    n5 = 5
    frac = np.arange(0.0, 1.0 - 1e-06, 1.0 / n5, dtype=np.float32)
    bins = np.searchsorted(np.arange(1.0 / side, 1.0, 1.0 / side, dtype=np.float32), frac, side="right")
    pos_ids = (bins[:, None] * side + bins).reshape(-1)
    x = a["x"][:, :, :80, :80].reshape(NB, 3, n5, 16, n5, 16)
    patches = x.transpose(1, 3, 5, 0, 2, 4).reshape(KP // 128, 128, NB, NPATCH).transpose(1, 0, 2, 3)
    ids = np.zeros((T, NB), np.int32)
    ids[NPATCH:] = a["x_txt"].T
    qkv_b = a["L1_attn_qkv_b"]
    far = np.arange(T)[None, :] - np.arange(T)[:, None]
    decay = np.where(far >= 0, np.float32(0.99) ** far.astype(np.float32), np.float32(0)).astype(np.float32)
    tiled = lambda v: v.reshape(-1, 2, 2, HPU, 64).transpose(0, 1, 3, 2, 4).reshape(v.shape)
    in_rows = lambda v, p: v.reshape(v.shape[0], -1, p, v.shape[2]).transpose(0, 2, 1, 3)
    t = {
        "patchT": patches,
        "convT": a["L0_tok_conv_w"].reshape(D, KP).T.reshape(KP // 128, 128, D).transpose(1, 0, 2),
        "pos_rows": a["L0_tok_pos_table"][pos_ids], "conv_b": rows(a["L0_tok_conv_b"], NPATCH),
        "ids": ids, "words": a["L0_txt_token_embeddings"],
        "Wq": a["L0_attn_Wq"], "Wk": a["L0_attn_Wk"], "Wv": a["L0_attn_Wv"],
        "r_kernel": tiled(a["L0_attn_r_kernel"].reshape(D, FF)),
        "posT": a["L0_attn_position_embeds"][1:1 + NREL].T, "Wo": a["L0_attn_Wo"],
        "r_w_bias": per128(tiled(a["L0_attn_r_w_bias"].reshape(1, -1))), "r_r_bias": per128(tiled(a["L0_attn_r_r_bias"].reshape(1, -1))),
        "bk": per128(tiled(a["L0_attn_bk"][None])), "bv": rows(a["L0_attn_bv"]), "bo": rows(a["L0_attn_bo"]),
        "gamma": rows(a["L0_attn_gamma"]), "beta": rows(a["L0_attn_beta"]),
        "slots": a["L0_ffn_slots"], "slot_scale": a["L0_ffn_scale"][:, None],
        "norm_weight": rows(a["L0_ffn_norm_weight"]),
        "fc2_bias": a["L0_ffn_fc2_bias"].reshape(NSLOT, 2, KD).transpose(2, 1, 0),
        "fc1": np.concatenate([in_rows(a["L0_ffn_fc1_weight"], KD),
                               np.stack([a["L0_ffn_fc1_bias"], np.zeros((NSLOT, FF), np.float32)], 1)[:, None]], 1),
        "fc2": in_rows(a["L0_ffn_fc2_weight"], 128),
        "in_proj": a["L1_attn_in_proj_w"], "out_proj": a["L1_attn_out_proj_w"], "qkv1": a["L1_attn_qkv_w"],
        "proj1": a["L1_attn_attn_proj_w"], "ffn1": a["L1_attn_ffn1_w"], "ffn2": a["L1_attn_ffn2_w"],
        "conv1_w": a["L1_attn_conv_w"].reshape(CT3, 128, KCONV).transpose(1, 0, 2),
        "conv1_b": per128(a["L1_attn_conv_b"]),
        "ln_g": np.stack([a[f"L1_attn_ln{n}_g"].reshape(2, KD) for n in (1, 2, 3)]).transpose(2, 0, 1),
        "ln_b": np.stack([a[f"L1_attn_ln{n}_b"].reshape(2, KD) for n in (1, 2, 3)]).transpose(2, 0, 1),
        "qk1_b": qkv_b[:2 * D].reshape(2, UPB, HPU, 16).transpose(0, 1, 3, 2),
        "v1_b": rows(qkv_b[2 * D:]), "proj1_b": rows(a["L1_attn_attn_proj_b"]),
        "ffn1_b": per128(a["L1_attn_ffn1_b"]), "ffn2_b": rows(a["L1_attn_ffn2_b"]),
        "router1": a["L1_ffn_router_w"].T.reshape(2, KD, NE).transpose(1, 0, 2),
        "m1w1": in_rows(a["L1_ffn_w1"].transpose(0, 2, 1), KD), "m1w2": in_rows(a["L1_ffn_w2"].transpose(0, 2, 1), 128),
        "q2": tiled(a["L2_attn_w_q"]), "k2": tiled(a["L2_attn_w_k"]), "v2": a["L2_attn_w_v"], "o2": a["L2_attn_w_o"],
        "o2_b": rows(a["L2_attn_b_o"]), "in2": a["L2_ffn_in_weight"].T, "in2_b": per128(a["L2_ffn_in_bias"]),
        "up2": a["L2_ffn_out_weight"],
        "qkv3": a["L3_attn_W_qkv"], "qk3_b": a["L3_attn_b_qkv"][:2 * D].reshape(4, KD).T,
        "v3_b": rows(a["L3_attn_b_qkv"][2 * D:]), "decay": decay,
        "router3": a["L3_ffn_router_w"].T, "m3w1": in_rows(a["L3_ffn_w1"], KD), "m3w2": in_rows(a["L3_ffn_w2"], 128),
        "m3b1": a["L3_ffn_b1"].reshape(NE, FT, 128).transpose(2, 0, 1), "m3b2": a["L3_ffn_b2"],
    }
    return {k: np.ascontiguousarray(v) for k, v in t.items()}


def program(nc, shapes, notes):
    t = {name: nc.dram_tensor(f"in_{name}", shape, dt, kind="ExternalInput").ap()
         for name, (shape, dt) in shapes.items()}
    out = nc.dram_tensor("out_h", (T, NB, D), F32, kind="ExternalOutput").ap()
    row = HEADS * NREL
    scratch = nc.dram_tensor("pos_scratch", (NB, T, row), F32, kind="Internal").ap()
    flat = scratch.rearrange("b t n -> (b t n)")
    build(nc, t, out, scratch, flat, notes)


def kernel(**inputs):
    import concourse.bacc as _bacc
    from concourse.bass_utils import run_bass_kernel_spmd as _run

    t = laid_out(inputs)
    shapes = {k: (v.shape, mybir.dt.from_np(v.dtype)) for k, v in t.items()}
    notes = {}
    program(_bacc.Bacc("TRN2", target_bir_lowering=False, num_devices=1), shapes, notes)
    nc = _bacc.Bacc("TRN2", target_bir_lowering=False, num_devices=1)
    program(nc, shapes, notes)
    r = _run(nc, [{f"in_{k}": v for k, v in t.items()}], core_ids=[0])
    return np.ascontiguousarray(r.results[0]["out_h"].transpose(1, 0, 2))
```

```python
from contextlib import ExitStack, contextmanager

import numpy as np

import concourse.bass as bass
from concourse import mybir

F32 = mybir.dt.float32
F32R = mybir.dt.float32r
I32 = mybir.dt.int32
ACT = mybir.ActivationFunctionType
ALU = mybir.AluOpType
AX = mybir.AxisListType

NB = 16
T = 102
NPATCH = 25
D = 192
KD = 96
GB = 4
NG = NB // GB
TG = GB * T
HEADS = 12
HPU = 3
UPB = HEADS // HPU
TU = HPU * T
FF = 768
FT = FF // 128
NSLOT = 64
NE = 8
I1 = 512
INNER = 384
CT3 = INNER // 128
KCONV = 4
RING = 4
NREL = 2 * T - 1
VOCAB = 50257
KP = 768
EPS = 1e-5

POS_PAIRS = ((0, 1), (3, 4), (2, 6), (5, 9), (7, 8), (10, 11))

MARKS = tuple(range(8))

W0_LOADS = 16 * (12 + 3 + 7)
W1_LOADS = 6 + 8 + 8
W2_LOADS = 8 + 7

SBANKS, TBANKS, OBANKS, XBANKS, FBANKS = (0, 1), (2, 3), (4, 5), (6, 7), (2, 3, 6, 7)


class Count:

    def __init__(self, who, notes):
        self.who, self.notes = who, notes
        self.total, self.turn, self.per = {}, {}, {}
        self.i = None
        self.loops = 0
        self.turns_of_banks = {}

    def now(self, name):
        n = self.total.get(name, 0) + self.turn.get(name, 0)
        per = self.per.get(name, 0)
        return n + self.i * per if self.i is not None and per else n

    def one(self, name, by=1):
        self.turn[name] = self.turn.get(name, 0) + by
        return by

    def take(self, name, by=1):
        self.one(name, by)
        return self.now(name)

    def bank(self, banks):
        n = self.turns_of_banks.get(banks, 0)
        self.turns_of_banks[banks] = n + 1
        return banks[n % len(banks)]

    def first_banks(self):
        self.turns_of_banks = {}

    def _settle(self, times):
        for name, n in self.turn.items():
            self.total[name] = self.total.get(name, 0) + n * times
        self.turn, self.per, self.turns_of_banks = {}, {}, {}
        self.i = None

    @contextmanager
    def loop(self, engine, times):
        self._settle(1)
        key = (self.who, self.loops)
        self.loops += 1
        self.per = dict(self.notes.get(key, {}))
        with engine.Fori(0, times) as i:
            self.i = i
            yield i
            self.notes[key] = dict(self.turn)
        self._settle(times)


def build(nc, t, out, scratch, flat, notes):
    ctx = ExitStack()
    with ctx:
        def sb(name, shape, dt=F32):
            return ctx.enter_context(nc.sbuf_tensor(name, shape, dt))

        sem = {}

        def signal(*names):
            for name in names:
                sem[name] = ctx.enter_context(nc.semaphore(name))

        shapes = {"KT": [128, 6, TG],
                  "V": [T, GB * HEADS * 64],
                  "HT": [128, FT, TG],
                  **{f"W1_{r}": [KD + 1, 2, FF] for r in range(RING)},
                  **{f"W2_{r}": [128, FT, D] for r in range(RING)},
                  "SLOTS": [128, 2 * 2 * NSLOT * NB + NB * T],
                  "AREA": [128, 13620]}
        with ExitStack() as first:
            whole = {name: first.enter_context(nc.sbuf_tensor(name, shape, F32)) for name, shape in shapes.items()}
        rounded = {name: sb(f"{name}_R", shape, F32R) for name, shape in shapes.items()}
        KT, V, HT, SLOTS, AREA = (whole[n] for n in ("KT", "V", "HT", "SLOTS", "AREA"))
        W1B, W2 = ([whole[f"W{n}_{r}"] for r in range(RING)] for n in (1, 2))
        H = sb("H", [T, NB, D])
        XN = sb("XN", [T, GB, D])
        X1 = sb("X1", [T, GB, D])
        XT = sb("XT", [KD, 2, TG])
        QT = sb("QT", [128, 6, TG])
        PB = [sb(f"PB{j}", [T, 4, T]) for j in range(2)]
        PT = [sb(f"PT{j}", [T, 4, T]) for j in range(2)]
        ON = [sb(f"ON{j}", [T, FF]) for j in range(2)]
        OT = [sb(f"OT{j}", [128, 6, T]) for j in range(2)]
        W1 = [w[0:KD] for w in W1B]
        YT = SLOTS[0:KD, 0:2048].rearrange("p (k s b) -> p k s b", k=2, s=NSLOT)
        Y2T = SLOTS[0:KD, 2048:4096].rearrange("p (k s b) -> p k s b", k=2, s=NSLOT)
        XA = SLOTS[0:T, 0:NB * D].rearrange("p (b d) -> p b d", b=NB)
        CT = SLOTS[0:NSLOT, 4096:4096 + NB * T].rearrange("p (b t) -> p b t", b=NB)
        PB.append(ON[1][:, 0:4 * T].rearrange("p (h t) -> p h t", h=4))
        per_slot = lambda buf: buf[:].rearrange("p h t -> p (h t)")[:, 0:GB * NSLOT].rearrange(
            "p (b s) -> p b s", b=GB)
        LG4, CW, DW = per_slot(PT[0]), per_slot(PB[1]), per_slot(PT[1])
        DP = PB[0][0:NSLOT, :, :]
        Y2 = [ON[j][0:NSLOT, 0:D] for j in range(2)]
        flat_of = lambda buf, parts, c0, c1: buf[0:parts].rearrange("p k t -> p (k t)")[:, c0:c1]
        XS = flat_of(KT, KD + 1, 0, 2 * 128).rearrange("p (k s b) -> p k s b", k=2, s=RING)
        HR = flat_of(QT, 128, 0, FF)
        YR = flat_of(QT, 128, FF, FF + D)
        HS = HT[:, :, 0:128]
        by_k = lambda ap: ap.rearrange("p (k t) -> p k t", k=2)
        XALL_HR = by_k(rounded["SLOTS"][0:KD, 0:2 * NB * T])
        XALL_LR = by_k(rounded["AREA"][0:KD, 0:2 * NB * T])
        HT_HR, HT_LR = rounded["KT"], rounded["HT"]
        W1_HR = [by_k(rounded["V"][0:KD, j * 2 * FF:(j + 1) * 2 * FF]) for j in range(2)]
        W1_LR = [rounded[f"W1_{r}"][0:KD] for r in range(RING)]
        after = 2 * NB * T
        W2_HR = [rounded["SLOTS"][:, after + j * FT * D:after + (j + 1) * FT * D].rearrange(
            "p (f d) -> p f d", f=FT) for j in range(2)]
        W2_LR = [rounded[f"W2_{r}"] for r in range(RING)]
        XND = [XN, ON[0][:, 0:GB * D].rearrange("p (b d) -> p b d", b=GB)]
        SL, SL2 = ON[0][0:NSLOT, D:2 * D], ON[1][0:NSLOT, D:2 * D]
        ident = sb("ident", [128, 128])
        ones = sb("ones", [128, 128])
        marked = sb("marked", [1, 8])
        amarked = sb("amarked", [1, 8])
        expo = sb("expo", [128, 2, GB])
        ST = sb("ST", [T, GB, 6])
        MV = sb("MV", [T, GB, 2])
        VE = sb("VE", [T, GB])
        RS = sb("RS", [T, GB])
        MX = sb("MX", [T, GB])
        SM = sb("SM", [T, GB])
        RC = sb("RC", [T, GB])
        TS = [sb(f"TS{j}", [T, GB]) for j in range(2)]
        NMU, SMU, RCU = (sb(name, [T, 3, GB]) for name in ("NMU", "SMU", "RCU"))
        IDS = sb("IDS", [T - NPATCH, NB], I32)
        LG = sb("LG", [T, NB, NE])
        E1 = [QT[0:T, j, 0:NB * NE].rearrange("p (b e) -> p b e", b=NB) for j in range(6)]
        E2 = [sb(f"E2_{j}", [T, NB]) for j in range(3)]
        RUN = sb("RUN", [T, NE])
        ORDER = sb("ORDER", [T, NB, NE])
        WT8 = KT[0:NE, 0:4, :].rearrange("p k (b t) -> p (k b) t", b=4)


        def area():
            at = [0]

            def piece(parts, *shape):
                n = int(np.prod(shape))
                ap = AREA[0:parts, at[0]:at[0] + n]
                at[0] += n
                assert at[0] <= 13620
                if len(shape) == 2:
                    ap = ap.rearrange("p (a b) -> p a b", a=shape[0])
                elif len(shape) == 3:
                    ap = ap.rearrange("p (a b c) -> p a b c", a=shape[0], b=shape[1])
                return ap
            return piece

        a0 = area()
        wq0, wk0, wv0 = a0(KD, 2, 384), a0(KD, 2, 384), a0(KD, 2, KD)
        rker, posT, RT = a0(KD, 2, FF), a0(KD, 2, NREL), a0(128, 6, NREL)
        wo0 = a0(128, 3, D)
        rw0, rr0, bk0 = a0(128, 6), a0(128, 6), a0(128, 6)
        bv0, bo0, gamma0, beta0 = a0(T, D), a0(T, D), a0(T, D), a0(T, D)
        QR = a0(128, 6, TG)
        PR = a0(T, HEADS, NREL)
        POS = [a0(T, HEADS, T) for _ in range(2)]
        patchT = HT[:, :, 0:NB * NPATCH].rearrange("p k (b n) -> p k b n", b=NB)
        convT = KT[:, :, 0:D]
        posE = ON[0][0:NPATCH, 2 * D:4 * D].rearrange("p (a d) -> p a d", a=2)
        slS = sb("slS", [NSLOT, 1])
        slT = sb("slT", [KD, 2, NSLOT])
        nw0 = sb("nw0", [T, D])
        fb2 = sb("fb2", [KD, 2, NSLOT])

        a1 = area()
        XALL = a1(KD, 2, NB * T)
        win1, wout1 = a1(KD, 2, 2 * INNER), a1(128, CT3, D)
        cw1, cb1 = a1(128, CT3, KCONV), a1(128, CT3)
        g1 = a1(KD, 3, 2)
        b1 = a1(KD, 3, 2)
        wqkv1, wqk1 = a1(KD, 2, 3 * D), a1(KD, 2, 2 * 384)
        bqk1, bv1 = a1(128, 6), a1(T, D)
        wp1, bp1 = a1(128, 3, D), a1(T, D)
        wf1, bf1, wf2, bf2 = a1(KD, 2, FF), a1(128, FT), a1(128, FT, D), a1(T, D)
        rt1 = sb("rt1", [KD, 2, NE])

        a2 = area()
        a2(KD, 2, NB * T)
        wq2, wk2, wv2 = a2(KD, 2, FF), a2(KD, 2, FF), a2(KD, 2, FF)
        wo2, bo2 = a2(128, 6, D), a2(T, D)
        wi2, bi2, wu2 = a2(KD, 2, FF), a2(128, FT), a2(128, FT, D)
        wqkv3, bqk3, bv3 = a2(KD, 2, 3 * D), a2(KD, 4), a2(T, D)
        decay = a2(T, T)
        rt3, bb1, bb2 = a2(KD, 2, NE), a2(128, NE, FT), a2(NE, D)

        psum = [ctx.enter_context(nc.psum_tensor(f"bank{k}", [128, 512], F32)) for k in range(8)]

        for k in range(8):
            signal(f"bank_full{k}", f"bank_free{k}")
        for r in range(RING):
            signal(f"w1_loaded{r}", f"w1_used{r}", f"w2_loaded{r}", f"w2_used{r}")
        signal("patches_loaded", "ids_loaded", "words_loaded", "w0_loaded", "w1_loaded", "w2_loaded",
               "slots_loaded",
               "constants_ready", "area_cleared", "w0_cleared", "padded",
               "vector_step", "pool_step",
               "vector_passed", "tensor_passed",
               "power_in", "power_out",
               "xn_ready", "xn_taken",
               "xt_ready",
               "xt_copied",
               "scores_ready",
               "probs_in", "probs_ready",
               "sums_ready",
               "exp_ready",
               "pr_ready", "pr_stored", "pos_loaded0", "pos_loaded1", "pos_used",
               "conv_ready", "gate_ready", "gated",
               "slot_in", "yt_ready",
               "slot_rows",
               "w1_split", "w2_split",
               "hidden_ready", "hidden_split",

               "attn0_done", "attn1_done",
               "router_ready", "out_ready", "out_stored")

        block = ctx.enter_context(nc.Block())

        def head(buf, h, per_tile, dk, cols):
            unit, j = h // HPU, h % HPU
            p = (unit % per_tile) * (128 // per_tile)
            return buf[p:p + dk, (unit // per_tile) * HPU + j, cols]

        def cols(bb):
            return slice(bb * T, (bb + 1) * T)

        UNITS = GB * UPB
        STEPS = UNITS + 5
        AVBANK, PROJBANK = OBANKS

        def av_place(dv, h):
            if dv == 16:
                return 32 * (h % 4), 32, h // 4, 0
            return 64 * (h % 2), 64, h // 2 % 3, h // 6

        def av_filled(dv, unit):
            return unit % (UPB if dv == 16 else UPB // 2) == (UPB if dv == 16 else UPB // 2) - 1

        def by_head(dv):
            width = 32 if dv == 16 else dv
            return V[:, 0:GB * HEADS * width].rearrange("p (h d) -> p h d", d=width)

        def last_of(step):
            return step // UPB if 0 <= step < UNITS and step % UPB == UPB - 1 else None

        @block.sync
        def _(sp):
            at = Count("sp", notes)

            def load(dst, src, name):
                sp.dma_start(dst, src).then_inc(sem[name], at.one(name, 16))

            sp.sem_inc(sem["pr_stored"], at.one("pr_stored", 16))
            at.one("pos_used")

            load(patchT, t["patchT"], "patches_loaded")
            load(convT, t["convT"], "patches_loaded")
            load(posE[:, 0, :], t["pos_rows"], "patches_loaded")
            load(posE[:, 1, :], t["conv_b"], "patches_loaded")
            sp.wait_ge(sem["w0_cleared"], 3)
            for g in range(4):
                rows = slice((g % 2) * 48, (g % 2) * 48 + 48)
                for w, name in ((wq0, "Wq"), (wk0, "Wk")):
                    tiles = w[rows, g // 2, :].rearrange("p (j two d) -> p j two d", j=HPU, two=2)
                    load(tiles[:, :, g % 2, :], t[name][g].rearrange("i (j d) -> i j d", j=HPU), "w0_loaded")
                load(wv0[rows, g // 2, (g % 2) * 48:(g % 2) * 48 + 48], t["Wv"][g], "w0_loaded")
            load(rker, t["r_kernel"].rearrange("(k p) n -> p k n", p=KD), "w0_loaded")
            load(posT, t["posT"].rearrange("(k p) n -> p k n", p=KD), "w0_loaded")
            load(wo0, t["Wo"], "w0_loaded")
            for dst, name in ((rw0, "r_w_bias"), (rr0, "r_r_bias"), (bk0, "bk"), (bv0, "bv"), (bo0, "bo"),
                              (gamma0, "gamma"), (beta0, "beta")):
                load(dst, t[name], "w0_loaded")
            for dst, name in ((SL, "slots"), (slS, "slot_scale"), (nw0, "norm_weight"), (fb2, "fc2_bias"), (rt1, "router1")):
                load(dst if name == "slots" else dst[:], t[name], "slots_loaded")

            def fill_w1(r, w1, rounds=1):
                sp.wait_ge(sem[f"w1_used{r}"], at.now(f"w1_used{r}"))
                at.one(f"w1_used{r}", rounds)
                sp.dma_start(W1B[r][0:w1.shape[0], :, 0:w1.shape[2]], w1).then_inc(sem[f"w1_loaded{r}"], 16)

            def fill_w2(r, w2):
                sp.wait_ge(sem[f"w2_used{r}"], at.now(f"w2_used{r}"))
                at.one(f"w2_used{r}")
                sp.dma_start(W2[r][:, 0:w2.shape[1], :], w2).then_inc(sem[f"w2_loaded{r}"], 16)

            def fill(r, w1, w2):
                fill_w1(r, w1, NG)
                fill_w2(r, w2)

            def fill_slots(first):
                for r in range(RING):
                    fill_w1(r, t["fc1"][bass.ds(first + r, 1)].rearrange("o p k f -> (o p) k f"))
                for r in range(RING):
                    fill_w2(r, t["fc2"][bass.ds(first + r, 1)].rearrange("o p k f -> (o p) k f"))

            fill_slots(0)

            with at.loop(sp, NG) as g:
                for bb in range(GB):
                    here = scratch[bass.ds(g * GB + bb, 1)].rearrange("o t n -> (o t) n")
                    sp.wait_ge(sem["pr_ready"], at.take("pr_ready"))
                    sp.dma_start(here, PR.rearrange("p h n -> p (h n)")
                                 ).then_inc(sem["pr_stored"], at.one("pr_stored", 16))
                    sp.wait_ge(sem["pr_stored"], at.now("pr_stored"))
                    if bb < 2:
                        sp.wait_ge(sem["pos_used"], at.now("pos_used"))
                    else:
                        sp.wait_ge(sem["pos_used"], at.take("pos_used"))
                    row = HEADS * NREL
                    shifted = bass.AP(tensor=flat.tensor, offset=(g * GB + bb) * (T * row) + (T - 1),
                                      ap=[[row - 1, T], [NREL, HEADS], [1, T]])
                    sp.dma_start(POS[bb % 2], shifted).then_inc(sem[f"pos_loaded{bb % 2}"], 16)
                for _ in range(2):
                    at.one("pos_used")

            def load_area(pieces, name):
                for dst, src, p in pieces:
                    load(dst, t[src].rearrange("(k p) n -> p k n", p=p) if p else t[src], name)

            sp.wait_ge(sem["attn0_done"], 1)
            sp.wait_ge(sem["area_cleared"], 1)
            load_area(((win1, "in_proj", KD), (wout1, "out_proj", 128), (wqkv1, "qkv1", KD), (wp1, "proj1", 0),
                       (wf1, "ffn1", KD), (wf2, "ffn2", 128), (cw1, "conv1_w", 0), (cb1, "conv1_b", 0),
                       (g1, "ln_g", 0), (b1, "ln_b", 0), (bv1, "v1_b", 0), (bp1, "proj1_b", 0),
                       (bf1, "ffn1_b", 0), (bf2, "ffn2_b", 0)), "w1_loaded")
            for q in range(2):
                for u in range(UPB):
                    load(bqk1[32 * u:32 * u + 16, 3 * q:3 * q + 3], t["qk1_b"][q, u], "w1_loaded")

            with at.loop(sp, NSLOT // RING - 1) as j:
                fill_slots(j * RING + RING)
            for e in range(NE):
                if e == RING:
                    sp.wait_ge(sem["attn1_done"], 1)
                    load_area(((wq2, "q2", KD), (wk2, "k2", KD), (wv2, "v2", KD), (wo2, "o2", 128),
                               (wi2, "in2", KD), (wu2, "up2", 128), (wqkv3, "qkv3", KD), (rt3, "router3", KD),
                               (bo2, "o2_b", 0), (bi2, "in2_b", 0), (bqk3, "qk3_b", 0), (bv3, "v3_b", 0),
                               (decay, "decay", 0), (bb1, "m3b1", 0), (bb2, "m3b2", 0)), "w2_loaded")
                fill(e % RING, t["m1w1"][e], t["m1w2"][e])
            for e in range(NE):
                fill(e % RING, t["m3w1"][e], t["m3w2"][e])

            with at.loop(sp, NG) as g:
                sp.wait_ge(sem["out_ready"], at.take("out_ready"))
                sp.dma_start(out[:, bass.ds(g * GB, GB), :], H[:, bass.ds(g * GB, GB), :]
                             ).then_inc(sem["out_stored"], at.one("out_stored", 16))
            sp.wait_ge(sem["out_stored"], 16 * NG)

        @block.gpsimd
        def _(pool):
            at = Count("pool", notes)

            def step(ins):
                ins.then_inc(sem["pool_step"], at.one("pool_step"))
                pool.wait_ge(sem["pool_step"], at.now("pool_step"))

            pool.dma_start(IDS[:], t["ids"]).then_inc(sem["ids_loaded"], 16)
            for w in (wq0, wk0, wv0):
                pool.memset(w, 0.0).then_inc(sem["w0_cleared"], 1)
            step(pool.memset(ident[:], 0.0))
            step(pool.affine_select(out=ident[:], in_=ident[:], compare_op=ALU.not_equal, fill=1.0, base=0,
                                    pattern=[[-1, 128]], channel_multiplier=1))
            pool.memset(ones[:], 1.0)
            pool.memset(expo[:, 0, :], -0.5)
            pool.memset(expo[:, 1, :], 0.5)
            pool.memset(H[:], 0.0).then_inc(sem["constants_ready"], 1)
            pool.wait_ge(sem["constants_ready"], 1)
            pool.wait_ge(sem["ids_loaded"], 16)
            for b in range(NB):
                pool.indirect_dma_start(H[NPATCH:, b, :], None, t["words"],
                                        bass.IndirectOffsetOnAxis(ap=IDS[:, b:b + 1], axis=0),
                                        bounds_check=VOCAB - 1, oob_is_err=False
                                        ).then_inc(sem["words_loaded"], 16)
            pool.memset(V[:], 0.0)
            for e in range(NE):
                last = pool.memset(ORDER[:, :, e:e + 1], float(NE - e))
            last.then_inc(sem["constants_ready"], 1)

            def power(half, rows=T, width=GB):
                pool.wait_ge(sem["power_in"], at.take("power_in"))
                pool.tensor_tensor(RS[0:rows, 0:width], VE[0:rows, 0:width], expo[0:rows, half, 0:width],
                                   ALU.pow).then_inc(sem["power_out"], at.one("power_out"))

            power(1, NSLOT, 1)
            def powers(n):
                for _ in range(n):
                    power(0)

            def probabilities():
                for n in range(UNITS):
                    pool.wait_ge(sem["sums_ready"], at.take("sums_ready"))
                    p = PB[n % 3][:, 0:HPU, :]
                    scale = RCU[:, n % 3, 0:HPU].unsqueeze(2).to_broadcast([T, HPU, T])
                    pool.tensor_tensor(p, p, scale, ALU.mult).then_inc(sem["probs_ready"], 1)

            def dispatch_powers():
                power(0)
                power(1)

            powers(1)
            with at.loop(pool, NG - 1):
                powers(1)
                probabilities()
                powers(1)
            dispatch_powers()
            probabilities()
            powers(1)

            pool.wait_ge(sem["attn0_done"], 1)
            pool.memset(bqk1, 0.0).then_inc(sem["area_cleared"], 1)
            pool.wait_ge(sem["area_cleared"], 1)
            step(pool.memset(XS[0:KD], 0.0))
            step(pool.memset(XS[KD:KD + 1], 1.0))
            with at.loop(pool, NG - 1):
                dispatch_powers()
            pool.wait_ge(sem["yt_ready"], 1 + NG)
            with at.loop(pool, NSLOT // RING) as j:
                for r in range(RING):
                    pool.wait_ge(sem[f"w1_used{r}"], at.now(f"w1_used{r}"))
                    at.one(f"w1_used{r}")
                pool.tensor_copy(XS[0:KD, :, :, 0:NB], YT[:, :, bass.ds(j * RING, RING), :]
                                 ).then_inc(sem["slot_rows"], at.one("slot_rows"))
            step(pool.memset(wqk1, 0.0))
            pool.wait_ge(sem["w1_loaded"], 16 * W1_LOADS)
            for k in range(2):
                for q in range(2):
                    dst = wqk1[:, k, q * 384:(q + 1) * 384].rearrange("p (j u d) -> p u j d", j=HPU, d=32)
                    src = wqkv1[:, k, q * D:(q + 1) * D].rearrange("p (u j d) -> p u j d", j=HPU, d=16)
                    last = pool.tensor_copy(dst[:, :, :, 0:16], src)
            last.then_inc(sem["padded"], 1)

            def gate(place):
                for c in range(CT3):
                    pool.wait_ge(sem["gate_ready"], at.take("gate_ready"))
                    pool.tensor_tensor(QT[:, CT3 * place + c, :], HT[:, c, :], HT[:, 3 + c, :], ALU.mult
                                       ).then_inc(sem["gated"], at.one("gated"))

            pool.sem_inc(sem["gated"], CT3)
            powers(4)
            gate(0)
            with at.loop(pool, (NG - 2) // 2):
                for place in (1, 0):
                    powers(2)
                    gate(place)
            gate((NG - 1) % 2)
            powers(1)
            def attention_inputs():
                with at.loop(pool, NG - 1):
                    powers(1)
                    probabilities()
                powers(1)
                probabilities()

            def used(e):
                pool.wait_ge(sem[f"w1_used{e % RING}"], at.take(f"w1_used{e % RING}", NG))
                pool.wait_ge(sem[f"w2_used{e % RING}"], at.take(f"w2_used{e % RING}"))

            def split(name, e, cols):
                r, j = e % RING, e % 2
                c = (slice(None), slice(None), slice(0, cols)) if name == "w1" else (slice(None), slice(0, cols))
                src, high, low = (W1[r], W1_HR[j], W1_LR[r]) if name == "w1" else (W2[r], W2_HR[j], W2_LR[r])
                pool.wait_ge(sem[f"{name}_loaded{r}"], at.take(f"{name}_loaded{r}", 16))
                step(pool.tensor_copy(high[c], src[c]))
                pool.tensor_tensor(low[c], src[c], high[c], ALU.subtract
                                   ).then_inc(sem[f"{name}_split"], at.one(f"{name}_split"))

            def split_early(tiles):
                for e in range(2):
                    split("w2", e, tiles)

            def split_weights(w1_cols, tiles):
                for e in range(2):
                    split("w1", e, w1_cols)
                for e in range(2, NE):
                    used(e - 2)
                    split("w1", e, w1_cols)
                    split("w2", e, tiles)
                used(NE - 2)
                used(NE - 1)

            for r in range(RING):
                for name in ("w1_loaded", "w2_loaded"):
                    at.one(f"{name}{r}", 16 * (NSLOT // RING))
                at.one(f"w2_used{r}", NSLOT // RING)
            attention_inputs()
            split_early(I1 // 128)
            with at.loop(pool, NG - 1):
                powers(1)

            def router_copies():
                def copy(g):
                    pool.wait_ge(sem["xt_ready"], at.take("xt_ready"))
                    here = (slice(None), slice(None), bass.ds(g * TG, TG))
                    pool.tensor_tensor(XALL_LR[here], XT[:], XALL_HR[here], ALU.subtract
                                       ).then_inc(sem["xt_copied"], at.one("xt_copied"))
                powers(1)
                with at.loop(pool, NG - 1) as g:
                    powers(1)
                    copy(g)
                copy(NG - 1)

            router_copies()
            split_weights(I1, I1 // 128)
            powers(1)
            attention_inputs()
            split_early(FT)
            with at.loop(pool, 2 * NG - 1):
                powers(1)
            router_copies()
            split_weights(FF, FT)

        @block.vector
        def _(dve):
            at = Count("dve", notes)
            at.one("yt_ready")
            tt, ts, stt = dve.tensor_tensor, dve.tensor_scalar, dve.scalar_tensor_tensor

            def step(ins):
                ins.then_inc(sem["vector_step"], at.one("vector_step"))
                dve.wait_ge(sem["vector_step"], at.now("vector_step"))

            def give(ins, name):
                ins.then_inc(sem[name], at.one(name))

            def full(k):
                dve.wait_ge(sem[f"bank_full{k}"], at.take(f"bank_full{k}"))
                return psum[k]

            def mark(name):
                n = at.bank(MARKS)
                give(dve.memset(marked[:, n:n + 1], 0.0), name)

            def free(ins, k):
                ins.then_inc(sem[f"bank_free{k}"], at.one(f"bank_free{k}"))
                dve.wait_ge(sem[f"bank_free{k}"], at.now(f"bank_free{k}"))

            def power(ins):
                give(ins, "power_in")
                dve.wait_ge(sem["power_out"], at.take("power_out"))

            def wide(ap, n):
                return ap.unsqueeze(2).to_broadcast([ap.shape[0], ap.shape[1], n])

            def statistics(src):
                dve.sem_inc(sem["vector_passed"], 1)
                for bb in range(GB):
                    last = dve.bn_stats(ST[:, bb, :], src(bb))
                step(last)
                dve.sem_inc(sem["vector_passed"], 1)
                for bb in range(GB):
                    last = dve.bn_aggr(MV[:, bb, :], ST[:, bb, :])
                step(last)

            def layernorm(src, dst, eps=EPS, name=None):
                statistics(src)
                power(ts(VE[:], MV[:, :, 1], eps, None, ALU.add))
                if name:
                    dve.wait_ge(sem["xn_taken"], at.now(name))
                for bb in range(GB):
                    last = ts(dst(bb), src(bb), MV[:, bb, 0:1], RS[:, bb:bb + 1], ALU.subtract, ALU.mult)
                if name:
                    give(last, name)
                    dve.wait_ge(sem[name], at.now(name))
                else:
                    step(last)

            xn = lambda bb: XN[:, bb, :]
            x1 = lambda bb: X1[:, bb, :]

            def group(buf, g):
                return buf[:, bass.ds(g * GB, GB), :]

            def spread(v):
                return v.unsqueeze(1).to_broadcast([T, GB, D])

            def in_turns(prepare, consume, then):
                with at.loop(dve, NG - 1) as g:
                    prepare(g + 1)
                    consume(g)
                then()
                consume(NG - 1)
                at.first_banks()

            def a_of(g):
                return lambda bb: XA[:, bass.ds(g * GB + bb, 1), :].rearrange("p o d -> p (o d)")

            def h_of(g):
                return lambda bb: H[:, bass.ds(g * GB + bb, 1), :].rearrange("p o d -> p (o d)")

            def maxima(n, pos, scale):
                k = at.bank(SBANKS)
                dve.wait_ge(sem["scores_ready"], at.take("scores_ready"))
                scores = psum[k][0:T, 0:TU].rearrange("p (h t) -> p h t", h=HPU)
                bb, unit = n // UPB, n % UPB
                if pos:
                    if unit == 0:
                        dve.wait_ge(sem[f"pos_loaded{bb % 2}"], at.take(f"pos_loaded{bb % 2}", 16))
                    p = PB[n % 3][:, 0:HPU, :]
                    ins = tt(p, scores, POS[bb % 2][:, HPU * unit:HPU * unit + HPU, :], ALU.add)
                    if unit == UPB - 1:
                        give(ins, "pos_used")
                        dve.wait_ge(sem["pos_used"], at.now("pos_used"))
                    else:
                        step(ins)
                    scores = p
                step(dve.tensor_reduce(MX[:, 0:HPU], scores, AX.X, ALU.max))
                give(ts(NMU[:, n % 3, 0:HPU], MX[:, 0:HPU], -scale, None, ALU.mult), "probs_in")
                dve.wait_ge(sem["probs_in"], at.now("probs_in"))

            def inverse_sums(n):
                dve.wait_ge(sem["exp_ready"], at.take("exp_ready"))
                give(dve.reciprocal(RCU[:, n % 3, 0:HPU], SMU[:, n % 3, 0:HPU]), "sums_ready")
                dve.wait_ge(sem["sums_ready"], at.now("sums_ready"))

            def attention(dv, pos, scale, finish):
                for s in range(STEPS):
                    n = s - 4
                    if 0 <= n < UNITS and av_filled(dv, n % UPB):
                        tile = 3 * av_place(dv, HPU * (n % UPB))[3]
                        src = full(AVBANK)[:, 0:3 * T].rearrange("p (k t) -> p k t", k=3)
                        free(dve.tensor_copy(OT[n // UPB % 2][:, tile:tile + 3, :], src), AVBANK)
                    if last_of(s - 5) is not None:
                        finish(last_of(s - 5), full(PROJBANK)[0:T, 0:D], PROJBANK)
                    if s < UNITS:
                        maxima(s, pos, scale)
                    if 0 <= s - 1 < UNITS:
                        inverse_sums(s - 1)

            def values(v, dv, bias):
                per = 2 * D // dv
                v5 = by_head(dv)
                for first in range(0, GB * HEADS, per):
                    k = at.bank(OBANKS)
                    src = full(k)[0:T, 0:per * dv].rearrange("p (h d) -> p h d", d=dv)
                    if bias is None:
                        last = dve.tensor_copy(v5[:, first:first + per, 0:dv], src)
                    else:
                        for j in range(per // HEADS):
                            last = tt(v5[:, first + j * HEADS:first + (j + 1) * HEADS, 0:dv],
                                      src[:, j * HEADS:(j + 1) * HEADS, :],
                                      bias.rearrange("p (h d) -> p h d", d=dv), ALU.add)
                    free(last, k)

            def pairs(consume):
                for first in range(0, GB, 2):
                    k = at.bank(OBANKS)
                    o = full(k)
                    last = None
                    for bb in (first, first + 1):
                        last = consume(bb, o[0:T, (bb - first) * D:(bb - first + 1) * D])
                    free(last, k)

            for k in SBANKS + OBANKS:
                dve.sem_inc(sem[f"bank_free{k}"], at.one(f"bank_free{k}"))
            dve.sem_inc(sem["pos_used"], at.one("pos_used"))

            def unit_slots():
                dve.wait_ge(sem["slots_loaded"], 16 * 5)
                step(dve.tensor_tensor_reduce(out=SL2, in0=SL, in1=SL, scale=1.0, scalar=0.0,
                                              op0=ALU.mult, op1=ALU.add, accum_out=SM[0:NSLOT, 0:1]))
                power(ts(VE[0:NSLOT, 0:1], SM[0:NSLOT, 0:1], 1.0, None, ALU.mult))
                step(ts(MX[0:NSLOT, 0:1], RS[0:NSLOT, 0:1], EPS, None, ALU.max))
                step(dve.reciprocal(RC[0:NSLOT, 0:1], MX[0:NSLOT, 0:1]))
                give(ts(SL2, SL, RC[0:NSLOT, 0:1], slS[:, 0:1], ALU.mult, ALU.mult), "xn_ready")

            dve.wait_ge(sem["patches_loaded"], 64)
            dve.wait_ge(sem["constants_ready"], 1)
            step(tt(posE[:, 0, :], posE[:, 0, :], posE[:, 1, :], ALU.add))
            for first in range(0, NB, 2):
                if first == 10:
                    unit_slots()
                k = at.bank(OBANKS)
                o = full(k)[0:NPATCH, 0:2 * D].rearrange("p (b d) -> p b d", b=2)
                for j in range(2):
                    last = tt(H[0:NPATCH, first + j, :], o[:, j, :], posE[:, 0, :], ALU.add)
                free(last, k)

            def prepare_d(g, par):
                statistics(h_of(g))
                power(ts(VE[:], MV[:, :, 1], 1.0 + EPS, EPS * EPS, ALU.mult, ALU.add))
                if isinstance(g, int) and g == 0:
                    dve.wait_ge(sem["xn_taken"], at.now("xn_ready"))
                else:
                    dve.wait_ge(sem["yt_ready"], at.now("yt_ready"))
                    at.one("yt_ready")
                x, ts_inv = XND[par], TS[par]
                for bb in range(GB):
                    last = ts(X1[:, bb, :], h_of(g)(bb), MV[:, bb, 0:1], RS[:, bb:bb + 1], ALU.subtract, ALU.mult)
                step(last)
                give(tt(x[:], X1[:], spread(nw0[:]), ALU.mult), "xn_ready")
                dve.wait_ge(sem["xn_ready"], at.now("xn_ready"))
                for bb in range(GB):
                    last = dve.tensor_tensor_reduce(out=X1[:, bb, :], in0=x[:, bb, :], in1=x[:, bb, :],
                                                    scale=1.0, scalar=0.0, op0=ALU.mult, op1=ALU.add,
                                                    accum_out=SM[:, bb:bb + 1])
                step(last)
                power(ts(VE[:], SM[:], 1.0, None, ALU.mult))
                step(ts(ts_inv[:], RS[:], EPS, None, ALU.max))
                step(dve.reciprocal(ts_inv[:], ts_inv[:]))

            dve.wait_ge(sem["w0_loaded"], W0_LOADS)
            def prepare_a0(g):
                layernorm(h_of(g), xn, name="xn_ready")
                step(tt(group(XA, g), XN[:], spread(bo0), ALU.add))

            def attend_0(g):
                values(V, 16, bv0)
                attention(16, True, 0.125, lambda bb, o, k: free(tt(a_of(g)(bb), o, a_of(g)(bb), ALU.add), k))
                layernorm(a_of(g), a_of(g), eps=1e-9)
                step(tt(group(XA, g), group(XA, g), spread(gamma0), ALU.mult))
                step(tt(group(XA, g), group(XA, g), spread(beta0), ALU.add))
                step(tt(group(H, g), group(H, g), group(XA, g), ALU.add))

            dve.wait_ge(sem["words_loaded"], 16 * NB)
            dve.wait_ge(sem["constants_ready"], 2)
            prepare_a0(0)
            in_turns(prepare_a0, attend_0, lambda: prepare_d(0, 0))
            mark("attn0_done")

            def dispatch(par):
                k = at.bank(OBANKS)
                o = full(k)[0:T, 0:GB * NSLOT].rearrange("p (b s) -> p b s", b=GB)
                free(tt(LG4, o, wide(TS[par][:], NSLOT), ALU.mult), k)
                give(dve.tensor_reduce(MX[:], LG4, AX.X, ALU.max), "slot_in")
                dve.wait_ge(sem["slot_in"], at.now("slot_in"))
                give(tt(CW, LG4, wide(MX[:], NSLOT), ALU.subtract), "probs_in")
                dve.wait_ge(sem["probs_in"], at.now("probs_in"))
                k = at.bank(SBANKS)
                dve.wait_ge(sem["scores_ready"], at.take("scores_ready"))
                o = psum[k][0:NSLOT, 0:TG].rearrange("p (b t) -> p b t", b=GB)
                step(dve.tensor_reduce(MX[0:NSLOT, :], o, AX.X, ALU.max))
                give(tt(DP, o, wide(MX[0:NSLOT, :], T), ALU.subtract), "probs_in")
                dve.wait_ge(sem["exp_ready"], at.take("exp_ready"))
                step(dve.tensor_reduce(SM[:], CW, AX.X, ALU.add))
                step(dve.reciprocal(RC[:], SM[:]))
                give(tt(CW, CW, wide(RC[:], NSLOT), ALU.mult), "slot_in")
                dve.wait_ge(sem["exp_ready"], at.take("exp_ready"))
                step(dve.tensor_reduce(SM[0:NSLOT, :], DP, AX.X, ALU.add))
                step(dve.reciprocal(RC[0:NSLOT, :], SM[0:NSLOT, :]))
                give(tt(DP, DP, wide(RC[0:NSLOT, :], T), ALU.mult), "slot_in")

            with at.loop(dve, NG // 2 - 1) as i:
                for par in range(2):
                    prepare_d(2 * i + par + 1, 1 - par)
                    dispatch(par)
            prepare_d(NG - 1, 1)
            dispatch(0)
            dispatch(1)

            with at.loop(dve, NSLOT // RING) as j:
                for half in range(2):
                    k = at.bank(SBANKS)
                    src = full(k)[:, 0:3 * 128].rearrange("p (f c) -> p f c", f=3)
                    free(dve.tensor_copy(HS[:, 3 * half:3 * half + 3, :], src), k)
                k = at.bank(OBANKS)
                free(dve.tensor_copy(YR, full(k)[:, 0:D]), k)
                k = at.bank(OBANKS)
                o = full(k)[0:KD, 0:2 * 128].rearrange("p (m s b) -> p m s b", m=2, s=RING)
                for m in range(2):
                    s = bass.ds(j * RING, RING)
                    last = tt(Y2T[:, m, s, :], o[:, m, :, 0:NB], wide(fb2[:, m, s], NB), ALU.add)
                free(last, k)

            for first in range(0, NB, 2):
                k = at.bank(OBANKS)
                o = full(k)[0:T, 0:2 * D].rearrange("p (b d) -> p b d", b=2)
                free(tt(H[:, first:first + 2, :], H[:, first:first + 2, :], o, ALU.add), k)

            dve.wait_ge(sem["padded"], 1)
            def prepare_c1(g):
                layernorm(h_of(g), a_of(g))
                power(ts(VE[:], MV[:, :, 1], 1.0 + EPS, EPS * EPS, ALU.mult, ALU.add))
                dve.wait_ge(sem["xn_taken"], at.now("xn_ready"))
                for bb in range(GB):
                    last = ts(xn(bb), h_of(g)(bb), MV[:, bb, 0:1], RS[:, bb:bb + 1], ALU.subtract, ALU.mult)
                give(last, "xn_ready")
                dve.wait_ge(sem["xn_ready"], at.now("xn_ready"))

            def convolve(g):
                for c in range(CT3):
                    dve.wait_ge(sem["gated"], at.take("gated"))
                    k = at.bank(SBANKS)
                    src = full(k)[:, 0:TG].rearrange("p (b t) -> p b t", b=GB)
                    y = HT[:, c, :].rearrange("p (b t) -> p b t", b=GB)
                    step(ts(y, src, cw1[:, c, 3:4], cb1[:, c:c + 1], ALU.mult, ALU.add))
                    for lag in (1, 2):
                        step(stt(y[:, :, lag:], src[:, :, :T - lag], cw1[:, c, 3 - lag:4 - lag],
                                 y[:, :, lag:], ALU.mult, ALU.add))
                    give(stt(y[:, :, 3:], src[:, :, :T - 3], cw1[:, c, 0:1], y[:, :, 3:],
                             ALU.mult, ALU.add), "conv_ready")
                    mark(f"bank_free{k}")

            def convolved(g):
                pairs(lambda bb, o: tt(a_of(g)(bb), a_of(g)(bb), o, ALU.add))

            def prepare_a1(g):
                layernorm(a_of(g), xn, name="xn_ready")
                step(tt(group(XA, g), group(XA, g), spread(bp1), ALU.add))

            def attend_1(g):
                values(V, 16, bv1)
                attention(16, False, 0.25, lambda bb, o, k: free(tt(a_of(g)(bb), a_of(g)(bb), o, ALU.add), k))

            def prepare_f1(g):
                layernorm(a_of(g), xn, name="xn_ready")
                step(tt(group(XA, g), group(XA, g), spread(bf2), ALU.add))

            def mlp_1(g):
                pairs(lambda bb, o: tt(a_of(g)(bb), a_of(g)(bb), o, ALU.add))
                step(tt(group(H, g), group(H, g), group(XA, g), ALU.add))

            def prepare_h(g):
                layernorm(h_of(g), xn, name="xn_ready")

            prepare_c1(0)
            prepare_c1(1)
            convolve(0)
            with at.loop(dve, NG - 2) as i:
                prepare_c1(i + 2)
                convolve(i + 1)
                convolved(i)
            convolve(NG - 1)
            convolved(NG - 2)
            prepare_a1(0)
            convolved(NG - 1)
            in_turns(prepare_a1, attend_1, lambda: prepare_f1(0))
            in_turns(prepare_f1, mlp_1, lambda: prepare_h(0))
            mark("attn1_done")

            def logits(g):
                k = at.bank(OBANKS)
                o = full(k)[0:T, 0:GB * NE].rearrange("p (b e) -> p b e", b=GB)
                free(dve.tensor_copy(LG[:, bass.ds(g * GB, GB), :], o), k)

            def probabilities():
                step(dve.tensor_reduce(E2[0][:], LG[:], AX.X, ALU.max))
                give(tt(E1[0], LG[:], wide(E2[0][:], NE), ALU.subtract), "probs_in")
                dve.wait_ge(sem["exp_ready"], at.take("exp_ready"))
                step(dve.tensor_reduce(E2[0][:], E1[0], AX.X, ALU.add))
                step(dve.reciprocal(E2[1][:], E2[0][:]))
                step(tt(E1[0], E1[0], wide(E2[1][:], NE), ALU.mult))

            def best_two():
                step(dve.tensor_copy(E1[2], E1[0]))
                for n in range(2):
                    step(dve.tensor_reduce(E2[0][:], E1[2], AX.X, ALU.max))
                    step(tt(E1[3], E1[2], wide(E2[0][:], NE), ALU.is_equal))
                    step(tt(E1[3], E1[3], ORDER[:], ALU.mult))
                    step(dve.tensor_reduce(E2[1][:], E1[3], AX.X, ALU.max))
                    step(tt(E1[4 + n], ORDER[:], wide(E2[1][:], NE), ALU.is_equal))
                    if n == 0:
                        step(stt(E1[2], E1[4], -2.0, E1[2], ALU.mult, ALU.add))
                step(tt(E1[4], E1[4], E1[5], ALU.add))
                step(tt(E1[1], E1[0], E1[4], ALU.mult))

            def share():
                step(dve.tensor_reduce(E2[0][:], E1[1], AX.X, ALU.add))
                step(dve.reciprocal(E2[1][:], E2[0][:]))
                step(tt(E1[1], E1[1], wide(E2[1][:], NE), ALU.mult))

            def experts(tiles):
                for e in range(NE):
                    with at.loop(dve, NG) as g:
                        for m in range(tiles):
                            dve.wait_ge(sem["hidden_ready"], at.take("hidden_ready"))
                            give(tt(HT_LR[:, m, :], HT[:, m, :], HT_HR[:, m, :], ALU.subtract), "hidden_split")
                        for bb in range(GB):
                            k = at.bank(SBANKS if bb < 2 else OBANKS)
                            h = h_of(g)(bb)
                            free(stt(h, full(k)[0:T, 0:D], E1[1][:, bass.ds(g * GB + bb, 1), e], h,
                                     ALU.mult, ALU.add), k)
                    mark(f"w2_used{e % RING}")

            in_turns(prepare_h, logits, lambda: None)
            probabilities()
            mark("router_ready")
            best_two()
            k = at.bank(OBANKS)
            o = full(k)[0:T, 0:NB * NE].rearrange("p (b e) -> p e b", e=NE)
            free(dve.tensor_reduce(RUN[:], o, AX.X, ALU.add), k)
            step(ts(RUN[:], RUN[:], -1.0, 1.0 - 0.9, ALU.add, ALU.mult))
            step(ts(RUN[:], RUN[:], 1.0, 0.01, ALU.add, ALU.add))
            step(dve.reciprocal(RUN[:], RUN[:]))
            step(tt(E1[1], E1[1], RUN[:].unsqueeze(1).to_broadcast([T, NB, NE]), ALU.mult))
            share()
            experts(I1 // 128)

            dve.wait_ge(sem["w2_loaded"], 16 * W2_LOADS)
            def prepare_a2(g):
                layernorm(h_of(g), xn, name="xn_ready")
                step(tt(group(H, g), group(H, g), spread(bo2), ALU.add))

            def attend_2(g):
                values(V, 64, None)
                attention(64, False, 0.125, lambda bb, o, k: free(tt(h_of(g)(bb), h_of(g)(bb), o, ALU.add), k))

            def mlp_2(g):
                pairs(lambda bb, o: tt(h_of(g)(bb), h_of(g)(bb), o, ALU.add))

            def attend_3(g):
                for first in range(0, GB, 2):
                    k = at.bank(OBANKS)
                    o = full(k)
                    for bb in (first, first + 1):
                        last = tt(V[:, bb * D:(bb + 1) * D], o[0:T, (bb - first) * D:(bb - first + 1) * D],
                                  bv3, ALU.add)
                    free(last, k)
                k = at.bank(SBANKS)
                o = full(k)[0:T, 0:TG].rearrange("p (b t) -> p b t", b=GB)
                free(stt(PT[0][:], o, float(np.float32(1) / np.sqrt(np.float32(D))),
                         decay.unsqueeze(1).to_broadcast([T, GB, T]), ALU.mult, ALU.mult), k)
                mlp_2(g)

            prepare_a2(0)
            in_turns(prepare_a2, attend_2, lambda: prepare_h(0))

            in_turns(prepare_h, mlp_2, lambda: prepare_h(0))
            in_turns(prepare_h, attend_3, lambda: prepare_h(0))

            in_turns(prepare_h, logits, lambda: None)
            probabilities()
            best_two()
            share()
            mark("router_ready")
            for first in range(0, NB, 2):
                k = at.bank(OBANKS)
                o = full(k)[0:T, 0:2 * D].rearrange("p (b d) -> p b d", b=2)
                free(tt(H[:, first:first + 2, :], H[:, first:first + 2, :], o, ALU.add), k)
            experts(FT)
            for _ in range(NG):
                mark("out_ready")

        @block.scalar
        def _(act):
            at = Count("act", notes)
            activation = act.activation

            def give(ins, name):
                ins.then_inc(sem[name], at.one(name))

            def full(k):
                act.wait_ge(sem[f"bank_full{k}"], at.take(f"bank_full{k}"))
                return psum[k]

            def free(ins, k):
                give(ins, f"bank_free{k}")

            def mark(name):
                n = at.bank(MARKS)
                give(activation(amarked[:, n:n + 1], ident[0:1, 0:1], ACT.Copy), name)

            def turned(dst, scale=None, bias=None):
                for part in range(2):
                    k = at.bank(XBANKS)
                    src = full(k)[0:KD, 0:TG]
                    if scale is None:
                        free(activation(dst[:, part, :], src, ACT.Copy), k)
                    else:
                        free(activation(dst[:, part, :], src, ACT.Identity, scale=scale[:, part:part + 1],
                                        bias=bias[:, part:part + 1]), k)

            def hidden(tiles, func, bias):
                for m in range(tiles):
                    k = at.bank(FBANKS)
                    src = full(k)[:, 0:TG]
                    free(activation(HT[:, m, :], src, func, bias=0.0 if bias is None else bias(m)), k)

            def hidden_parts(tiles, func, bias):
                def high(m, k, n):
                    act.wait_ge(sem[f"bank_free{k}"], n)
                    give(activation(HT_HR[:, m, :], HT[:, m, :], ACT.Copy), "hidden_ready")

                last = None
                for m in range(tiles):
                    k = at.bank(FBANKS)
                    free(activation(HT[:, m, :], full(k)[:, 0:TG], func, bias=0.0 if bias is None else bias(m)), k)
                    if last:
                        high(*last)
                    last = m, k, at.now(f"bank_free{k}") + 1
                high(*last)

            def exponentials(buf, scale=1.0, name="probs_ready"):
                act.wait_ge(sem["probs_in"], at.take("probs_in"))
                give(activation(buf, buf, ACT.Exp, scale=scale), name)

            def attention(scale, pos=None):
                for s in range(STEPS):
                    if s < UNITS:
                        k = at.bank(SBANKS)
                        act.wait_ge(sem["probs_in"], at.take("probs_in"))
                        for j in range(HPU):
                            p = PB[s % 3][:, j, :]
                            last = activation(p, p if pos else psum[k][0:T, cols(j)], ACT.Exp, scale=scale,
                                              bias=NMU[:, s % 3, j:j + 1], accum_out=SMU[:, s % 3, j:j + 1])
                        give(last, "exp_ready")
                    if 0 <= s - 2 < UNITS:
                        k = at.bank(TBANKS)
                        src = full(k)[0:T, 0:TU].rearrange("p (h t) -> p h t", h=HPU)
                        free(activation(PT[s % 2][:, 0:HPU, :], src, ACT.Copy), k)
                    if pos and s in (UPB, 2 * UPB):
                        pos()

            for k in TBANKS + XBANKS:
                act.sem_inc(sem[f"bank_free{k}"], 1)
            act.sem_inc(sem["yt_ready"], 1)

            act.wait_ge(sem["constants_ready"], 1)
            k = at.bank(XBANKS)
            src = full(k)[0:KD, 0:2 * NSLOT].rearrange("p (k s) -> p k s", k=2)
            free(activation(slT[:], src, ACT.Copy), k)

            act.wait_ge(sem["w0_loaded"], W0_LOADS)
            for p in range(6):
                k = at.bank(TBANKS)
                free(activation(RT[:, p, :], full(k)[:, 0:NREL], ACT.Copy), k)
            with at.loop(act, NG) as g:
                turned(XT)
                for p in range(6):
                    k = at.bank(XBANKS)
                    src = full(k)[:, 0:TG]
                    activation(QT[:, p, :], src, ACT.Identity, bias=rw0[:, p:p + 1])
                    free(activation(QR[:, p, :], src, ACT.Identity, bias=rr0[:, p:p + 1]), k)
                def pos_rows():
                    act.wait_ge(sem["pr_stored"], at.now("pr_ready") * 16 + 16)
                    for h0, h1 in POS_PAIRS:
                        k = at.bank(XBANKS)
                        src = full(k)[0:T, 0:2 * NREL].rearrange("p (h n) -> p h n", h=2)
                        free(activation(PR[:, h0:h1 + 1:h1 - h0, 0:NREL], src, ACT.Copy), k)
                    mark("pr_ready")

                pos_rows()
                for p in range(6):
                    k = at.bank(XBANKS)
                    free(activation(KT[:, p, :], full(k)[:, 0:TG], ACT.Identity, bias=bk0[:, p:p + 1]), k)
                pos_rows()
                attention(0.125, pos_rows)

            with at.loop(act, NG // 2) as i:
                for g in (2 * i, 2 * i + 1):
                    turned(XT)
                    exponentials(CW, name="exp_ready")
                    exponentials(DP, name="exp_ready")
                    k = at.bank(TBANKS)
                    src = full(k)[0:NSLOT, 0:TG].rearrange("p (b t) -> p b t", b=GB)
                    free(activation(CT[:, bass.ds(g * GB, GB), :], src, ACT.Copy), k)
                    k = at.bank(TBANKS)
                    src = full(k)[0:T, 0:GB * NSLOT].rearrange("p (b s) -> p b s", b=GB)
                    free(activation(DW, src, ACT.Copy), k)
                    k = at.bank(XBANKS)
                    src = full(k)[0:KD, :].rearrange("p (k b s) -> p k s b", k=2, b=GB)
                    activation(YT[:, 0, :, bass.ds(g * GB, GB)], src[:, 0], ACT.Copy)
                    free(activation(YT[:, 1, :, bass.ds(g * GB, GB)], src[:, 1], ACT.Copy), k)
                    mark("yt_ready")
            with at.loop(act, NSLOT // RING) as j:
                for c0, c1 in ((0, 512), (512, FF)):
                    k = at.bank(TBANKS)
                    free(activation(HR[:, c0:c1], full(k)[:, 0:c1 - c0], ACT.Gelu), k)
            for b in range(NB):
                k = at.bank(XBANKS)
                free(activation(Y2[b % 2], full(k)[0:NSLOT, 0:D], ACT.Copy), k)

            act.wait_ge(sem["w1_loaded"], 16 * W1_LOADS)
            act.wait_ge(sem["padded"], 1)
            with at.loop(act, NG) as g:
                turned(XT, g1[:, 0, :], b1[:, 0, :])
                for c in range(CT3):
                    act.wait_ge(sem["gated"], at.take("gated"))
                    k = at.bank(TBANKS)
                    free(activation(HT[:, 3 + c, :], full(k)[:, 0:TG], ACT.Silu), k)
                    act.wait_ge(sem["conv_ready"], at.take("conv_ready"))
                    give(activation(HT[:, c, :], HT[:, c, :], ACT.Silu), "gate_ready")
            with at.loop(act, NG) as g:
                turned(XT, g1[:, 1, :], b1[:, 1, :])
                for dst in range(6):
                    k = at.bank(XBANKS)
                    free(activation((QT, KT)[dst // 3][:, dst % 3, :], full(k)[:, 0:TG], ACT.Identity,
                                    bias=bqk1[:, dst:dst + 1]), k)
                attention(0.25)
            with at.loop(act, NG) as g:
                turned(XT, g1[:, 2, :], b1[:, 2, :])
                hidden(FT, ACT.Gelu, lambda m: bf1[:, m:m + 1])

            def router_inputs():
                with at.loop(act, NG) as g:
                    for part in range(2):
                        k = at.bank(XBANKS)
                        src = full(k)[0:KD, 0:TG]
                        activation(XT[:, part, :], src, ACT.Copy)
                        free(activation(XALL_HR[:, part, bass.ds(g * TG, TG)], src, ACT.Copy), k)
                    mark("xt_ready")

            act.wait_ge(sem["attn1_done"], 1)
            router_inputs()
            exponentials(E1[0], name="exp_ready")
            for e in range(NE):
                with at.loop(act, NG) as g:
                    hidden_parts(I1 // 128, ACT.Silu, None)

            act.wait_ge(sem["w2_loaded"], 16 * W2_LOADS)
            with at.loop(act, NG) as g:
                turned(XT)
                for buf in (QT, KT):
                    for p in range(6):
                        k = at.bank(XBANKS)
                        free(activation(buf[:, p, :], full(k)[:, 0:TG], ACT.Copy), k)
                attention(0.125)

            with at.loop(act, NG) as g:
                turned(XT)
                hidden(FT, ACT.Gelu, lambda m: bi2[:, m:m + 1])
            with at.loop(act, NG) as g:
                turned(XT)
                for dst in range(4):
                    k = at.bank(XBANKS)
                    free(activation((QT, KT)[dst // 2][0:KD, dst % 2, :], full(k)[0:KD, 0:TG], ACT.Identity,
                                    bias=bqk3[:, dst:dst + 1]), k)

            router_inputs()
            exponentials(E1[0], name="exp_ready")
            for first in range(0, NB, 4):
                k = at.bank(TBANKS)
                src = full(k)[0:NE, 0:TG].rearrange("p (b t) -> p b t", b=4)
                free(activation(WT8[:, first:first + 4, :], src, ACT.Copy), k)
            for e in range(NE):
                with at.loop(act, NG) as g:
                    hidden_parts(FT, ACT.Gelu, lambda m: bb1[:, e, m:m + 1])

        @block.tensor
        def _(pe):
            at = Count("pe", notes)

            def claim(banks, k=None):
                k = at.bank(banks) if k is None else k
                pe.wait_ge(sem[f"bank_free{k}"], at.now(f"bank_full{k}") + 1)
                return k, psum[k]

            def filled(ins, k):
                ins.then_inc(sem[f"bank_full{k}"], at.one(f"bank_full{k}"))
                return k, at.now(f"bank_full{k}")

            def moved(*fillings):
                for k, n in fillings:
                    pe.wait_ge(sem[f"bank_free{k}"], n + 1)

            def product(dst, pieces):
                for n, (lhsT, rhs) in enumerate(pieces):
                    last = pe.matmul(dst, lhsT, rhs, start=n == 0, stop=n == len(pieces) - 1)
                    if n == 0 and len(pieces) > 1:
                        say_taken(last)
                return last

            fresh = []

            def say_taken(ins):
                if fresh:
                    fresh.clear()
                    ins.then_inc(sem["xn_taken"], 1)

            def turn_group(src):
                out = []
                for part in range(2):
                    k, p = claim(XBANKS)
                    for bb in range(GB):
                        last = pe.transpose(p[0:KD, cols(bb)], src[:, bb, part * KD:(part + 1) * KD],
                                            ident[0:T, 0:T])
                    out.append(filled(last, k))
                return out

            def xt(x=XN):
                pe.wait_ge(sem["xn_ready"], at.take("xn_ready"))
                moved(*turn_group(x))
                fresh.append(True)

            def two(w, n0, n1, x=XT):
                return [(w[:, part, n0:n1], x[:, part, :]) for part in range(2)]

            def token_rows(x, bb, w, n0=0, n1=D):
                return [(x[:, part, cols(bb)], w[:, part, n0:n1]) for part in range(w.shape[1])]

            def pairs(pieces):
                out = []
                for first in range(0, GB, 2):
                    k, p = claim(OBANKS)
                    for bb in (first, first + 1):
                        last = product(p[0:T, (bb - first) * D:(bb - first + 1) * D], pieces(bb))
                    out.append(filled(last, k))
                return out

            def mlp(tiles, w1, x, w2, w1_used=None):
                tokens = []
                for m in range(tiles):
                    k, p = claim(FBANKS)
                    last = product(p[:, 0:TG], [(w1[:, part, m * 128:(m + 1) * 128], x(part)) for part in range(2)])
                    tokens.append(filled(last, k))
                for first in range(0, GB, 2):
                    k, p = claim(OBANKS)
                    for bb in (first, first + 1):
                        for m in range(tiles):
                            if bb == 0:
                                moved(tokens[m])
                            last = pe.matmul(p[0:T, (bb - first) * D:(bb - first + 1) * D], HT[:, m, cols(bb)],
                                             w2[:, m, 0:D], start=m == 0, stop=m == tiles - 1)
                            if bb == 0 and m == 0 and w1_used:
                                last.then_inc(sem[w1_used], at.one(w1_used))
                    filled(last, k)

            def attention(dk, per_tile, dv, wo, v_moved, pos=None):
                pt_moved, o_moved = {}, {}
                for s in range(STEPS):
                    if s < UNITS:
                        bb, unit = s // UPB, s % UPB
                        k = at.bank(SBANKS)
                        if s < 2:
                            pe.wait_ge(sem[f"bank_free{k}"], at.now(f"bank_full{k}") + 1)
                        else:
                            pe.wait_ge(sem["exp_ready"], at.take("exp_ready"))
                        for j in range(HPU):
                            h = HPU * unit + j
                            last = pe.matmul(psum[k][0:T, cols(j)], head(QT, h, per_tile, dk, cols(bb)),
                                             head(KT, h, per_tile, dk, cols(bb)), start=True, stop=True)
                        last.then_inc(sem["scores_ready"], at.one("scores_ready"))
                    n = s - 3
                    if 0 <= n < UNITS:
                        bb, unit = n // UPB, n % UPB
                        if n == 0:
                            moved(*v_moved)
                        moved(pt_moved[n])
                        if unit == 0 or av_filled(dv, unit - 1):
                            claim(None, AVBANK)
                        for j in range(HPU):
                            h = HPU * unit + j
                            row, rows, tile, _ = av_place(dv, h)
                            last = pe.matmul(psum[AVBANK][row:row + rows, cols(tile)],
                                             by_head(dv)[:, bb * HEADS + h, :], PT[n % 2][:, j, :],
                                             start=True, stop=True)
                        if av_filled(dv, unit):
                            o_moved[bb] = filled(last, AVBANK)
                    n = s - 2
                    if 0 <= n < UNITS:
                        pe.wait_ge(sem["probs_ready"], at.take("probs_ready"))
                        k, p = claim(TBANKS)
                        for j in range(HPU):
                            last = pe.transpose(p[0:T, cols(j)], PB[n % 3][:, j, :], ident[0:T, 0:T])
                        pt_moved[n] = filled(last, k)
                    if pos and s in (UPB, 2 * UPB):
                        pos(2 if s == UPB else 3)
                    bb = last_of(s - 4)
                    if bb is not None:
                        moved(o_moved[bb])
                        k, p = claim(None, PROJBANK)
                        filled(product(p[0:T, 0:D], [(OT[bb % 2][:, n, :], wo[:, n, :])
                                                     for n in range(3 if dv == 16 else 6)]), k)
                at.one("exp_ready", 2)

            pe.wait_ge(sem["patches_loaded"], 64)
            for first in range(0, NB, 2):
                k, p = claim(OBANKS)
                for j in range(2):
                    last = product(p[0:NPATCH, j * D:(j + 1) * D],
                                   [(patchT[:, n, first + j, :], convT[:, n, :]) for n in range(KP // 128)])
                f = filled(last, k)
            moved(f)

            pe.wait_ge(sem["constants_ready"], 1)
            pe.wait_ge(sem["xn_ready"], at.take("xn_ready"))
            k, p = claim(XBANKS)
            for part in range(2):
                last = pe.transpose(p[0:KD, part * NSLOT:(part + 1) * NSLOT], SL2[:, part * KD:(part + 1) * KD],
                                    ident[0:NSLOT, 0:NSLOT])
            filled(last, k)
            fresh.append(True)

            pe.wait_ge(sem["w0_loaded"], W0_LOADS)
            r_moved = []
            for p6 in range(6):
                k, p = claim(TBANKS)
                r_moved.append(filled(product(p[:, 0:NREL], [(rker[:, part, p6 * 128:(p6 + 1) * 128],
                                                              posT[:, part, :]) for part in range(2)]), k))
            moved(*r_moved[-2:])
            with at.loop(pe, NG) as g:
                xt()
                v_moved = []
                for first in range(0, GB, 2):
                    k, p = claim(OBANKS)
                    for bb in (first, first + 1):
                        for part in range(2):
                            c = (bb - first) * D + part * KD
                            last = pe.matmul(p[0:T, c:c + KD], XT[:, part, cols(bb)], wv0[:, part, :],
                                             start=True, stop=True)
                            say_taken(last)
                    v_moved.append(filled(last, k))
                def project(w):
                    out = []
                    for p6 in range(6):
                        k, p = claim(XBANKS)
                        part, c = p6 // 3, (p6 % 3) * 128
                        out.append(filled(pe.matmul(p[:, 0:TG], w[:, part, c:c + 128], XT[:, part, :],
                                                    start=True, stop=True), k))
                    return out

                def pos(bb):
                    for pair in POS_PAIRS:
                        k, p = claim(XBANKS)
                        for j, h in enumerate(pair):
                            last = pe.matmul(p[0:T, j * NREL:(j + 1) * NREL], head(QR, h, 2, 64, cols(bb)),
                                             head(RT, h, 2, 64, slice(0, NREL)), start=True, stop=True)
                        filled(last, k)

                moved(*project(wq0)[-2:])
                pos(0)
                k_moved = project(wk0)
                pos(1)
                moved(*k_moved[-2:])
                attention(64, 2, 16, wo0, v_moved, pos)

            with at.loop(pe, NG // 2):
                for x in XND:
                    at.one("exp_ready", 2)
                    xt(x)
                    k, p = claim(OBANKS)
                    for bb in range(GB):
                        last = product(p[0:T, bb * NSLOT:(bb + 1) * NSLOT], token_rows(XT, bb, slT, 0, NSLOT))
                    filled(last, k)
                    pe.wait_ge(sem["slot_in"], at.take("slot_in"))
                    k = at.bank(SBANKS)
                    pe.wait_ge(sem[f"bank_free{k}"], at.now(f"bank_full{k}") + 1)
                    pe.sem_inc(sem["tensor_passed"], 1)
                    for bb in range(GB):
                        last = pe.transpose(psum[k][0:NSLOT, cols(bb)], LG4[:, bb, :], ident[0:T, 0:T])
                    last.then_inc(sem["scores_ready"], at.one("scores_ready"))
                    pe.wait_ge(sem["slot_in"], at.take("slot_in"))
                    k, p = claim(TBANKS)
                    pe.sem_inc(sem["tensor_passed"], 1)
                    for bb in range(GB):
                        last = pe.transpose(p[0:NSLOT, cols(bb)], CW[:, bb, :], ident[0:T, 0:T])
                    filled(last, k)
                    pe.wait_ge(sem["slot_in"], at.take("slot_in"))
                    k, p = claim(TBANKS)
                    pe.sem_inc(sem["tensor_passed"], 1)
                    for bb in range(GB):
                        last = pe.transpose(p[0:T, bb * NSLOT:(bb + 1) * NSLOT], DP[:, bb, :], ident[0:NSLOT, 0:NSLOT])
                    moved(filled(last, k))
                    k, p = claim(XBANKS)
                    for part in range(2):
                        for bb in range(GB):
                            c = (part * GB + bb) * NSLOT
                            last = pe.matmul(p[0:KD, c:c + NSLOT], x[:, bb, part * KD:(part + 1) * KD], DW[:, bb, :],
                                             start=True, stop=True)
                    y_moved = filled(last, k)
            last_bank = y_moved[0]
            pe.wait_ge(sem[f"bank_free{last_bank}"], at.now(f"bank_full{last_bank}") + 1)

            def slots_product(o, n, piece, used=None):
                for m in range(n):
                    for r in range(RING):
                        last = pe.matmul(o[32 * r:32 * r + 32, :], *piece(r, m), start=m == 0, stop=m == n - 1)
                        if used and m == n - 1 and r < RING - 1:
                            last.then_inc(sem[f"{used}{r}"], at.one(f"{used}{r}"))
                return last

            with at.loop(pe, NSLOT // RING) as j:
                pe.wait_ge(sem["slot_rows"], at.take("slot_rows"))
                for r in range(RING):
                    pe.wait_ge(sem[f"w1_loaded{r}"], at.take(f"w1_loaded{r}", 16))
                rows = (KD + 1, KD)
                hidden_moved = []
                for c0, c1 in ((0, 512), (512, FF)):
                    k, p = claim(TBANKS)
                    hidden_moved.append(filled(slots_product(p[:, 0:c1 - c0], 2, lambda r, m: (
                        XS[0:rows[m], m, r, :], W1B[r][0:rows[m], m, c0:c1])), k))
                moved(*hidden_moved)
                turned = []
                for half in range(2):
                    k, p = claim(SBANKS)
                    for f in range(3):
                        last = pe.transpose(p[:, f * 128:(f + 1) * 128],
                                            HR[:, (3 * half + f) * 128:(3 * half + f + 1) * 128], ident[:])
                        if f < RING // 2:
                            last.then_inc(sem[f"w1_used{2 * half + f}"], at.one(f"w1_used{2 * half + f}"))
                    turned.append(filled(last, k))
                for r in range(RING):
                    pe.wait_ge(sem[f"w2_loaded{r}"], at.take(f"w2_loaded{r}", 16))
                moved(*turned)
                k, p = claim(OBANKS)
                moved(filled(slots_product(p[:, 0:D], FT, lambda r, f: (
                    HS[:, f, 32 * r:32 * r + 32], W2[r][:, f, :]), "w2_used"), k))
                k, p = claim(OBANKS)
                for part in range(2):
                    last = pe.transpose(p[0:KD, part * 128:(part + 1) * 128], YR[:, part * KD:(part + 1) * KD],
                                        ident[:])
                    if part == 0:
                        last.then_inc(sem[f"w2_used{RING - 1}"], at.one(f"w2_used{RING - 1}"))
                y_moved = filled(last, k)
            pe.wait_ge(sem[f"bank_free{y_moved[0]}"], at.now(f"bank_full{y_moved[0]}") + 1)

            y2 = {}
            for s in range(NB + 1):
                if s < NB:
                    k, p = claim(XBANKS)
                    for part in range(2):
                        last = pe.transpose(p[0:NSLOT, part * KD:(part + 1) * KD], Y2T[:, part, :, s],
                                            ident[0:KD, 0:KD])
                    y2[s] = filled(last, k)
                if s >= 1:
                    b = s - 1
                    moved(y2[b])
                    if b % 2 == 0:
                        k, p = claim(OBANKS)
                        kk = k
                    last = pe.matmul(psum[kk][0:T, (b % 2) * D:(b % 2 + 1) * D], CT[:, b, :], Y2[b % 2],
                                     start=True, stop=True)
                    if b % 2:
                        filled(last, kk)

            pe.wait_ge(sem["w1_loaded"], 16 * W1_LOADS)
            pe.wait_ge(sem["padded"], 1)
            def convolution_in():
                at.first_banks()
                xt()
                for c in range(CT3):
                    k, p = claim(SBANKS)
                    filled(product(p[:, 0:TG], two(win1, c * 128, (c + 1) * 128)), k)
                    k, p = claim(TBANKS)
                    filled(product(p[:, 0:TG], two(win1, INNER + c * 128, INNER + (c + 1) * 128)), k)

            def convolution_out(place):
                pe.wait_ge(sem["gated"], at.take("gated", CT3) + CT3)
                pairs(lambda bb: token_rows(QT[:, CT3 * place:CT3 * place + CT3, :], bb, wout1))

            convolution_in()
            with at.loop(pe, (NG - 2) // 2):
                for place in range(2):
                    convolution_in()
                    convolution_out(place)
            convolution_in()
            convolution_out(0)
            convolution_out(1)
            with at.loop(pe, NG) as g:
                xt()
                qk = []
                for dst in range(6):
                    k, p = claim(XBANKS)
                    qk.append(filled(product(p[:, 0:TG], two(wqk1, dst * 128, (dst + 1) * 128)), k))
                v_moved = pairs(lambda bb: token_rows(XT, bb, wqkv1, 2 * D, 3 * D))
                moved(*qk[-2:])
                attention(16, 4, 16, wp1, v_moved)
            with at.loop(pe, NG) as g:
                xt()
                mlp(FT, wf1, lambda part: XT[:, part, :], wf2)

            def router_inputs(w):
                with at.loop(pe, NG) as g:
                    xt()
                    k, p = claim(OBANKS)
                    for bb in range(GB):
                        last = product(p[0:T, bb * NE:(bb + 1) * NE], token_rows(XT, bb, w, 0, NE))
                    filled(last, k)
                    pe.wait_ge(sem["xt_copied"], at.take("xt_copied"))

            def by_parts(stationary, moving):
                (s_high, s_low), (m_high, m_low) = stationary, moving
                return [(s_high, m_high), (s_high, m_low), (s_low, m_high)]

            def experts(tiles):
                for e in range(NE):
                    r = e % RING
                    pe.wait_ge(sem["w1_split"], at.take("w1_split"))
                    pe.wait_ge(sem["w2_split"], at.take("w2_split"))
                    with at.loop(pe, NG) as g:
                        for m in range(tiles):
                            k, p = claim(FBANKS)
                            c = slice(m * 128, (m + 1) * 128)
                            pieces = []
                            for part in range(2):
                                pieces += by_parts([w[:, part, c] for w in (W1_HR[e % 2], W1_LR[r])],
                                                   [x[:, part, bass.ds(g * TG, TG)] for x in (XALL_HR, XALL_LR)])
                            filled(product(p[:, 0:TG], pieces), k)
                        banks = [claim(SBANKS if bb < 2 else OBANKS) for bb in range(GB)]
                        for m in range(tiles):
                            pe.wait_ge(sem["hidden_split"], at.take("hidden_split"))
                            for bb, (k, p) in enumerate(banks):
                                for n, (lhsT, rhs) in enumerate(by_parts(
                                        [h[:, m, cols(bb)] for h in (HT_HR, HT_LR)],
                                        [w[:, m, :] for w in (W2_HR[e % 2], W2_LR[r])])):
                                    last = pe.matmul(p[0:T, 0:D], lhsT, rhs, start=m == 0 and n == 0,
                                                     stop=m == tiles - 1 and n == 2)
                                    if bb == 0 and m == 0 and n == 0:
                                        last.then_inc(sem[f"w1_used{r}"], at.one(f"w1_used{r}"))
                                if m == tiles - 1:
                                    filled(last, k)

            router_inputs(rt1)
            at.one("exp_ready")
            pe.wait_ge(sem["router_ready"], at.take("router_ready"))
            k, p = claim(OBANKS)
            filled(pe.matmul(p[0:T, 0:NB * NE], ones[0:T, 0:T], E1[0].rearrange("p b e -> p (b e)"),
                             start=True, stop=True), k)
            experts(I1 // 128)

            pe.wait_ge(sem["w2_loaded"], 16 * W2_LOADS)
            with at.loop(pe, NG) as g:
                xt()
                qk = []
                for w in (wq2, wk2):
                    for p6 in range(6):
                        k, p = claim(XBANKS)
                        qk.append(filled(product(p[:, 0:TG], two(w, p6 * 128, (p6 + 1) * 128)), k))
                v_moved = []
                for bb in range(GB):
                    for c in range(0, FF, 2 * D):
                        k, p = claim(OBANKS)
                        v_moved.append(filled(product(p[0:T, 0:2 * D], token_rows(XT, bb, wv2, c, c + 2 * D)), k))
                moved(*qk[-2:])
                attention(64, 2, 64, wo2, v_moved[-2:])

            with at.loop(pe, NG) as g:
                xt()
                mlp(FT, wi2, lambda part: XT[:, part, :], wu2)
            with at.loop(pe, NG) as g:
                xt()
                qk = []
                for dst in range(4):
                    k, p = claim(XBANKS)
                    qk.append(filled(product(p[0:KD, 0:TG], two(wqkv3, dst * KD, (dst + 1) * KD)), k))
                v_moved = pairs(lambda bb: token_rows(XT, bb, wqkv3, 2 * D, 3 * D))
                moved(*qk[-2:])
                k, p = claim(SBANKS)
                for bb in range(GB):
                    last = product(p[0:T, cols(bb)], [(KT[0:KD, part, cols(bb)], QT[0:KD, part, cols(bb)])
                                                      for part in range(2)])
                moved(*v_moved, filled(last, k))
                pairs(lambda bb: [(PT[0][:, bb, :], V[:, bb * D:(bb + 1) * D])])

            router_inputs(rt3)
            pe.wait_ge(sem["router_ready"], at.take("router_ready"))
            w_moved = []
            for first in range(0, NB, 4):
                k, p = claim(TBANKS)
                for j in range(4):
                    last = pe.transpose(p[0:NE, cols(j)], E1[1][:, first + j, :], ident[0:T, 0:T])
                w_moved.append(filled(last, k))
            moved(*w_moved[-2:])
            for first in range(0, NB, 2):
                k, p = claim(OBANKS)
                for j in range(2):
                    last = pe.matmul(p[0:T, j * D:(j + 1) * D], WT8[:, first + j, :], bb2, start=True, stop=True)
                filled(last, k)
            experts(FT)


def laid_out(i):
    a = {k: np.asarray(v) for k, v in i.items()}
    rows = lambda v, n=T: np.ascontiguousarray(np.broadcast_to(v, (n,) + v.shape))
    per128 = lambda v: v.reshape(-1, 128).T
    side = 32
    n5 = 5
    frac = np.arange(0.0, 1.0 - 1e-06, 1.0 / n5, dtype=np.float32)
    bins = np.searchsorted(np.arange(1.0 / side, 1.0, 1.0 / side, dtype=np.float32), frac, side="right")
    pos_ids = (bins[:, None] * side + bins).reshape(-1)
    x = a["x"][:, :, :80, :80].reshape(NB, 3, n5, 16, n5, 16)
    patches = x.transpose(1, 3, 5, 0, 2, 4).reshape(KP // 128, 128, NB, NPATCH).transpose(1, 0, 2, 3)
    ids = a["x_txt"].T
    qkv_b = a["L1_attn_qkv_b"]
    far = np.arange(T)[None, :] - np.arange(T)[:, None]
    decay = np.where(far >= 0, np.float32(0.99) ** far.astype(np.float32), np.float32(0)).astype(np.float32)
    tiled = lambda v: v.reshape(-1, 2, 2, HPU, 64).transpose(0, 1, 3, 2, 4).reshape(v.shape)
    spread16 = lambda w: np.pad(w.reshape(HEADS // 4, 4, 16, D), ((0, 0), (0, 0), (0, 16), (0, 0))
                                ).reshape(HEADS // 4, 128, D).transpose(1, 0, 2)
    in_rows = lambda v, p: v.reshape(v.shape[0], -1, p, v.shape[2]).transpose(0, 2, 1, 3)
    t = {
        "patchT": patches,
        "convT": a["L0_tok_conv_w"].reshape(D, KP).T.reshape(KP // 128, 128, D).transpose(1, 0, 2),
        "pos_rows": a["L0_tok_pos_table"][pos_ids], "conv_b": rows(a["L0_tok_conv_b"], NPATCH),
        "ids": ids, "words": a["L0_txt_token_embeddings"],
        "Wq": a["L0_attn_Wq"], "Wk": a["L0_attn_Wk"], "Wv": a["L0_attn_Wv"],
        "r_kernel": tiled(a["L0_attn_r_kernel"].reshape(D, FF)),
        "posT": a["L0_attn_position_embeds"][1:1 + NREL].T, "Wo": spread16(a["L0_attn_Wo"]),
        "r_w_bias": per128(tiled(a["L0_attn_r_w_bias"].reshape(1, -1))), "r_r_bias": per128(tiled(a["L0_attn_r_r_bias"].reshape(1, -1))),
        "bk": per128(tiled(a["L0_attn_bk"][None])), "bv": rows(a["L0_attn_bv"]), "bo": rows(a["L0_attn_bo"]),
        "gamma": rows(a["L0_attn_gamma"]), "beta": rows(a["L0_attn_beta"]),
        "slots": a["L0_ffn_slots"], "slot_scale": a["L0_ffn_scale"][:, None],
        "norm_weight": rows(a["L0_ffn_norm_weight"]),
        "fc2_bias": a["L0_ffn_fc2_bias"].reshape(NSLOT, 2, KD).transpose(2, 1, 0),
        "fc1": np.concatenate([in_rows(a["L0_ffn_fc1_weight"], KD),
                               np.stack([a["L0_ffn_fc1_bias"], np.zeros((NSLOT, FF), np.float32)], 1)[:, None]], 1),
        "fc2": in_rows(a["L0_ffn_fc2_weight"], 128),
        "in_proj": a["L1_attn_in_proj_w"], "out_proj": a["L1_attn_out_proj_w"], "qkv1": a["L1_attn_qkv_w"],
        "proj1": spread16(a["L1_attn_attn_proj_w"]), "ffn1": a["L1_attn_ffn1_w"], "ffn2": a["L1_attn_ffn2_w"],
        "conv1_w": a["L1_attn_conv_w"].reshape(CT3, 128, KCONV).transpose(1, 0, 2),
        "conv1_b": per128(a["L1_attn_conv_b"]),
        "ln_g": np.stack([a[f"L1_attn_ln{n}_g"].reshape(2, KD) for n in (1, 2, 3)]).transpose(2, 0, 1),
        "ln_b": np.stack([a[f"L1_attn_ln{n}_b"].reshape(2, KD) for n in (1, 2, 3)]).transpose(2, 0, 1),
        "qk1_b": qkv_b[:2 * D].reshape(2, UPB, HPU, 16).transpose(0, 1, 3, 2),
        "v1_b": rows(qkv_b[2 * D:]), "proj1_b": rows(a["L1_attn_attn_proj_b"]),
        "ffn1_b": per128(a["L1_attn_ffn1_b"]), "ffn2_b": rows(a["L1_attn_ffn2_b"]),
        "router1": a["L1_ffn_router_w"].T.reshape(2, KD, NE).transpose(1, 0, 2),
        "m1w1": in_rows(a["L1_ffn_w1"].transpose(0, 2, 1), KD), "m1w2": in_rows(a["L1_ffn_w2"].transpose(0, 2, 1), 128),
        "q2": tiled(a["L2_attn_w_q"]), "k2": tiled(a["L2_attn_w_k"]), "v2": a["L2_attn_w_v"], "o2": a["L2_attn_w_o"],
        "o2_b": rows(a["L2_attn_b_o"]), "in2": a["L2_ffn_in_weight"].T, "in2_b": per128(a["L2_ffn_in_bias"]),
        "up2": a["L2_ffn_out_weight"],
        "qkv3": a["L3_attn_W_qkv"], "qk3_b": a["L3_attn_b_qkv"][:2 * D].reshape(4, KD).T,
        "v3_b": rows(a["L3_attn_b_qkv"][2 * D:]), "decay": decay,
        "router3": a["L3_ffn_router_w"].T, "m3w1": in_rows(a["L3_ffn_w1"], KD), "m3w2": in_rows(a["L3_ffn_w2"], 128),
        "m3b1": a["L3_ffn_b1"].reshape(NE, FT, 128).transpose(2, 0, 1), "m3b2": a["L3_ffn_b2"],
    }
    return {k: np.ascontiguousarray(v) for k, v in t.items()}


def program(nc, shapes, notes):
    t = {name: nc.dram_tensor(f"in_{name}", shape, dt, kind="ExternalInput").ap()
         for name, (shape, dt) in shapes.items()}
    out = nc.dram_tensor("out_h", (T, NB, D), F32, kind="ExternalOutput").ap()
    row = HEADS * NREL
    scratch = nc.dram_tensor("pos_scratch", (NB, T, row), F32, kind="Internal").ap()
    flat = scratch.rearrange("b t n -> (b t n)")
    build(nc, t, out, scratch, flat, notes)


def kernel(**inputs):
    import concourse.bacc as _bacc
    from concourse.bass_utils import run_bass_kernel_spmd as _run

    t = laid_out(inputs)
    shapes = {k: (v.shape, mybir.dt.from_np(v.dtype)) for k, v in t.items()}
    notes = {}
    program(_bacc.Bacc("TRN2", target_bir_lowering=False, num_devices=1), shapes, notes)
    nc = _bacc.Bacc("TRN2", target_bir_lowering=False, num_devices=1)
    program(nc, shapes, notes)
    r = _run(nc, [{f"in_{k}": v for k, v in t.items()}], core_ids=[0])
    return np.ascontiguousarray(r.results[0]["out_h"].transpose(1, 0, 2))
```
